# Optimizing a Trainium2 kernel written in Bass

```python
import numpy as np
import jax
import jax.numpy as jnp

def _softmax(x, axis=-1):
    return jax.nn.softmax(x, axis=axis)

def _gelu(x):
    return jax.nn.gelu(x, approximate=True)

def _silu(x):
    return jax.nn.silu(x)

def _sigmoid(x):
    return jax.nn.sigmoid(x)

def _layernorm(x, axis=-1, eps=1e-05):
    m = jnp.mean(x, axis=axis, keepdims=True)
    v = jnp.var(x, axis=axis, keepdims=True)
    return (x - m) / jnp.sqrt(v + eps)

def _scatter_add(tgt, idx, src, axis=0):
    return tgt.at[idx].add(src)

def _segment_sum(src, seg, n):
    return jax.ops.segment_sum(src, seg, n)
kernel_name = 'mk_flamingo_gated_d2_seqx_r4_863781'

def setup_inputs(seed: int=0):
    np.random.seed(seed)
    _w = jnp.asarray

    def _rec_inputs():
        import jax
        import jax.numpy as jnp
        _rk = jax.random.key(seed)
        x = -0.0003929 + 0.9999 * jax.random.normal(jax.random.fold_in(_rk, 1), (8, 256, 512), jnp.float32)
        _lenS = 256 - jax.random.randint(jax.random.fold_in(_rk, 7), (8,), 0, max(1, 256 // 4) + 1, jnp.int32)
        _lenS2 = 256 - jax.random.randint(jax.random.fold_in(_rk, 8), (8,), 0, max(1, 256 // 4) + 1, jnp.int32)
        _ctx_2048P = jax.random.normal(jax.random.fold_in(_rk, 11), (8, 16, 512), jnp.float32)
        _ctx_2048c = jax.random.dirichlet(jax.random.fold_in(_rk, 511), 0.3 * jnp.ones((16,), jnp.float32), (8, 256))
        _ctx_2048t = jnp.einsum('bsk,bkd->bsd', _ctx_2048c, _ctx_2048P)
        _ctx_2048t = _ctx_2048t * jax.lax.rsqrt(jnp.mean(jnp.square(_ctx_2048t)) + 1e-12) * 0.953939
        ctx_2048 = 2.81802e-05 + 1.00001 * (_ctx_2048t + 0.3 * jax.random.normal(jax.random.fold_in(_rk, 611), (8, 256, 512), jnp.float32))
        _validS = jnp.arange(256)[None, :] < _lenS[:, None]
        _validS2 = jnp.arange(256)[None, :] < _lenS2[:, None]
        _causal = jnp.tril(jnp.ones((256, 256), dtype=bool))
        mask_BxS2_bk0 = jnp.logical_not(jnp.broadcast_to(_validS2[:, :], (8, 256)))
        _g = jax.random.normal(jax.random.fold_in(_rk, 9001), (2, 2), jnp.float32)
        _g = jnp.sign(_g) * jnp.maximum(jnp.abs(_g), 1.0) + (_g == 0) * 1.0
        g_xattn = _g[0]
        g_ffn = _g[1]
        return (x, ctx_2048, mask_BxS2_bk0, g_xattn, g_ffn)
    x, ctx_2048, mask_BxS2_bk0, g_xattn, g_ffn = _rec_inputs()

    def _L0_xattn_setup():
        import jax, jax.numpy as jnp
        import numpy as np
        N, D, L = (8, 256, 512)
        key = jax.random.key(seed)
        ks = jax.random.split(key, 5)
        s = 1.0 / np.sqrt(D)
        return {'X1': jax.random.normal(ks[0], (N, D, L), dtype=jnp.float32), 'X2': jax.random.normal(ks[1], (N, D, L), dtype=jnp.float32), 'QW': jax.random.normal(ks[2], (D, D), dtype=jnp.float32) * s, 'Qb': jnp.zeros((D,), dtype=jnp.float32), 'KW': jax.random.normal(ks[3], (D, D), dtype=jnp.float32) * s, 'Kb': jnp.zeros((D,), dtype=jnp.float32), 'VW': jax.random.normal(ks[4], (D, D), dtype=jnp.float32) * s, 'Vb': jnp.zeros((D,), dtype=jnp.float32)}
    _L0_xattn_all = _L0_xattn_setup()
    _L0_xattn_in = {k: v for k, v in _L0_xattn_all.items() if k in ('QW', 'Qb', 'KW', 'Kb', 'VW', 'Vb')}
    del _L0_xattn_all

    def _L0_ffn_setup():
        import jax, jax.numpy as jnp
        import numpy as np
        NUM_EXPERTS = 32
        TOP_K = 8
        SELECT_TOP_K = 4
        THRESHOLD = 0.5
        HIDDEN = 512
        D_FF = 192

        def _moe_forward(hidden_states, gate_weight, gate_up_proj, down_proj, similarity):
            B, S_len, H = hidden_states.shape
            E, K, Ssel = (NUM_EXPERTS, TOP_K, SELECT_TOP_K)
            x = hidden_states.reshape(-1, H)
            router_logits = x @ gate_weight.T
            router_probs = jax.nn.softmax(router_logits.astype(jnp.float32), axis=-1).astype(router_logits.dtype)
            router_top_value, router_indices = jax.lax.top_k(router_probs, K)
            routing_weights = router_top_value / jnp.clip(jnp.sum(router_top_value, axis=-1, keepdims=True), 1e-12, None)
            sim = similarity.astype(jnp.float32)
            sim = sim.at[jnp.arange(E), jnp.arange(E)].set(1.0)
            prim = router_indices[:, :Ssel]
            sec = router_indices[:, Ssel:]
            sim_cand = sim[sec[:, :, None], prim[:, None, :]]
            best_sim = jnp.max(sim_cand, axis=-1)
            best_i = jnp.argmax(sim_cand, axis=-1)
            prim_rep = jnp.broadcast_to(prim[:, None, :], sim_cand.shape)
            best_primary = jnp.take_along_axis(prim_rep, best_i[..., None], axis=-1)[..., 0]
            new_sec = jnp.where(best_sim < THRESHOLD, sec, best_primary) if THRESHOLD > 0.0 else best_primary
            rerouted_indices = jnp.concatenate([prim, new_sec], axis=1)
            combine = jnp.sum(jax.nn.one_hot(rerouted_indices, E, dtype=routing_weights.dtype) * routing_weights[..., None], axis=1)

            def expert_step(y, params):
                wgu, wd, cw = params
                gu = x @ wgu.T
                g, u = jnp.split(gu, 2, axis=-1)
                h = jax.nn.silu(g) * u
                y = y + h @ wd.T * cw[:, None]
                return (y, None)
            y0 = jnp.zeros_like(x)
            y, _ = jax.lax.scan(expert_step, y0, (gate_up_proj, down_proj, combine.T))
            return y.reshape(B, S_len, H)
        key = jax.random.key(seed)
        ks = jax.random.split(key, 5)
        hidden_states = jax.random.normal(ks[0], (4, 512, HIDDEN), dtype=jnp.float32)
        gate_weight = jax.random.normal(ks[1], (NUM_EXPERTS, HIDDEN), dtype=jnp.float32) * 0.02
        gate_up_proj = jax.random.normal(ks[2], (NUM_EXPERTS, 2 * D_FF, HIDDEN), dtype=jnp.float32) * 0.02
        down_proj = jax.random.normal(ks[3], (NUM_EXPERTS, HIDDEN, D_FF), dtype=jnp.float32) * 0.02
        similarity = jax.random.uniform(ks[4], (NUM_EXPERTS, NUM_EXPERTS), dtype=jnp.float32)
        return {'hidden_states': hidden_states, 'gate_weight': gate_weight, 'gate_up_proj': gate_up_proj, 'down_proj': down_proj, 'similarity': similarity}
    _L0_ffn_all = _L0_ffn_setup()
    _L0_ffn_in = {k: v for k, v in _L0_ffn_all.items() if k in ('gate_weight', 'gate_up_proj', 'down_proj', 'similarity')}
    del _L0_ffn_all

    def _L1_xattn_setup():
        import jax, jax.numpy as jnp
        import numpy as np
        key = jax.random.key(seed)
        k1, k2, k3 = jax.random.split(key, 3)
        B, S, D, M = (8, 512, 512, 128)
        hidden_states = jax.random.normal(k1, (B, S, D), dtype=jnp.float32)
        memory_tokens = jax.random.normal(k2, (B, M, D), dtype=jnp.float32)
        memory_mask = jax.random.randint(k3, (B, M), 0, 2).astype(jnp.bool_)
        return {'hidden_states': hidden_states, 'memory_tokens': memory_tokens, 'memory_mask': memory_mask}
    _L1_xattn_all = _L1_xattn_setup()
    _L1_xattn_in = {k: v for k, v in _L1_xattn_all.items() if k in ()}
    del _L1_xattn_all

    def _L1_ffn_setup():
        import jax, jax.numpy as jnp
        import numpy as np
        K = 2

        def gelu(v):
            return jax.nn.gelu(v, approximate=False)
        key = jax.random.key(seed)
        ks = jax.random.split(key, 10)
        B, S, D, H, E = (4, 512, 512, 256, 8)
        SH = 2 * H
        u = lambda k_, shape, b: jax.random.uniform(k_, shape, jnp.float32, -b, b)
        return {'x': jax.random.normal(ks[0], (B, S, D), jnp.float32), 'gate_w': u(ks[1], (D, E), 1.0 / D), 'w1': u(ks[2], (E, D, H), 1.0 / D), 'b1': u(ks[3], (E, H), 1.0 / np.sqrt(D)), 'w2': u(ks[4], (E, H, D), 1.0 / H), 'b2': u(ks[5], (E, D), 1.0 / np.sqrt(H)), 'shared_w1': u(ks[6], (D, SH), 1.0 / D), 'shared_b1': u(ks[7], (SH,), 1.0 / np.sqrt(D)), 'shared_w2': u(ks[8], (SH, D), 1.0 / SH), 'shared_b2': u(ks[9], (D,), 1.0 / np.sqrt(SH))}
    _L1_ffn_all = _L1_ffn_setup()
    _L1_ffn_in = {k: v for k, v in _L1_ffn_all.items() if k in ('gate_w', 'w1', 'b1', 'w2', 'b2', 'shared_w1', 'shared_b1', 'shared_w2', 'shared_b2')}
    del _L1_ffn_all
    return {'x': x, 'ctx_2048': ctx_2048, 'mask_BxS2_bk0': mask_BxS2_bk0, 'g_xattn': g_xattn, 'g_ffn': g_ffn, 'L0_xattn_QW': _L0_xattn_in['QW'], 'L0_xattn_Qb': _L0_xattn_in['Qb'], 'L0_xattn_KW': _L0_xattn_in['KW'], 'L0_xattn_Kb': _L0_xattn_in['Kb'], 'L0_xattn_VW': _L0_xattn_in['VW'], 'L0_xattn_Vb': _L0_xattn_in['Vb'], 'L0_ffn_gate_weight': _L0_ffn_in['gate_weight'], 'L0_ffn_gate_up_proj': _L0_ffn_in['gate_up_proj'], 'L0_ffn_down_proj': _L0_ffn_in['down_proj'], 'L0_ffn_similarity': _L0_ffn_in['similarity'], 'L1_ffn_gate_w': _L1_ffn_in['gate_w'], 'L1_ffn_w1': _L1_ffn_in['w1'], 'L1_ffn_b1': _L1_ffn_in['b1'], 'L1_ffn_w2': _L1_ffn_in['w2'], 'L1_ffn_b2': _L1_ffn_in['b2'], 'L1_ffn_shared_w1': _L1_ffn_in['shared_w1'], 'L1_ffn_shared_b1': _L1_ffn_in['shared_b1'], 'L1_ffn_shared_w2': _L1_ffn_in['shared_w2'], 'L1_ffn_shared_b2': _L1_ffn_in['shared_b2']}

def reference(x, ctx_2048, mask_BxS2_bk0, g_xattn, g_ffn, L0_xattn_QW, L0_xattn_Qb, L0_xattn_KW, L0_xattn_Kb, L0_xattn_VW, L0_xattn_Vb, L0_ffn_gate_weight, L0_ffn_gate_up_proj, L0_ffn_down_proj, L0_ffn_similarity, L1_ffn_gate_w, L1_ffn_w1, L1_ffn_b1, L1_ffn_w2, L1_ffn_b2, L1_ffn_shared_w1, L1_ffn_shared_b1, L1_ffn_shared_w2, L1_ffn_shared_b2):
    import jax
    import jax.numpy as jnp

    def _L0_xattn_ref(X1, X2, QW, Qb, KW, Kb, VW, Vb):
        import jax, jax.numpy as jnp
        import numpy as np
        N, D, L = (8, 256, 512)
        q = jnp.einsum('ndl,ed->nle', X1, QW) + Qb
        k = jnp.einsum('ndl,ed->nle', X2, KW) + Kb
        v = jnp.einsum('ndl,ed->nle', X2, VW) + Vb
        scores = jnp.einsum('nqd,nkd->nqk', q, k)
        attn = jax.nn.softmax(scores, axis=-1)
        H = jnp.einsum('nqk,nkd->nqd', attn, v)
        return jnp.swapaxes(H, -1, -2)

    def _L0_ffn_ref(hidden_states, gate_weight, gate_up_proj, down_proj, similarity):
        import jax, jax.numpy as jnp
        import numpy as np
        NUM_EXPERTS = 32
        TOP_K = 8
        SELECT_TOP_K = 4
        THRESHOLD = 0.5
        HIDDEN = 512
        D_FF = 192

        def _moe_forward(hidden_states, gate_weight, gate_up_proj, down_proj, similarity):
            B, S_len, H = hidden_states.shape
            E, K, Ssel = (NUM_EXPERTS, TOP_K, SELECT_TOP_K)
            x = hidden_states.reshape(-1, H)
            router_logits = x @ gate_weight.T
            router_probs = jax.nn.softmax(router_logits.astype(jnp.float32), axis=-1).astype(router_logits.dtype)
            router_top_value, router_indices = jax.lax.top_k(router_probs, K)
            routing_weights = router_top_value / jnp.clip(jnp.sum(router_top_value, axis=-1, keepdims=True), 1e-12, None)
            sim = similarity.astype(jnp.float32)
            sim = sim.at[jnp.arange(E), jnp.arange(E)].set(1.0)
            prim = router_indices[:, :Ssel]
            sec = router_indices[:, Ssel:]
            sim_cand = sim[sec[:, :, None], prim[:, None, :]]
            best_sim = jnp.max(sim_cand, axis=-1)
            best_i = jnp.argmax(sim_cand, axis=-1)
            prim_rep = jnp.broadcast_to(prim[:, None, :], sim_cand.shape)
            best_primary = jnp.take_along_axis(prim_rep, best_i[..., None], axis=-1)[..., 0]
            new_sec = jnp.where(best_sim < THRESHOLD, sec, best_primary) if THRESHOLD > 0.0 else best_primary
            rerouted_indices = jnp.concatenate([prim, new_sec], axis=1)
            combine = jnp.sum(jax.nn.one_hot(rerouted_indices, E, dtype=routing_weights.dtype) * routing_weights[..., None], axis=1)

            def expert_step(y, params):
                wgu, wd, cw = params
                gu = x @ wgu.T
                g, u = jnp.split(gu, 2, axis=-1)
                h = jax.nn.silu(g) * u
                y = y + h @ wd.T * cw[:, None]
                return (y, None)
            y0 = jnp.zeros_like(x)
            y, _ = jax.lax.scan(expert_step, y0, (gate_up_proj, down_proj, combine.T))
            return y.reshape(B, S_len, H)
        return _moe_forward(hidden_states, gate_weight, gate_up_proj, down_proj, similarity)

    def _L1_xattn_ref(hidden_states, memory_tokens, memory_mask):
        import jax, jax.numpy as jnp
        import numpy as np
        B, S, D = hidden_states.shape
        scale = 1.0 / jnp.sqrt(jnp.asarray(D, hidden_states.dtype))
        scores = jnp.einsum('bsd,bmd->bsm', hidden_states, memory_tokens) * scale
        neg_inf = jnp.asarray(-1e+30, scores.dtype)
        scores = jnp.where(memory_mask[:, None, :], scores, neg_inf)
        attn = jax.nn.softmax(scores, axis=-1)
        readout = jnp.einsum('bsm,bmd->bsd', attn, memory_tokens)
        valid_b = jnp.any(memory_mask, axis=-1)
        out = jnp.where(valid_b[:, None, None], readout, jnp.zeros_like(readout))
        return out

    def _L1_ffn_ref(x, gate_w, w1, b1, w2, b2, shared_w1, shared_b1, shared_w2, shared_b2):
        import jax, jax.numpy as jnp
        import numpy as np
        K = 2

        def gelu(v):
            return jax.nn.gelu(v, approximate=False)
        B, S, D = x.shape
        E = gate_w.shape[1]
        xf = x.reshape(-1, D)
        logits = xf @ gate_w
        top_logits, top_idx = jax.lax.top_k(logits, K)
        top_gates = jax.nn.softmax(top_logits, axis=-1)
        gates = jnp.sum(jax.nn.one_hot(top_idx, E, dtype=xf.dtype) * top_gates[..., None], axis=1)
        h = gelu(jnp.einsum('nd,edh->neh', xf, w1) + b1)
        out_e = jnp.einsum('neh,ehd->ned', h, w2) + b2
        routed = jnp.einsum('ne,ned->nd', gates, out_e)
        shared = gelu(xf @ shared_w1 + shared_b1) @ shared_w2 + shared_b2
        return (routed + shared).reshape(B, S, D)
    x = x + jnp.tanh(g_xattn[0]) * _L0_xattn_ref(_layernorm(x, axis=-1), ctx_2048, L0_xattn_QW, L0_xattn_Qb, L0_xattn_KW, L0_xattn_Kb, L0_xattn_VW, L0_xattn_Vb)
    x = x + jnp.tanh(g_ffn[0]) * _L0_ffn_ref(_layernorm(x, axis=-1), L0_ffn_gate_weight, L0_ffn_gate_up_proj, L0_ffn_down_proj, L0_ffn_similarity)
    x = x + jnp.tanh(g_xattn[1]) * _L1_xattn_ref(_layernorm(x, axis=-1), ctx_2048, mask_BxS2_bk0)
    x = x + jnp.tanh(g_ffn[1]) * _L1_ffn_ref(_layernorm(x, axis=-1), L1_ffn_gate_w, L1_ffn_w1, L1_ffn_b1, L1_ffn_w2, L1_ffn_b2, L1_ffn_shared_w1, L1_ffn_shared_b1, L1_ffn_shared_w2, L1_ffn_shared_b2)
    return x

_drawn_inputs = setup_inputs


def setup_inputs(seed=0):
    import zlib

    import numpy as np

    out = dict(_drawn_inputs(seed))
    spreads = {'g_ffn': (-1.0, 0.6),
     'L0_xattn_Qb': (0.0, 0.1),
     'L0_xattn_Kb': (0.0, 2.0),
     'L0_xattn_Vb': (0.0, 0.666)}
    factors = {'L0_ffn_gate_weight': 7.244,
     'L0_ffn_gate_up_proj': 6.75,
     'L0_ffn_down_proj': 6.754,
     'L0_ffn_similarity': 8.0,
     'L1_ffn_gate_w': 20.868,
     'L1_ffn_w1': 64.0,
     'L1_ffn_b1': 64.0,
     'L1_ffn_w2': 64.0,
     'L1_ffn_b2': 15.247,
     'L1_ffn_shared_w1': 64.0,
     'L1_ffn_shared_b1': 64.0,
     'L1_ffn_shared_w2': 64.0,
     'L1_ffn_shared_b2': 15.864}
    for name, (base, spread) in spreads.items():
        noise = np.random.default_rng([zlib.crc32(name.encode()), seed]).standard_normal(out[name].shape)
        drawn = base * np.exp(spread * noise) if base else spread * noise
        out[name] = jnp.asarray(drawn.astype(out[name].dtype))
    for name, factor in factors.items():
        out[name] = (out[name] * factor).astype(out[name].dtype)
    return out
```

```python
import concourse.bass as bass
from concourse import mybir
from concourse.alu_op_type import AluOpType as ALU
from contextlib import ExitStack

F32 = mybir.dt.float32
F16 = mybir.dt.float16
BF16 = mybir.dt.bfloat16
I32 = mybir.dt.int32
U32 = mybir.dt.uint32
U8 = mybir.dt.uint8
ACT = mybir.ActivationFunctionType
AX = mybir.AxisListType

P = 128
NB, S, L = 8, 256, 512
T = NB * S // P
TB = S // P
KC = L // P
EPS = 1e-5

QT = L // P
E0, TOPK, PRIM, F0 = 32, 8, 4, 192
FH = F0 // 2
THRESHOLD = 0.5
ROW = L + E0
G0 = NB * S * TOPK // P + E0
E1, K1, F1 = 8, 2, 256
ROW1 = L + E1
G1 = NB * S * K1 // P + E1
NONE = 4096


def at(i, per, k):
    return i * per + k


def flamingo_kernel(nc, x, ctx, ctx_t, mask, gains, w_qkv, b_qkv, gate0, sim, w_up, w_down,
                    gate1, w1, b1, w2, b2, sw1, sb1, sw2, sb2, out):
    es = ExitStack()
    with es:
        def sb(name, shape, dt=F32):
            return es.enter_context(nc.sbuf_tensor(name, shape, dt))

        def sem(name):
            return es.enter_context(nc.semaphore(name))

        x_v = x.rearrange("n (j p) l -> p (n j) l", p=P)
        out_v = out.rearrange("n (j p) l -> p (n j) l", p=P)

        def dram(name, shape):
            return nc.dram_tensor(name, shape, F32, kind="Internal").ap()

        rows0_d = dram("rows0_d", [NB * S, ROW])
        rows1_d = dram("rows1_d", [NB * S, ROW1])
        x2_d = dram("x2_d", [NB * S, L])
        rows0_v = rows0_d.rearrange("(t p) l -> p t l", p=P)
        rows1_v = rows1_d.rearrange("(t p) l -> p t l", p=P)
        x2_v = x2_d.rearrange("(t p) l -> p t l", p=P)
        out_rows = out.rearrange("n s l -> (n s) l")

        bank = [es.enter_context(nc.psum_tensor(f"bank{i}", [P, 512], F32)) for i in range(8)]
        X = sb("X", [P, T, L])
        XL = sb("XL", [P, T, L])
        xl_flat = XL[:].rearrange("p t l -> p (t l)")
        big = sb("big", [P, 2 * QT * L])
        ident = sb("ident", [P, P])
        eps_t = sb("eps_t", [P, 1])
        gain_in = sb("gain_in", [P, 4])
        gain = sb("gain", [P, 4])
        stats = sb("stats", [P, T, 6])
        mv = [sb(f"mv{k}", [P, T, 2]) for k in range(4)]
        rstd = [sb(f"rstd{k}", [P, T, 1]) for k in range(4)]
        W = sb("W", [P, 3, TB, S])
        WB = sb("WB", [P, 3, TB])
        vbg = sb("vbg", [P, TB])
        qkv = sb("qkv", [P, 4 * TB * L])
        qT, kT, C = (qkv[:, k * TB * L:(k + 1) * TB * L].rearrange("p (j l) -> p j l", j=TB) for k in (0, 1, 3))
        v = qkv[:, 2 * TB * L:3 * TB * L].rearrange("p (j e) -> p j e", j=QT)
        attn = big[:, 0:QT * L].rearrange("p (j l) -> p j l", j=QT)
        attnT = big[:, QT * L:].rearrange("p (j l) -> p j l", j=QT)
        negmax = sb("negmax", [P, QT])
        sumexp = sb("sumexp", [P, QT])
        rsum = sb("rsum", [P, QT])
        XN = [sb(f"XN{b}", [P, L]) for b in range(2)]
        XT = [sb(f"XT{b}", [P, KC, P]) for b in range(2)]
        gate0_sb = sb("gate0_sb", [P, KC, E0])
        gate1_sb = sb("gate1_sb", [P, KC, E1])
        simd = sb("simd", [P, P])
        below = sb("below", [P, P], BF16)
        ones_b = sb("ones_b", [P, P], BF16)
        iota_e = sb("iota_e", [P, E0])
        iota_p = sb("iota_p", [P, P, TOPK], F16)
        iota_g = sb("iota_g", [P, G0 + 2, TOPK], F16)
        ones_e = sb("ones_e", [P, E0])
        token1 = sb("token1", [P, T])
        lg = sb("lg", [P, T, E0])
        e32 = sb("e32", [P, T, E0])
        v8 = sb("v8", [P, T, TOPK])
        i8 = sb("i8", [P, T, TOPK], U32)
        i8f = sb("i8f", [P, T, TOPK])
        e8 = sb("e8", [P, T, TOPK])
        t16 = sb("t16", [P, T])
        fw = sb("fw", [P, T, TOPK])
        act8 = sb("act8", [P, T, TOPK])
        cand = sb("cand", [P, T, 4, PRIM])
        best = sb("best", [P, T, 4])
        sel = sb("sel", [P, T, 4, PRIM])
        left = sb("left", [P, T, 4])
        keep = sb("keep", [P, T, 4])
        moved = sb("moved", [P, T, 4])
        madd4 = sb("madd4", [P, T, 4, PRIM])
        comb = sb("comb", [P, T, E0])
        chosen = sb("chosen", [P, T, E0], BF16)
        cnt_i = sb("cnt_i", [P, E0], I32)
        tiles = sb("tiles", [P, E0])
        tiles_cum = sb("tiles_cum", [P, E0])
        base = sb("base", [P, E0])
        gp = sb("gp", [P, T, E0])
        slot = sb("slot", [P, T, TOPK])
        slot_i = sb("slot_i", [P, T, TOPK], I32)
        part_i = sb("part_i", [P, T, TOPK], I32)
        slot_p = sb("slot_p", [P, T, TOPK], F16)
        slot_g = sb("slot_g", [P, T, TOPK], F16)
        hot_p = [sb(f"hot_p{b}", [P, P, TOPK], F16) for b in range(2)]
        hot_g = [sb(f"hot_g{b}", [P, G0 + 2, TOPK], F16) for b in range(2)]
        cum_col = sb("cum_col", [E0, 1])
        cum_diag = sb("cum_diag", [E0, E0])
        ended = sb("ended", [E0, G0 + 2], BF16)
        lst = sb("lst", [P, G0 + 2])
        lst_i = [sb(f"lst_i{k}", [P, G0 + 2], I32) for k in range(2)]
        lst2 = sb("lst2", [P, G0 + 2])
        zero_g = sb("zero_g", [P, G0 + 2], F16)
        tab = [sb(f"tab{k}", [1, G0 + 2], I32) for k in range(2)]
        done_i = [sb(f"done_i{k}", [1, E0], I32) for k in range(2)]
        pairs_f = sb("pairs_f", [1, 1])
        pairs_i = [sb(f"pairs_i{k}", [1, 1], I32) for k in range(2)]
        XG = [sb(f"XG{b}", [P, ROW]) for b in range(2)]
        gi = [sb(f"gi{b}", [P, 1], I32) for b in range(2)]
        si = [sb(f"si{b}", [P, 1], I32) for b in range(2)]
        XE = sb("XE", [P, KC, P])
        wbuf = sb("wbuf", [P, 2 * KC * 2 * F0 + 2 * 2 * L])
        wup = wbuf[:, 0:2 * KC * 2 * F0].rearrange("p (b c f) -> p b c f", b=2, c=KC)
        wdn = wbuf[:, 2 * KC * 2 * F0:].rearrange("p (b k l) -> p b k l", b=2, k=2)
        sw1_sb = wbuf[:, 0:KC * L].rearrange("p (c f) -> p c f", c=KC)
        sw2_sb = wbuf[:, KC * L:2 * KC * L].rearrange("p (c f) -> p c f", c=KC)
        sb1_bc = wbuf[:, 2 * KC * L:2 * KC * L + L]
        sb2_bc = wbuf[:, 2 * KC * L + L:2 * KC * L + 2 * L]
        b1_bc = xl_flat[:, 0:E1 * F1].rearrange("p (e f) -> p e f", e=E1)
        b2_bc = xl_flat[:, E1 * F1:E1 * (F1 + L)].rearrange("p (e f) -> p e f", e=E1)
        sg = sb("sg", [P, 512])
        hm = sb("hm", [P, 512])
        hT = sb("hT", [P, KC, P])
        Y = [sb(f"Y{b}", [P, L]) for b in range(2)]
        cw = [sb(f"cw{b}", [P, 1]) for b in range(2)]
        cbuf = sb("cbuf", [P, 2 * TB * L + 2 * KC * S])
        C4 = cbuf[:, 0:2 * TB * L].rearrange("p (b j l) -> p b j l", b=2, j=TB)
        CT = cbuf[:, 2 * TB * L:].rearrange("p (b c m) -> p b c m", b=2, c=KC)
        w1_sb = cbuf[:, 0:2 * KC * F1].rearrange("p (b c f) -> p b c f", b=2, c=KC)
        w2_sb = cbuf[:, 2 * KC * F1:].rearrange("p (b k l) -> p b k l", b=2, k=2)
        mask_u = sb("mask_u", [P, NB, S], U8)
        mmul = qkv[:, 0:NB * S].rearrange("p (n m) -> p n m", n=NB)
        madd = qkv[:, NB * S:].rearrange("p (n m) -> p n m", n=NB)
        vgain = sb("vgain", [P, NB])
        XT4 = big[:, 0:KC * S].rearrange("p (c s) -> p c s", c=KC)
        sc4, attn4, attnT4 = (big[:, KC * S + k * TB * S:KC * S + (k + 1) * TB * S].rearrange("p (j m) -> p j m", j=TB)
                              for k in range(3))
        negmax4 = sb("negmax4", [P, TB])
        sumexp4 = sb("sumexp4", [P, TB])
        rsum4 = sb("rsum4", [P, TB])

        class Log:
            def __init__(self, eng, name):
                self.eng, self.sem, self.n = eng, sem(name), 0

            def __call__(self, ins):
                ins.then_inc(self.sem, 1)
                self.n += 1

            def wait(self):
                self.eng.wait_ge(self.sem, self.n)

        x_in = [sem(f"x_in{i}") for i in range(4)]
        w_in = sem("w_in")
        r_in = sem("r_in")
        ctx_in = sem("ctx_in")
        const_ok = sem("const_ok")
        gain_ok = sem("gain_ok")
        vbg_ok = sem("vbg_ok")
        std_ok = [sem(f"std_ok{k}") for k in range(4)]
        rstd_ok = [sem(f"rstd_ok{k}") for k in range(4)]
        xl_ready = sem("xl_ready")
        vb_added = sem("vb_added")
        qk_mm, v_mm, s_mm, t_mm, a_mm = (sem(f"{k}_mm") for k in "qk v s t a".split())
        act1 = sem("act1")
        max_ready = sem("max_ready")
        rsum_ok = sem("rsum_ok")
        attn_ready = sem("attn_ready")
        dve1 = sem("dve1")
        st_ok = [sem(f"st_ok{k}") for k in range(4)]
        mv_ok = [sem(f"mv_ok{k}") for k in range(4)]
        x_st = sem("x_st")
        xn2, tr2, xt2, lg2 = sem("xn2"), sem("tr2"), sem("xt2"), sem("lg2")
        row_st = [sem(f"row_st{b}") for b in range(2)]
        exp_in, exp_ok = sem("exp_in"), sem("exp_ok")
        hot_ok, hotT, hotT_ok, simr = sem("hot_ok"), sem("hotT"), sem("hotT_ok"), sem("simr")
        comb_ok = sem("comb_ok")
        comb_st = sem("comb_st")
        chosen_ok, pos_mm = sem("chosen_ok"), sem("pos_mm")
        simr_ok = sem("simr_ok")
        hots_ok = [sem(f"hots_ok{m}") for m in range(2)]
        hots_scaled = [sem(f"hots_scaled{m}") for m in range(2)]
        hots_mm = [sem(f"hots_mm{m}") for m in range(2)]
        ended_ok, tab_mm = sem("ended_ok"), sem("tab_mm")
        lg_ok = sem("lg_ok")
        tab_ok = [sem(f"tab_ok{m}") for m in range(2)]
        lst_ok = sem("lst_ok")
        gathers_begun, adds_begun, pool_done, all_stored = (
            sem(k) for k in "gathers_begun adds_begun pool_done all_stored".split())
        mask_ok, vgain_ok = sem("mask_ok"), sem("vgain_ok")
        c4_in = [sem(f"c4_in{b}") for b in range(2)]
        x3_in = [sem(f"x3_in{q}") for q in range(4)]
        (xn4, x4_mm, xt4, s4_mm, sc_ok, max4, exp4, t4_mm, at4, rs4_ok, r4_mm, dve4) = (
            sem(k) for k in "xn4 x4_mm xt4 s4_mm sc_ok max4 exp4 t4_mm at4 rs4_ok r4_mm dve4".split())
        s_in, b_in, xn5, sb2_ok, sb2_added, yb_ok = (sem(k) for k in "s_in b_in xn5 sb2_ok sb2_added yb_ok".split())
        row1_st = [sem(f"row1_st{b}") for b in range(2)]
        out_st = [sem(f"out_st{b}") for b in range(2)]

        def expert_sems(m, names):
            return {n: sem(f"{n}{m}") for n in names.split()}

        per_tile = "tr_mm xe_ready up_mm hm_ready ht_mm ht_ready down_mm y_ready "
        sparse = per_tile + "wload_a wload_b weights_ready gath_a gath_b gi_ok si_ok cw_ok scattered "
        M0 = expert_sems("0", sparse + "act_ready")
        M1 = expert_sems("1", sparse + "pre_ok")
        MS = expert_sems("_shared", per_tile + "pre_ok")
        block = es.enter_context(nc.Block())

        hot = big[:].rearrange("p (t k e) -> p t k e", t=T, k=TOPK)
        wide = xl_flat[:, 0:T * TOPK * E0].rearrange("p (t k e) -> p t k e", t=T, k=TOPK)
        wide4 = xl_flat[:, 0:T * 4 * E0].rearrange("p (t k e) -> p t k e", t=T, k=4)
        hotT_sb = xl_flat[:, 4096:4096 + T * P].rearrange("p (t q) -> p t q", t=T)
        simr_sb = xl_flat[:, 6144:6144 + T * P].rearrange("p (t j e) -> p t j e", t=T, j=4)

        def pairs_of(eng, m, gmax):
            return eng.value_load(pairs_i[m][0:1, 0:1], min_val=0, max_val=gmax // 2 - 3) + 3

        @block.sync
        def _(sp):
            def context(n):
                return ctx[bass.ds(n, 1), :, :].rearrange("a (j p) l -> p (a j) l", p=P)

            for q in range(4):
                sp.dma_start(X[:, 4 * q:4 * q + 4, :], x_v[:, 4 * q:4 * q + 4, :]).then_inc(x_in[q], 16)
                if q == 0:
                    sp.dma_start(gain_in[:], gains.to_broadcast([P, 4])).then_inc(w_in, 16)
                    sp.dma_start(W[:], w_qkv).then_inc(w_in, 16)
                    sp.dma_start(WB[:], b_qkv).then_inc(w_in, 16)
                    sp.dma_start(C, context(0)).then_inc(ctx_in, 16)
            sp.dma_start(gate0_sb[:], gate0).then_inc(r_in, 16)
            sp.dma_start(gate1_sb[:], gate1).then_inc(r_in, 16)
            sp.wait_ge(const_ok, 4)
            for j in range(4):
                sp.dma_start(simd[j * E0:(j + 1) * E0, j * E0:(j + 1) * E0], sim).then_inc(r_in, 16)
            sp.dma_start(mask_u[:], mask.rearrange("(a n) m -> a n m", a=1).to_broadcast([P, NB, S])).then_inc(r_in, 16)
            with sp.Fori(0, NB - 1) as i:
                sp.wait_ge(v_mm, at(i, 2, 2))
                sp.dma_start(C, context(i + 1)).then_inc(ctx_in, 16)

            sp.wait_ge(dve1, 6 * NB + 6)
            sp.dma_start(x2_v, X[:]).then_inc(x_st, 16)
            with sp.Fori(0, TB * NB // 2) as i:
                for b in range(2):
                    sp.wait_ge(xn2, at(i, 2, b + 1))
                    sp.dma_start(rows0_v[:, bass.ds(i * 2 + b, 1), 0:L],
                                 XN[b][:].rearrange("p (a l) -> p a l", a=1)).then_inc(row_st[b], 16)
            sp.wait_ge(comb_ok, 1)
            sp.dma_start(rows0_v[:, :, L:ROW], comb[:]).then_inc(comb_st, 16)

            def load_weights(M, m, n_experts, load):
                def one(e, b, wait):
                    if wait is not None:
                        sp.wait_ge(M["down_mm"], wait)
                    load(e, b, (M["wload_a"], M["wload_b"])[b])

                for b in range(2):
                    one(b, b, None)
                sp.wait_ge(M["wload_a"], 32)
                sp.sem_inc(M["weights_ready"], 1)
                sp.wait_ge(M["wload_b"], 32)
                sp.sem_inc(M["weights_ready"], 1)
                with sp.Fori(0, n_experts // 2 - 1) as i:
                    for b in range(2):
                        done = sp.value_load(done_i[m][0:1, bass.ds(i * 2 + b, 1)], min_val=1, max_val=G0 + 1)
                        one(i * 2 + 2 + b, b, done)
                        sp.wait_ge((M["wload_a"], M["wload_b"])[b], at(i, 32, 64))
                        sp.sem_inc(M["weights_ready"], 1)

            def load0(e, b, s):
                sp.dma_start(wup[:, b:b + 1, :, :], w_up[bass.ds(e, 1), :, :, :].rearrange("e p c f -> p e c f")).then_inc(s, 16)
                sp.dma_start(wdn[0:FH, b:b + 1, :, :], w_down[bass.ds(e, 1), :, :, :].rearrange("e p k l -> p e k l")).then_inc(s, 16)

            sp.wait_ge(tab_ok[0], 1)
            load_weights(M0, 0, E0, load0)

            def load_ctx4(n, b):
                sp.dma_start(C4[:, b, :, :], context(n)).then_inc(c4_in[b], 16)
                sp.dma_start(CT[:, b:b + 1, :, :], ctx_t[bass.ds(n, 1), :, :, :].rearrange("a p c m -> p a c m")).then_inc(c4_in[b], 16)

            load_ctx4(0, 0)
            load_ctx4(1, 1)
            pairs0 = pairs_of(sp, 0, G0)
            sp.wait_ge(M0["scattered"], pairs0 * 32)
            for q in range(4):
                sp.dma_start(X[:, 4 * q:4 * q + 4, :], x2_v[:, 4 * q:4 * q + 4, :]).then_inc(x3_in[q], 16)
            sp.dma_start(sw1_sb, sw1).then_inc(s_in, 16)
            sp.dma_start(sw2_sb, sw2).then_inc(s_in, 16)
            sp.dma_start(sb1_bc, sb1.to_broadcast([P, L])).then_inc(s_in, 16)
            sp.dma_start(sb2_bc, sb2.to_broadcast([P, L])).then_inc(s_in, 16)
            sp.dma_start(b1_bc, b1.to_broadcast([P, E1 * F1]).rearrange("p (e f) -> p e f", e=E1)).then_inc(b_in, 16)
            sp.dma_start(b2_bc, b2.to_broadcast([P, E1 * L]).rearrange("p (e f) -> p e f", e=E1)).then_inc(b_in, 16)
            with sp.Fori(0, NB // 2 - 1) as i:
                for b in range(2):
                    sp.wait_ge(r4_mm, at(i, 4, 2 * b + 2))
                    load_ctx4(i * 2 + 2 + b, b)
            def store_row1(t, b, n):
                sp.wait_ge(xn5, n)
                sp.dma_start(rows1_v[:, bass.ds(t, 1), 0:L],
                             XN[b][:].rearrange("p (a l) -> p a l", a=1)).then_inc(row1_st[b], 16)

            def store_out(t, b, n):
                sp.wait_ge(MS["y_ready"], n)
                sp.dma_start(out_v[:, bass.ds(t, 1), :],
                             Y[b][:].rearrange("p (a l) -> p a l", a=1)).then_inc(out_st[b], 16)

            for b in range(2):
                store_row1(b, b, b + 1)
            with sp.Fori(0, T // 2 - 1) as i:
                for b in range(2):
                    store_row1(i * 2 + 2 + b, b, at(i, 2, 3 + b))
                    store_out(i * 2 + b, b, at(i, 2, 3 + b))
            for b in range(2):
                store_out(T - 2 + b, b, T + 1 + b)
            sp.wait_ge(comb_ok, 2)
            sp.dma_start(rows1_v[:, :, L:ROW1], comb[:, :, 0:E1]).then_inc(comb_st, 16)

            def load1(e, b, s):
                sp.dma_start(w1_sb[:, b:b + 1, :, :], w1[bass.ds(e, 1), :, :, :].rearrange("e p c f -> p e c f")).then_inc(s, 16)
                sp.dma_start(w2_sb[:, b:b + 1, :, :], w2[bass.ds(e, 1), :, :, :].rearrange("e p k l -> p e k l")).then_inc(s, 16)

            sp.wait_ge(tab_ok[1], 1)
            load_weights(M1, 1, E1, load1)
            pairs1 = pairs_of(sp, 1, G1)
            for s in row_st + row1_st + out_st:
                sp.wait_ge(s, 16 * T // 2)
            sp.wait_ge(M1["scattered"], pairs1 * 32)
            sp.sem_inc(all_stored, 1)
            sp.wait_ge(comb_st, 32)
            sp.wait_ge(x_st, 16)

        @block.gpsimd
        def _(pool):
            pool.memset(ident[:], 0.0).then_inc(const_ok, 1)
            pool.memset(eps_t[:], EPS).then_inc(const_ok, 1)
            pool.memset(ones_b[:], 1.0).then_inc(const_ok, 1)
            pool.memset(simd[:], 0.0).then_inc(const_ok, 1)
            pool.memset(below[:], 1.0).then_inc(const_ok, 1)
            pool.wait_ge(const_ok, 5)
            pool.affine_select(out=ident[:], in_=ident[:], compare_op=ALU.not_equal, fill=1.0, base=0,
                               pattern=[[-1, P]], channel_multiplier=1).then_inc(const_ok, 1)
            pool.affine_select(out=below[:], in_=below[:], compare_op=ALU.is_gt, fill=0.0, base=0,
                               pattern=[[1, P]], channel_multiplier=-1).then_inc(const_ok, 1)
            pool.wait_ge(vbg_ok, 1)
            with pool.Fori(0, NB) as n:
                for j in range(TB):
                    pool.wait_ge(xl_ready, at(n, TB, j + 1))
                    xt = X[:, bass.ds(n * TB + j, 1), :]
                    pool.tensor_tensor(xt, xt, vbg[:, j:j + 1].unsqueeze(1).to_broadcast([P, 1, L]),
                                       ALU.add).then_inc(vb_added, 1)
            ints = dict(allow_small_or_imprecise_dtypes=True)
            pool.iota(iota_e[:], pattern=[[1, E0]], base=0, channel_multiplier=0, **ints).then_inc(const_ok, 1)
            pool.iota(iota_p[:], pattern=[[1, P], [0, TOPK]], base=0, channel_multiplier=0, **ints).then_inc(const_ok, 1)
            pool.iota(iota_g[:], pattern=[[1, G0 + 2], [0, TOPK]], base=0, channel_multiplier=0, **ints).then_inc(const_ok, 1)
            pool.iota(token1[:], pattern=[[P, T]], base=1, channel_multiplier=1, **ints).then_inc(const_ok, 1)
            pool.memset(ones_e[:], 1.0).then_inc(const_ok, 1)
            pool.memset(zero_g[:], 0.0).then_inc(const_ok, 1)
            pool.memset(XG[0][:], 0.0).then_inc(const_ok, 1)
            pool.memset(XG[1][:], 0.0).then_inc(const_ok, 1)
            pool.wait_ge(r_in, 16 * 7)
            pool.affine_select(out=simd[:], in_=simd[:], compare_op=ALU.not_equal, fill=1.0, base=0,
                               pattern=[[-1, P]], channel_multiplier=1).then_inc(const_ok, 1)
            pool.wait_ge(dve1, 6 * NB + 6)
            pool.tensor_copy(mmul, mask_u[:]).then_inc(mask_ok, 1)
            pool.wait_ge(mask_ok, 1)
            pool.tensor_scalar(madd, mmul, 1e30, -1e30, ALU.mult, ALU.add).then_inc(mask_ok, 1)
            pool.wait_ge(vgain_ok, 1)
            pool.tensor_scalar(mmul, mmul, float(L) ** -0.5, None, ALU.mult).then_inc(mask_ok, 1)

            def experts(M, m, width, rows, dest, gmax):
                pool.wait_ge(lst_ok, m + 1)
                gath = (M["gath_a"], M["gath_b"])

                def gather(g, b, count):
                    pool.tensor_copy(gi[b][:], lst_i[m][:, bass.ds(g, 1)]).then_inc(M["gi_ok"], 1)
                    pool.wait_ge(M["gi_ok"], count)
                    pool.sem_inc(gathers_begun, 1)
                    pool.indirect_dma_start(out=XG[b][:, 0:width], out_offset=None, in_=rows,
                                            in_offset=bass.IndirectOffsetOnAxis(ap=gi[b][:, 0:1], axis=0),
                                            bounds_check=NB * S - 1, oob_is_err=False).then_inc(gath[b], 16)

                gather(0, 0, 1)
                gather(1, 1, 2)
                pairs = pairs_of(pool, m, gmax)

                def take(g, b, n):
                    pool.wait_ge(M["tr_mm"], n)
                    pool.wait_ge(M["cw_ok"], n)
                    gather(g + 2, b, n + 2)

                def add(g, b, n, added):
                    if added is not None:
                        pool.wait_ge(M["scattered"], added)
                    pool.tensor_copy(si[b][:], lst_i[m][:, bass.ds(g, 1)]).then_inc(M["si_ok"], 1)
                    pool.wait_ge(M["si_ok"], n)
                    pool.wait_ge(M["y_ready"], n + 2)
                    pool.sem_inc(adds_begun, 1)
                    pool.indirect_dma_start(out=dest, out_offset=bass.IndirectOffsetOnAxis(ap=si[b][:, 0:1], axis=0),
                                            in_=Y[b][:], in_offset=None, bounds_check=NB * S - 1,
                                            oob_is_err=False, compute_op=ALU.add).then_inc(M["scattered"], 16)

                take(0, 0, 1)
                take(1, 1, 2)
                add(0, 0, 1, None)
                take(2, 0, 3)
                add(1, 1, 2, 16)
                with pool.Fori(1, pairs - 1) as i:
                    for b in range(2):
                        take(i * 2 + b + 1, 1 - b, at(i, 2, b + 2))
                        add(i * 2 + b, b, at(i, 2, b + 1), at(i, 32, 16 * b))
                take(pairs * 2 - 1, 1, pairs * 2)
                add(pairs * 2 - 2, 0, pairs * 2 - 1, pairs * 32 - 32)
                add(pairs * 2 - 1, 1, pairs * 2, pairs * 32 - 16)
                for b in range(2):
                    pool.wait_ge(gath[b], at(pairs, 16, 16))
                pool.sem_inc(pool_done, 1)

            for b in range(2):
                pool.wait_ge(row_st[b], 16 * T // 2)
            pool.wait_ge(comb_st, 16)
            pool.wait_ge(x_st, 16)
            experts(M0, 0, ROW, rows0_d, x2_d, G0)

            pool.wait_ge(sb2_ok, 1)
            with pool.Fori(0, T) as t:
                pool.wait_ge(xn5, at(t, 1, 1))
                pool.tensor_tensor(X[:, bass.ds(t, 1), :], X[:, bass.ds(t, 1), :],
                                   sb2_bc.rearrange("p (a l) -> p a l", a=1), ALU.add).then_inc(sb2_added, 1)
            for b in range(2):
                pool.wait_ge(row1_st[b], 16 * T // 2)
                pool.wait_ge(out_st[b], 16 * T // 2)
            pool.wait_ge(comb_st, 32)
            experts(M1, 1, ROW1, rows1_d, out_rows, G1)

        @block.scalar
        def _(act):
            act.wait_ge(w_in, 48)
            act.activation(gain[:], gain_in[:], ACT.Tanh).then_inc(gain_ok, 1)
            act.wait_ge(gain_ok, 1)
            act.activation(vbg[:], WB[:, 2, :], ACT.Copy, scale=gain[:, 0:1]).then_inc(vbg_ok, 1)
            act.wait_ge(const_ok, 2)

            def roots(k, lo, hi, count):
                act.wait_ge(mv_ok[k], count)
                act.activation(rstd[k][:, lo:hi, :], mv[k][:, lo:hi, 1:2], ACT.Sqrt,
                               bias=eps_t[:, 0:1]).then_inc(std_ok[k], 1)

            for q in range(4):
                roots(0, 4 * q, 4 * q + 4, 4 * q + 4)

            def project(n):
                for j in range(4):
                    act.wait_ge(qk_mm, at(n, 4, j + 1))
                    dst, b = (qT, 0) if j < 2 else (kT, 1)
                    act.activation(dst[:, j % 2, :], bank[j][:], ACT.Identity,
                                   bias=WB[:, b, j % 2:j % 2 + 1]).then_inc(act1, 1)

            def values(n):
                for j in range(2):
                    act.wait_ge(v_mm, at(n, 2, j + 1))
                    act.activation(v[:, 2 * j:2 * j + 2, :], bank[2 + j][:].rearrange("p (a e) -> p a e", a=2),
                                   ACT.Copy).then_inc(act1, 1)

            def exps(n):
                for j in range(QT):
                    act.wait_ge(max_ready, at(n, QT, j + 1))
                    act.activation(attn[:, j, :], bank[4 + j][:], ACT.Exp, bias=negmax[:, j:j + 1],
                                   accum_out=sumexp[:, j:j + 1]).then_inc(act1, 1)

            project(0)
            values(0)
            exps(0)
            with act.Fori(0, NB - 1) as i:
                project(i + 1)
                values(i + 1)
                exps(i + 1)

            roots(1, 0, T, T)

            def evac2(b, n):
                act.wait_ge(tr2, n)
                act.activation(XT[b][:], bank[b][:].rearrange("p (c q) -> p c q", c=KC), ACT.Copy).then_inc(xt2, 1)

            def evac_logits2(t, b, n):
                act.wait_ge(lg2, n)
                act.activation(lg[:, bass.ds(t, 1), :], bank[4 + b][:, 0:E0].rearrange("p (a e) -> p a e", a=1),
                               ACT.Copy).then_inc(lg_ok, 1)

            act.sem_inc(lg_ok, 2)
            evac2(0, 1)
            with act.Fori(0, T // 2 - 1) as i:
                evac2(1, at(i, 2, 2))
                evac_logits2(i * 2, 0, at(i, 2, 1))
                evac2(0, at(i, 2, 3))
                evac_logits2(i * 2 + 1, 1, at(i, 2, 2))
            evac2(1, T)
            evac_logits2(T - 2, 0, T - 1)
            evac_logits2(T - 1, 1, T)
            act.wait_ge(exp_in, 2)
            act.activation(e32[:], e32[:], ACT.Exp).then_inc(exp_ok, 1)
            act.activation(e8[:], e8[:], ACT.Exp).then_inc(exp_ok, 1)
            for q in range(4):
                act.wait_ge(hotT, q + 1)
                act.activation(hotT_sb[:, 4 * q:4 * q + 4, :], bank[q][:].rearrange("p (t q) -> p t q", t=4),
                               ACT.Copy).then_inc(hotT_ok, 1)
            for q in range(4):
                act.wait_ge(simr, q + 1)
                act.activation(simr_sb[:, 4 * q:4 * q + 4, :, :],
                               bank[4 + q][:].rearrange("p (t j e) -> p t j e", t=4, j=4),
                               ACT.Copy).then_inc(simr_ok, 1)

            def scale_places(m, K):
                with act.Fori(0, T // 2) as i:
                    for b in range(2):
                        act.wait_ge(hots_ok[m], at(i, 4, 2 * b + 1))
                        act.activation(hot_p[b][:, :, 0:K], hot_p[b][:, :, 0:K], ACT.Copy,
                                       scale=token1[:, bass.ds(i * 2 + b, 1)]).then_inc(hots_scaled[m], 1)

            scale_places(0, TOPK)

            def take_rows(M, n):
                act.wait_ge(M["tr_mm"], n)
                act.activation(XE[:], bank[0][:].rearrange("p (c q) -> p c q", c=KC), ACT.Copy).then_inc(M["xe_ready"], 1)

            def silu(g1):
                act.wait_ge(M0["up_mm"], g1)
                act.activation(sg[:, 0:F0], bank[1][:, 0:F0], ACT.Silu).then_inc(M0["act_ready"], 1)

            act.wait_ge(tab_ok[0], 1)
            pairs0 = pairs_of(act, 0, G0)
            take_rows(M0, 1)
            silu(1)
            take_rows(M0, 2)
            with act.Fori(0, pairs0 - 1) as i:
                for b in range(2):
                    silu(at(i, 2, 2 + b))
                    take_rows(M0, at(i, 2, 3 + b))
            silu(at(pairs0, 2, 0))

            roots(2, 0, T, T)

            def evac4(n):
                for j in range(TB):
                    act.wait_ge(x4_mm, at(n, 2, j + 1))
                    act.activation(XT4[:, :, j * P:(j + 1) * P], bank[j][:].rearrange("p (c q) -> p c q", c=KC),
                                   ACT.Copy).then_inc(xt4, 1)

            def evac_attn4(n):
                act.wait_ge(t4_mm, at(n, 1, 1))
                act.activation(attnT4, bank[2][:].rearrange("p (m s) -> p m s", m=2), ACT.Copy).then_inc(at4, 1)

            def exps4(n):
                for j in range(TB):
                    act.wait_ge(max4, at(n, 2, j + 1))
                    act.activation(attn4[:, j, :], sc4[:, j, :], ACT.Exp, bias=negmax4[:, j:j + 1],
                                   accum_out=sumexp4[:, j:j + 1]).then_inc(exp4, 1)

            evac4(0)
            exps4(0)
            with act.Fori(0, NB - 1) as i:
                evac4(i + 1)
                evac_attn4(i)
                exps4(i + 1)
            evac_attn4(NB - 1)

            roots(3, 0, T, T)

            def gelu(M, g1, width):
                act.wait_ge(M["pre_ok"], g1)
                act.activation(hm[:, 0:width], sg[:, 0:width], ACT.Gelu).then_inc(M["hm_ready"], 1)

            take_rows(MS, 1)
            gelu(MS, 1, L)
            take_rows(MS, 2)
            with act.Fori(0, T // 2 - 1) as i:
                for b in range(2):
                    gelu(MS, at(i, 2, 2 + b), L)
                    take_rows(MS, at(i, 2, 3 + b))
            gelu(MS, T, L)
            act.wait_ge(exp_in, 3)
            act.activation(e8[:, :, 0:1], e8[:, :, 0:1], ACT.Exp).then_inc(exp_ok, 1)

            scale_places(1, K1)

            act.wait_ge(tab_ok[1], 1)
            pairs1 = pairs_of(act, 1, G1)
            take_rows(M1, 1)
            gelu(M1, 1, F1)
            take_rows(M1, 2)
            with act.Fori(0, pairs1 - 1) as i:
                for b in range(2):
                    gelu(M1, at(i, 2, 2 + b), F1)
                    take_rows(M1, at(i, 2, 3 + b))
            gelu(M1, at(pairs1, 2, 0), F1)

        @block.tensor
        def _(pe):
            def project(n):
                pe.wait_ge(ctx_in, at(n, 16, 16))
                pe.wait_ge(xl_ready, at(n, 2, 2))
                for j in range(4):
                    w, e = j // 2, j % 2
                    for d in range(TB):
                        rhs = XL[:, bass.ds(n * TB + d, 1), :] if w == 0 else C[:, d, :]
                        mm = pe.matmul(bank[j][:], W[:, w, d, e * P:(e + 1) * P], rhs,
                                       start=(d == 0), stop=(d == TB - 1))
                    mm.then_inc(qk_mm, 1)

            def values(n):
                pe.wait_ge(act1, at(n, 10, 4))
                for lt in range(QT):
                    for d in range(TB):
                        mm = pe.matmul(bank[2 + lt // 2][:, (lt % 2) * S:(lt % 2 + 1) * S],
                                       C[:, d, lt * P:(lt + 1) * P], W[:, 2, d, :],
                                       start=(d == 0), stop=(d == TB - 1))
                    if lt % 2:
                        mm.then_inc(v_mm, 1)

            def scores(n, first):
                for j in range(QT):
                    if not first:
                        pe.wait_ge(dve1, at(n - 1, 6, 6 + j + 1))
                    for e in range(TB):
                        mm = pe.matmul(bank[4 + j][:], qT[:, e, j * P:(j + 1) * P], kT[:, e, :],
                                       start=(e == 0), stop=(e == TB - 1))
                    mm.then_inc(s_mm, 1)

            def transposes(n):
                for j in range(QT):
                    pe.wait_ge(attn_ready, at(n, QT, j + 1))
                    for k in range(QT):
                        mm = pe.transpose(bank[4 + j][:, k * P:(k + 1) * P], attn[:, j, k * P:(k + 1) * P],
                                          ident[:])
                    mm.then_inc(t_mm, 1)

            def apply(n):
                pe.wait_ge(dve1, at(n, 6, 6 + 4))
                for d in range(TB):
                    for k in range(QT):
                        mm = pe.matmul(bank[d][:], v[:, k, d * P:(d + 1) * P], attnT[:, k, :],
                                       start=(k == 0), stop=(k == QT - 1))
                    mm.then_inc(a_mm, 1)

            pe.wait_ge(const_ok, 7)
            pe.wait_ge(w_in, 48)
            project(0)
            values(0)
            scores(0, True)
            with pe.Fori(0, NB - 1) as i:
                pe.wait_ge(dve1, at(i, 6, 6))
                pe.wait_ge(act1, at(i, 10, 6))
                project(i + 1)
                transposes(i)
                pe.wait_ge(act1, at(i, 10, 10 + 2))
                apply(i)
                values(i + 1)
                scores(i + 1, False)
            transposes(NB - 1)
            pe.wait_ge(dve1, 6 * NB)
            pe.wait_ge(act1, 10 * NB)
            apply(NB - 1)

            def transpose_tile(dst, src, done):
                for c in range(KC):
                    mm = pe.transpose(dst[:, c * P:(c + 1) * P], src[:, c * P:(c + 1) * P], ident[:])
                mm.then_inc(done, 1)

            def tr(b, n):
                pe.wait_ge(xn2, n)
                transpose_tile(bank[b], XN[b], tr2)

            def logits(b, n):
                pe.wait_ge(xt2, n)
                pe.wait_ge(lg_ok, n)
                for c in range(KC):
                    mm = pe.matmul(bank[4 + b][:, 0:E0], XT[b][:, c, :], gate0_sb[:, c, :],
                                   start=(c == 0), stop=(c == KC - 1))
                mm.then_inc(lg2, 1)

            pe.wait_ge(r_in, 32)
            pe.wait_ge(dve1, 6 * NB + 6)
            tr(0, 1)
            with pe.Fori(0, T // 2 - 1) as i:
                tr(1, at(i, 2, 2))
                logits(0, at(i, 2, 1))
                tr(0, at(i, 2, 3))
                logits(1, at(i, 2, 2))
            tr(1, T)
            logits(0, T - 1)
            logits(1, T)

            pe.wait_ge(hot_ok, 1)
            for t in range(T):
                mm = pe.transpose(bank[t // 4][:, (t % 4) * P:(t % 4 + 1) * P],
                                  hot[:, t, PRIM:TOPK, :].rearrange("p k e -> p (k e)"), ident[:])
                if t % 4 == 3:
                    mm.then_inc(hotT, 1)
            pe.wait_ge(const_ok, 16)
            for t in range(T):
                if t % 4 == 0:
                    pe.wait_ge(hotT_ok, t // 4 + 1)
                mm = pe.matmul(bank[4 + t // 4][:, (t % 4) * P:(t % 4 + 1) * P], hotT_sb[:, t, :], simd[:],
                               start=True, stop=True)
                if t % 4 == 3:
                    mm.then_inc(simr, 1)

            def positions(m, E):
                pe.wait_ge(chosen_ok, m + 1)
                ch = chosen[:, :, 0:E]
                out_pos = bank[0][:, 0:T * E].rearrange("p (t e) -> p t e", t=T)
                pe.matmul(out_pos, below[:], ch, start=True, stop=False)
                for t in range(T - 1):
                    later = T - 1 - t
                    pe.matmul(out_pos[:, t + 1:T, :], ones_b[:],
                              ch[:, t:t + 1, :].to_broadcast([P, later, E]), start=False, stop=False)
                pe.matmul(out_pos, zero_g[:, 0:P], ch, start=False, stop=True)
                for t in range(T):
                    mm = pe.matmul(bank[1][:, 0:E], ones_b[:], ch[:, t, :], start=(t == 0), stop=(t == T - 1))
                mm.then_inc(pos_mm, 1)

            def lists(m, E, K, G):
                pe.wait_ge(ended_ok, m + 1)
                pe.matmul(bank[3][0:1, 0:G + 2], ones_b[0:E, 0:1], ended[0:E, 0:G + 2], start=True,
                          stop=True).then_inc(tab_mm, 1)
                dst = bank[2][:, 0:G + 2]
                pe.sem_inc(hots_mm[m], 2)
                pe.matmul(dst, iota_p[:, :, 0], zero_g[:, 0:G + 2], start=True, stop=False)
                with pe.Fori(0, T // 2) as i:
                    for b in range(2):
                        pe.wait_ge(hots_ok[m], at(i, 4, 2 * b + 2))
                        pe.wait_ge(hots_scaled[m], at(i, 2, b + 1))
                        for k in range(K):
                            mm = pe.matmul(dst, hot_p[b][:, :, k], hot_g[b][:, 0:G + 2, k], start=False, stop=False)
                        mm.then_inc(hots_mm[m], 1)
                pe.matmul(dst, iota_p[:, :, 0], zero_g[:, 0:G + 2], start=False, stop=True).then_inc(hots_mm[m], 1)

            positions(0, E0)
            lists(0, E0, TOPK, G0)

            def down(M, b, ready, free, chunks, size, wd, last_wait):
                pe.wait_ge(M["ht_ready"], ready)
                pe.wait_ge(M["y_ready"], free)
                for k in range(chunks):
                    mm = pe.matmul(bank[3 + b][:], hT[0:size, k, :], wd(k), start=(k == 0), stop=(k == chunks - 1))
                mm.then_inc(M["down_mm"], 1)

            def hidden_transposes(M, n, chunks, size):
                pe.wait_ge(M["hm_ready"], n)
                for k in range(chunks):
                    mm = pe.transpose(bank[2][0:size, k * P:(k + 1) * P], hm[:, k * size:(k + 1) * size], ident[:])
                mm.then_inc(M["ht_mm"], 1)

            def experts(M, m, wu, wd, width, size, gmax):
                pe.sem_inc(M["down_mm"], 1)
                pairs = pairs_of(pe, m, gmax)
                gath = (M["gath_a"], M["gath_b"])
                n_exp = wu.shape[0]

                def expert_of(g):
                    return pe.value_load(tab[m][0:1, bass.ds(g, 1)], min_val=0, max_val=31)

                def tr(b, n):
                    pe.wait_ge(gath[b], n)
                    transpose_tile(bank[0], XG[b], M["tr_mm"])

                def place(w, e, k):
                    p = bass.ds((e % 2), 1)
                    return w[0:size if w is wd else P, p, k, :]

                def tile(g, b, gcount, i, first, last):
                    e = expert_of(g)
                    pe.wait_ge(M["weights_ready"], e + 1)
                    pe.wait_ge(M["xe_ready"], g + 1)
                    for c in range(KC):
                        mm = pe.matmul(bank[1][:, 0:width], XE[:, c, :], place(wu, e, c), start=(c == 0), stop=(c == KC - 1))
                    mm.then_inc(M["up_mm"], 1)
                    if not last:
                        tr(1 - b, gcount)
                    if not first:
                        ed = expert_of(g - 1)
                        down(M, 1 - b, g, g, 2, size, lambda k: place(wd, ed, k), None)
                    hidden_transposes(M, g + 1, 2, size)

                tr(0, 16)
                tile(0, 0, 16, 0, True, False)
                with pe.Fori(0, pairs - 1) as i:
                    tile(i * 2 + 1, 1, at(i, 16, 32), i, False, False)
                    tile(i * 2 + 2, 0, at(i, 16, 32), i, False, False)
                g = pairs * 2 - 1
                tile(g, 1, None, None, False, True)
                ed = expert_of(g)
                down(M, 1, g + 1, g + 1, 2, size, lambda k: place(wd, ed, k), None)
                return pairs

            pe.wait_ge(tab_ok[0], 1)
            pairs = experts(M0, 0, wup, wdn, 2 * F0, FH, G0)

            def tr4(n):
                pe.wait_ge(xn4, at(n, 2, 2))
                for j in range(TB):
                    transpose_tile(bank[j], XN[j], x4_mm)

            def scores4(n, b, cin):
                pe.wait_ge(c4_in[b], cin) if b is not None else None
                pe.wait_ge(xt4, at(n, 2, 2))
                for j in range(TB):
                    for c in range(KC):
                        mm = pe.matmul(bank[5 + j][:, 0:S], XT4[:, c, j * P:(j + 1) * P], CT[:, b, c, :],
                                       start=(c == 0), stop=(c == KC - 1))
                    mm.then_inc(s4_mm, 1)

            def attn_transposes4(n):
                pe.wait_ge(exp4, at(n, 2, 2))
                for j in range(TB):
                    for k in range(2):
                        mm = pe.transpose(bank[2][:, k * S + j * P:k * S + (j + 1) * P],
                                          attn4[:, j, k * P:(k + 1) * P], ident[:])
                mm.then_inc(t4_mm, 1)

            def read4(n, b):
                pe.wait_ge(at4, at(n, 1, 1))
                for j in range(TB):
                    for k in range(2):
                        mm = pe.matmul(bank[3 + j][:], attnT4[:, k, j * P:(j + 1) * P], C4[:, b, k, :],
                                       start=(k == 0), stop=(k == 1))
                    mm.then_inc(r4_mm, 1)

            pe.wait_ge(M0["y_ready"], at(pairs, 2, 2))
            tr4(0)
            scores4(0, 0, 32)

            def step4(n, b, cin):
                tr4(n + 1)
                attn_transposes4(n)
                pe.wait_ge(dve4, at(n, 2, 2))
                read4(n, b)
                scores4(n + 1, 1 - b, cin)

            with pe.Fori(0, NB // 2 - 1) as i:
                step4(i * 2, 0, at(i, 32, 32))
                step4(i * 2 + 1, 1, at(i, 32, 64))
            step4(NB - 2, 0, 16 * NB)
            attn_transposes4(NB - 1)
            pe.wait_ge(dve4, at(NB - 1, 2, 2))
            read4(NB - 1, 1)

            pe.wait_ge(dve4, 2 * NB + 2)
            pe.wait_ge(s_in, 64)

            def tr5(b, n):
                pe.wait_ge(xn5, n)
                transpose_tile(bank[0], XN[b], MS["tr_mm"])

            def tile5(g, b, first, last):
                pe.wait_ge(MS["xe_ready"], g + 1)
                for c in range(KC):
                    pe.matmul(bank[5][:, bass.ds(g * E1, E1)], XE[:, c, :], gate1_sb[:, c, :],
                              start=(c == 0), stop=(c == KC - 1))
                for c in range(KC):
                    mm = pe.matmul(bank[1][:], XE[:, c, :], sw1_sb[:, c, :], start=(c == 0), stop=(c == KC - 1))
                mm.then_inc(MS["up_mm"], 1)
                if not last:
                    tr5(1 - b, g + 2)
                if not first:
                    down(MS, 1 - b, g, g, KC, P, lambda k: sw2_sb[:, k, :], None)
                hidden_transposes(MS, g + 1, KC, P)

            tr5(0, 1)
            tile5(0, 0, True, False)
            with pe.Fori(0, T // 2 - 1) as i:
                tile5(i * 2 + 1, 1, False, False)
                tile5(i * 2 + 2, 0, False, False)
            tile5(T - 1, 1, False, True)
            down(MS, 1, T, T, KC, P, lambda k: sw2_sb[:, k, :], None)

            positions(1, E1)
            lists(1, E1, K1, G1)
            pe.wait_ge(tab_ok[1], 1)
            pe.wait_ge(MS["y_ready"], T + 2)
            experts(M1, 1, w1_sb, w2_sb, F1, P, G1)

        @block.vector
        def _(dve):
            dve.sem_inc(dve1, 6)
            dve.sem_inc(dve4, 2)
            for M in (M0, M1, MS):
                dve.sem_inc(M["y_ready"], 2)

            def tile_stats(k, t):
                dve.bn_stats(stats[:, bass.ds(t, 1), :], X[:, bass.ds(t, 1), :]).then_inc(st_ok[k], 1)

            def moments(k, lo, hi):
                dve.wait_ge(st_ok[k], hi)
                for t in range(lo, hi):
                    dve.bn_aggr(mv[k][:, t, :], stats[:, t, :]).then_inc(mv_ok[k], 1)

            def inverse(k, lo, hi, n):
                dve.wait_ge(std_ok[k], n)
                dve.reciprocal(rstd[k][:, lo:hi, :], rstd[k][:, lo:hi, :]).then_inc(rstd_ok[k], 1)
                dve.wait_ge(rstd_ok[k], n)

            def norm(k, dst, t, done):
                dve.tensor_scalar(dst, X[:, bass.ds(t, 1), :], mv[k][:, bass.ds(t, 1), 0:1], rstd[k][:, bass.ds(t, 1), 0:1],
                                  ALU.subtract, ALU.mult).then_inc(done, 1)

            for q in range(4):
                dve.wait_ge(x_in[q], 16)
                for t in range(4 * q, 4 * q + 4):
                    tile_stats(0, t)
                moments(0, 4 * q, 4 * q + 4)
                inverse(0, 4 * q, 4 * q + 4, q + 1)
                dve.wait_ge(mv_ok[0], 4 * q + 4)
                for t in range(4 * q, 4 * q + 4):
                    norm(0, XL[:, t:t + 1, :], t, xl_ready)

            def softmax(n):
                def scale(j):
                    dve.wait_ge(act1, at(n, 10, 7 + j))
                    dve.reciprocal(rsum[:, j:j + 1], sumexp[:, j:j + 1]).then_inc(rsum_ok, 1)
                    dve.wait_ge(rsum_ok, at(n, QT, j + 1))
                    dve.tensor_scalar(attn[:, j, :], attn[:, j, :], rsum[:, j:j + 1], None,
                                      ALU.mult).then_inc(attn_ready, 1)

                for j in range(QT):
                    dve.wait_ge(s_mm, at(n, QT, j + 1))
                    dve.tensor_reduce(negmax[:, j:j + 1], bank[4 + j][:], AX.X, ALU.max,
                                      negate=True).then_inc(max_ready, 1)
                    if j:
                        scale(j - 1)
                scale(QT - 1)

            def outputs(n):
                for j in range(QT):
                    dve.wait_ge(t_mm, at(n, QT, j + 1))
                    dve.tensor_copy(attnT[:, :, j * P:(j + 1) * P],
                                    bank[4 + j][:].rearrange("p (k q) -> p k q", k=QT)).then_inc(dve1, 1)
                for d in range(TB):
                    dve.wait_ge(a_mm, at(n, 2, d + 1))
                    dve.wait_ge(vb_added, at(n, 2, d + 1))
                    xt = X[:, bass.ds(n * TB + d, 1), :]
                    dve.scalar_tensor_tensor(out=xt, in0=bank[d][:].rearrange("p (a l) -> p a l", a=1),
                                             scalar=gain[:, 0:1], in1=xt, op0=ALU.mult, op1=ALU.add).then_inc(dve1, 1)

            def row_stats(k, n, d, own, count):
                dve.wait_ge(own, count)
                tile_stats(k, n * TB + d)

            softmax(0)
            with dve.Fori(0, NB - 1) as i:
                outputs(i)
                softmax(i + 1)
                for d in range(TB):
                    row_stats(1, i, d, dve1, at(i, 6, 6 + 5 + d))
            outputs(NB - 1)
            for d in range(TB):
                row_stats(1, NB - 1, d, dve1, at(NB - 1, 6, 6 + 5 + d))

            moments(1, 0, T)
            inverse(1, 0, T, 1)

            def xn_tile(k, t, b, done, free_mm, count, stored, scount):
                if free_mm is not None:
                    dve.wait_ge(free_mm, count)
                if stored is not None:
                    dve.wait_ge(stored, scount)
                norm(k, XN[b][:].rearrange("p (a l) -> p a l", a=1), t, done)

            dve.wait_ge(mv_ok[1], T)
            for b in range(2):
                xn_tile(1, b, b, xn2, None, 0, None, 0)
            with dve.Fori(0, T // 2 - 1) as i:
                for b in range(2):
                    xn_tile(1, i * 2 + 2 + b, b, xn2, tr2, at(i, 2, b + 1), row_st[b], at(i, 16, 16))

            R = Log(dve, "routing_steps")

            def run(ins):
                R(ins)
                R.wait()

            dve.wait_ge(mask_ok, 2)
            dve.tensor_reduce(vgain[:], mmul, AX.X, ALU.max).then_inc(vgain_ok, 1)
            dve.wait_ge(vgain_ok, 1)
            dve.tensor_scalar(vgain[:], vgain[:], gain[:, 1:2], None, ALU.mult).then_inc(vgain_ok, 1)

            dve.wait_ge(lg_ok, T + 2)
            dve.wait_ge(const_ok, 15)
            for t in range(T):
                R(dve.max(v8[:, t, :], lg[:, t, :]))
            R.wait()
            for t in range(T):
                R(dve.max_index(i8[:, t, :], v8[:, t, :], lg[:, t, :]))
            top = v8[:, :, 0:1]
            dve.tensor_tensor(e32[:], lg[:], top.to_broadcast([P, T, E0]), ALU.subtract).then_inc(exp_in, 1)
            dve.tensor_tensor(e8[:], v8[:], top.to_broadcast([P, T, TOPK]), ALU.subtract).then_inc(exp_in, 1)
            R.wait()
            run(dve.tensor_copy(i8f[:], i8[:]))

            def last(ap, n):
                return ap.unsqueeze(len(ap.shape)).to_broadcast(list(ap.shape) + [n])

            def third(ap, n):
                s = list(ap.shape)
                return ap.unsqueeze(2).to_broadcast([s[0], s[1], n, s[2]])

            iota_te = iota_e[:].unsqueeze(1).to_broadcast([P, T * TOPK, E0])
            dve.tensor_tensor(hot.rearrange("p t k e -> p (t k) e"), iota_te,
                              last(i8f[:].rearrange("p t k -> p (t k)"), E0), ALU.is_equal).then_inc(hot_ok, 1)
            dve.wait_ge(hot_ok, 1)
            dve.wait_ge(exp_ok, 2)
            run(dve.tensor_reduce(t16[:], e32[:], AX.X, ALU.add))
            run(dve.reciprocal(t16[:], t16[:]))
            run(dve.tensor_tensor(e8[:], e8[:], last(t16[:], TOPK), ALU.mult))
            run(dve.tensor_reduce(t16[:], e8[:], AX.X, ALU.add))
            run(dve.tensor_scalar(t16[:], t16[:], 1e-12, None, ALU.max))
            run(dve.reciprocal(t16[:], t16[:]))
            run(dve.tensor_tensor(fw[:], e8[:], last(t16[:], TOPK), ALU.mult))
            run(dve.tensor_scalar(fw[:], fw[:], gain[:, 2:3], None, ALU.mult))
            dve.wait_ge(simr_ok, 4)
            for j in range(4):
                run(dve.tensor_tensor(wide4, third(simr_sb[:, :, j, :], PRIM), hot[:, :, 0:PRIM, :], ALU.mult))
                run(dve.tensor_reduce(cand[:, :, j, :], wide4, AX.X, ALU.add))
            run(dve.tensor_reduce(best[:], cand[:], AX.X, ALU.max))
            run(dve.tensor_tensor(sel[:], cand[:], last(best[:], PRIM), ALU.is_equal))
            run(dve.tensor_scalar(left[:], sel[:, :, :, 0], -1.0, 1.0, ALU.mult, ALU.add))
            for i in range(1, PRIM):
                run(dve.tensor_tensor(sel[:, :, :, i], sel[:, :, :, i], left[:], ALU.mult))
                if i < PRIM - 1:
                    run(dve.tensor_tensor(left[:], left[:], sel[:, :, :, i], ALU.subtract))
            run(dve.tensor_scalar(keep[:], best[:], THRESHOLD, None, ALU.is_lt))
            run(dve.tensor_tensor(keep[:], fw[:, :, PRIM:TOPK], keep[:], ALU.mult))
            run(dve.tensor_tensor(moved[:], fw[:, :, PRIM:TOPK], keep[:], ALU.subtract))
            run(dve.tensor_copy(fw[:, :, PRIM:TOPK], keep[:]))
            run(dve.tensor_tensor(madd4[:], sel[:], last(moved[:], PRIM), ALU.mult))
            run(dve.tensor_reduce(left[:], madd4[:].rearrange("p t j i -> p t i j"), AX.X, ALU.add))
            run(dve.tensor_tensor(fw[:, :, 0:PRIM], fw[:, :, 0:PRIM], left[:], ALU.add))

            def dispatch(m, E, K, G, hots, room):
                f = fw[:, :, 0:K]
                run(dve.tensor_tensor(room, hots, last(f, E), ALU.mult))
                dve.tensor_reduce(comb[:, :, 0:E], room.rearrange("p t k e -> p t e k"), AX.X,
                                  ALU.add).then_inc(comb_ok, 1)
                dve.wait_ge(comb_ok, m + 1)
                dve.tensor_scalar(chosen[:, :, 0:E], comb[:, :, 0:E], 0.0, None, ALU.not_equal).then_inc(chosen_ok, 1)
                run(dve.tensor_scalar(act8[:, :, 0:K], f, 0.0, None, ALU.not_equal))
                dve.wait_ge(pos_mm, m + 1)
                ci, tl, cum, bs = cnt_i[:, 0:E], tiles[:, 0:E], tiles_cum[:, 0:E], base[:, 0:E]
                run(dve.tensor_scalar(ci, bank[1][:, 0:E], float(P - 1), None, ALU.add))
                run(dve.tensor_scalar(ci, ci, 7, None, ALU.arith_shift_right))
                run(dve.tensor_copy(tl, ci))
                run(dve.tensor_tensor_scan(cum, ones_e[:, 0:E], tl, 0.0, ALU.mult, ALU.add))
                run(dve.tensor_tensor(cum_diag[0:E, 0:E], cum[0:E, :], ident[0:E, 0:E], ALU.mult))
                run(dve.tensor_reduce(cum_col[0:E, :], cum_diag[0:E, 0:E], AX.X, ALU.add))
                dve.tensor_scalar(ended[0:E, 0:G + 2], iota_g[0:E, 0:G + 2, 0], cum_col[0:E, 0:1], None,
                                  ALU.is_ge).then_inc(ended_ok, 1)
                run(dve.tensor_scalar(done_i[m][:, 0:E], cum[0:1, :], 1.0, None, ALU.add))
                run(dve.tensor_scalar(pairs_i[m][:], cum[0:1, E - 1:E], 1.0, None, ALU.add))
                run(dve.tensor_scalar(pairs_i[m][:], pairs_i[m][:], 1, None, ALU.arith_shift_right))
                run(dve.tensor_copy(pairs_f[:], pairs_i[m][:]))
                run(dve.tensor_scalar(pairs_i[m][:], pairs_f[:], -3.0, 0.0, ALU.add, ALU.max))
                run(dve.tensor_tensor(bs, cum, tl, ALU.subtract))
                run(dve.tensor_scalar(bs, bs, float(P), None, ALU.mult))
                g = gp[:, :, 0:E]
                run(dve.tensor_tensor(g, bank[0][:, 0:T * E].rearrange("p (t e) -> p t e", t=T),
                                      bs.unsqueeze(1).to_broadcast([P, T, E]), ALU.add))
                run(dve.tensor_tensor(room, hots, third(g, K), ALU.mult))
                dve.wait_ge(tab_mm, m + 1)
                dve.tensor_scalar(tab[m][:, 0:G + 2], bank[3][0:1, 0:G + 2], float(E - 1), None,
                                  ALU.min).then_inc(tab_ok[m], 1)
                s, a = slot[:, :, 0:K], act8[:, :, 0:K]
                run(dve.tensor_reduce(s, room, AX.X, ALU.add))
                run(dve.tensor_scalar(s, s, 1.0, None, ALU.add))
                run(dve.tensor_tensor(s, s, a, ALU.mult))
                run(dve.tensor_scalar(slot_i[:, :, 0:K], s, -1.0, None, ALU.add))
                run(dve.tensor_scalar(part_i[:, :, 0:K], slot_i[:, :, 0:K], P - 1, None, ALU.bitwise_and))
                run(dve.tensor_scalar(slot_i[:, :, 0:K], slot_i[:, :, 0:K], 7, None, ALU.arith_shift_right))
                run(dve.tensor_copy(slot_p[:, :, 0:K], part_i[:, :, 0:K]))
                run(dve.tensor_copy(slot_g[:, :, 0:K], slot_i[:, :, 0:K]))
                with dve.Fori(0, T // 2) as i:
                    for b in range(2):
                        dve.wait_ge(hots_mm[m], at(i, 2, b + 1))
                        for dst, numbers, slots, n in ((hot_p[b], iota_p, slot_p, P), (hot_g[b], iota_g, slot_g, G + 2)):
                            dve.tensor_tensor(dst[:, 0:n, 0:K], numbers[:, 0:n, 0:K],
                                              slots[:, bass.ds(i * 2 + b, 1), 0:K].to_broadcast([P, n, K]),
                                              ALU.is_equal).then_inc(hots_ok[m], 1)
                dve.wait_ge(hots_mm[m], T + 3)
                run(dve.tensor_copy(lst[:, 0:G + 2], bank[2][:, 0:G + 2]))
                run(dve.tensor_scalar(lst2[:, 0:G + 2], lst[:, 0:G + 2], 0.0, float(NONE), ALU.is_equal, ALU.mult))
                dve.scalar_tensor_tensor(out=lst_i[m][:, 0:G + 2], in0=lst[:, 0:G + 2], scalar=-1.0, in1=lst2[:, 0:G + 2],
                                         op0=ALU.add, op1=ALU.add).then_inc(lst_ok, 1)

            dispatch(0, E0, TOPK, G0, hot, wide)

            def hidden_out(M, n, chunks, size):
                dve.wait_ge(M["ht_mm"], n)
                dve.tensor_copy(hT[0:size, 0:chunks, :],
                                bank[2][0:size, 0:chunks * P].rearrange("p (k q) -> p k q", k=chunks)).then_inc(M["ht_ready"], 1)

            def experts(M, m, gmax, size, middle, weighted, n_e, needs_expert):
                pairs = pairs_of(dve, m, gmax)
                gath = (M["gath_a"], M["gath_b"])

                def expert_of(g):
                    return dve.value_load(tab[m][0:1, bass.ds(g, 1)], min_val=0, max_val=n_e - 1)

                def y(g, b, early):
                    ed = expert_of(g) if needs_expert else None
                    dve.wait_ge(M["down_mm"], g + 2)
                    dve.wait_ge(M["cw_ok"], g + 1)
                    if not early:
                        dve.wait_ge(M["scattered"], g * 16 - 16)
                    weighted(g, b, ed)

                def weights(g, b, gcount):
                    e = expert_of(g)
                    dve.wait_ge(gath[b], gcount)
                    dve.wait_ge(M["y_ready"], g + 1)
                    dve.tensor_copy(cw[b][:], XG[b][:, bass.ds(e + L, 1)]).then_inc(M["cw_ok"], 1)

                def tile(g, b, ahead, early=False, first=False):
                    middle(g, expert_of(g) if needs_expert else None)
                    if not first:
                        y(g - 1, 1 - b, early)
                    if ahead is not None:
                        weights(g + 1, 1 - b, ahead)
                    hidden_out(M, g + 1, 2, size)

                weights(0, 0, 16)
                tile(0, 0, 16, True, True)
                tile(1, 1, 32, True)
                tile(2, 0, 32, True)
                with dve.Fori(1, pairs - 1) as i:
                    tile(i * 2 + 1, 1, at(i, 16, 32))
                    tile(i * 2 + 2, 0, at(i, 16, 32))
                g = pairs * 2 - 1
                tile(g, 1, None)
                y(g, 1, False)

            def middle0(g, e):
                dve.wait_ge(M0["act_ready"], g + 1)
                dve.tensor_tensor(hm[:, 0:F0], bank[1][:, F0:2 * F0], sg[:, 0:F0], ALU.mult).then_inc(M0["hm_ready"], 1)

            def weighted0(g, b, ed):
                dve.tensor_scalar(Y[b][:], bank[3 + b][:], cw[b][:, 0:1], None, ALU.mult).then_inc(M0["y_ready"], 1)

            dve.wait_ge(lst_ok, 1)
            experts(M0, 0, G0, FH, middle0, weighted0, E0, False)

            for q in range(4):
                dve.wait_ge(x3_in[q], 16)
                for t in range(4 * q, 4 * q + 4):
                    tile_stats(2, t)
            moments(2, 0, T)
            inverse(2, 0, T, 1)
            dve.wait_ge(mv_ok[2], T)
            dve.wait_ge(vgain_ok, 2)
            dve.wait_ge(mask_ok, 3)

            def norm4(n):
                for j in range(TB):
                    norm(2, XN[j][:].rearrange("p (a l) -> p a l", a=1), n * TB + j, xn4)

            def softmax4(n):
                for j in range(TB):
                    dve.wait_ge(s4_mm, at(n, 2, j + 1))
                    dve.tensor_tensor(sc4[:, j:j + 1, :], bank[5 + j][:, 0:S].rearrange("p (a m) -> p a m", a=1),
                                      mmul[:, bass.ds(n, 1), :], ALU.mult).then_inc(sc_ok, 1)
                    dve.wait_ge(sc_ok, at(n, 4, 2 * j + 1))
                    dve.tensor_tensor(sc4[:, j:j + 1, :], sc4[:, j:j + 1, :], madd[:, bass.ds(n, 1), :],
                                      ALU.add).then_inc(sc_ok, 1)
                    dve.wait_ge(sc_ok, at(n, 4, 2 * j + 2))
                    dve.tensor_reduce(negmax4[:, j:j + 1], sc4[:, j, :], AX.X, ALU.max, negate=True).then_inc(max4, 1)

            def read_out4(n):
                dve.wait_ge(exp4, at(n, 2, 2))
                dve.reciprocal(rsum4[:], sumexp4[:]).then_inc(rs4_ok, 1)
                dve.wait_ge(rs4_ok, at(n, 2, 1))
                dve.tensor_scalar(rsum4[:], rsum4[:], vgain[:, bass.ds(n, 1)], None, ALU.mult).then_inc(rs4_ok, 1)
                dve.wait_ge(rs4_ok, at(n, 2, 2))
                for j in range(TB):
                    dve.wait_ge(r4_mm, at(n, 2, j + 1))
                    xt = X[:, bass.ds(n * TB + j, 1), :]
                    dve.scalar_tensor_tensor(out=xt, in0=bank[3 + j][:].rearrange("p (a l) -> p a l", a=1),
                                             scalar=rsum4[:, j:j + 1], in1=xt, op0=ALU.mult, op1=ALU.add).then_inc(dve4, 1)

            def stats4(n):
                for j in range(TB):
                    row_stats(3, n, j, dve4, at(n, 2, 2 + j + 1))

            norm4(0)
            softmax4(0)
            dve.wait_ge(x4_mm, 2)
            norm4(1)
            with dve.Fori(0, NB - 2) as i:
                read_out4(i)
                softmax4(i + 1)
                dve.wait_ge(x4_mm, at(i, 2, 4))
                norm4(i + 2)
                stats4(i)
            read_out4(NB - 2)
            softmax4(NB - 1)
            stats4(NB - 2)
            read_out4(NB - 1)
            stats4(NB - 1)

            moments(3, 0, T)
            inverse(3, 0, T, 1)
            dve.wait_ge(mv_ok[3], T)
            dve.wait_ge(x4_mm, 2 * NB)
            dve.wait_ge(s_in, 64)
            dve.tensor_scalar(sb2_bc, sb2_bc, gain[:, 3:4], None, ALU.mult).then_inc(sb2_ok, 1)

            def y5_tile(g, b, free):
                dve.wait_ge(MS["down_mm"], g + 1)
                dve.wait_ge(sb2_added, g + 1)
                if free is not None:
                    dve.wait_ge(out_st[b], free)
                a1 = "p (a l) -> p a l"
                dve.scalar_tensor_tensor(out=Y[b][:].rearrange(a1, a=1), in0=bank[3 + b][:].rearrange(a1, a=1),
                                         scalar=gain[:, 3:4], in1=X[:, bass.ds(g, 1), :], op0=ALU.mult,
                                         op1=ALU.add).then_inc(MS["y_ready"], 1)

            def tile5(g, b, ahead, first, free):
                dve.wait_ge(MS["up_mm"], g + 1)
                dve.tensor_tensor(sg[:], bank[1][:], sb1_bc, ALU.add).then_inc(MS["pre_ok"], 1)
                if ahead is not None:
                    xn_tile(3, g + 2, b, xn5, MS["tr_mm"], g + 1, row1_st[b], ahead)
                if not first:
                    y5_tile(g - 1, 1 - b, free)
                hidden_out(MS, g + 1, KC, P)

            for b in range(2):
                xn_tile(3, b, b, xn5, None, 0, None, 0)
            tile5(0, 0, 16, True, None)
            tile5(1, 1, 16, False, None)
            tile5(2, 0, 32, False, None)
            with dve.Fori(0, T // 2 - 3) as i:
                tile5(i * 2 + 3, 1, at(i, 16, 32), False, at(i, 16, 16))
                tile5(i * 2 + 4, 0, at(i, 16, 48), False, at(i, 16, 16))
            tile5(T - 3, 1, 16 * (T // 2 - 1), False, 16 * (T // 2 - 2))
            tile5(T - 2, 0, None, False, 16 * (T // 2 - 2))
            tile5(T - 1, 1, None, False, 16 * (T // 2 - 1))
            y5_tile(T - 1, 1, 16 * (T // 2 - 1))

            dve.wait_ge(MS["down_mm"], T)
            run(dve.tensor_copy(lg[:, :, 0:E1], bank[5][:, 0:T * E1].rearrange("p (t e) -> p t e", t=T)))
            for t in range(T):
                R(dve.max(v8[:, t, :], lg[:, t, 0:E1]))
            R.wait()
            for t in range(T):
                R(dve.max_index(i8[:, t, :], v8[:, t, :], lg[:, t, 0:E1]))
            dve.tensor_tensor(e8[:, :, 0:1], v8[:, :, 1:2], v8[:, :, 0:1], ALU.subtract).then_inc(exp_in, 1)
            R.wait()
            run(dve.tensor_copy(i8f[:], i8[:]))
            hot1 = big[:, 0:T * K1 * E1].rearrange("p (t k e) -> p t k e", t=T, k=K1)
            for k in range(K1):
                run(dve.tensor_tensor(hot1[:, :, k, :], iota_e[:, 0:E1].unsqueeze(1).to_broadcast([P, T, E1]),
                                      last(i8f[:, :, k], E1), ALU.is_equal))
            dve.wait_ge(exp_ok, 3)
            run(dve.tensor_scalar(fw[:, :, 0:1], e8[:, :, 0:1], 1.0, None, ALU.add))
            run(dve.reciprocal(fw[:, :, 0:1], fw[:, :, 0:1]))
            run(dve.tensor_tensor(fw[:, :, 1:2], fw[:, :, 0:1], e8[:, :, 0:1], ALU.mult))
            run(dve.tensor_scalar(fw[:, :, 0:2], fw[:, :, 0:2], gain[:, 3:4], None, ALU.mult))
            n = T * K1 * E1
            dispatch(1, E1, K1, G1, hot1, xl_flat[:, 6144:6144 + n].rearrange("p (t k e) -> p t k e", t=T, k=K1))

            def middle1(g, e):
                dve.wait_ge(M1["up_mm"], g + 1)
                dve.tensor_tensor(sg[:, 0:F1].rearrange("p (a f) -> p a f", a=1),
                                  bank[1][:, 0:F1].rearrange("p (a f) -> p a f", a=1),
                                  b1_bc[:, bass.ds(e, 1), :], ALU.add).then_inc(M1["pre_ok"], 1)

            def weighted1(g, b, ed):
                a1 = "p (a l) -> p a l"
                dve.tensor_tensor(Y[b][:].rearrange(a1, a=1), bank[3 + b][:].rearrange(a1, a=1),
                                  b2_bc[:, bass.ds(ed, 1), :], ALU.add).then_inc(yb_ok, 1)
                dve.wait_ge(yb_ok, g + 1)
                dve.tensor_scalar(Y[b][:], Y[b][:], cw[b][:, 0:1], None, ALU.mult).then_inc(M1["y_ready"], 1)

            dve.wait_ge(b_in, 32)
            dve.wait_ge(lst_ok, 2)
            experts(M1, 1, G1, P, middle1, weighted1, E1, True)


def kernel(**inputs):
    import numpy as _np
    import concourse.bacc as _bacc
    from concourse import mybir as _mybir
    from concourse.bass_utils import run_bass_kernel_spmd as _run

    def chunks(a, n):
        return a.reshape(n, a.shape[0] // n, a.shape[1]).transpose(1, 0, 2)

    a = {k: _np.asarray(v) for k, v in inputs.items()}
    arrays = dict(
        x=a["x"], ctx=a["ctx_2048"],
        ctx_t=a["ctx_2048"].transpose(0, 2, 1).reshape(NB, KC, P, S).transpose(0, 2, 1, 3),
        mask=a["mask_BxS2_bk0"],
        gains=_np.concatenate([a["g_xattn"], a["g_ffn"]]).reshape(1, 4),
        w_qkv=_np.stack([chunks(a["L0_xattn_" + k + "W"].T, TB) for k in "QKV"], axis=1),
        b_qkv=_np.stack([a["L0_xattn_" + k + "b"].reshape(TB, P).T for k in "QKV"], axis=1),
        gate0=chunks(a["L0_ffn_gate_weight"].T, KC), sim=a["L0_ffn_similarity"],
        w_up=a["L0_ffn_gate_up_proj"].transpose(0, 2, 1).reshape(E0, KC, P, 2 * F0).transpose(0, 2, 1, 3),
        w_down=a["L0_ffn_down_proj"].transpose(0, 2, 1).reshape(E0, 2, FH, L).transpose(0, 2, 1, 3),
        gate1=chunks(a["L1_ffn_gate_w"], KC),
        w1=a["L1_ffn_w1"].reshape(E1, KC, P, F1).transpose(0, 2, 1, 3), b1=a["L1_ffn_b1"].reshape(1, E1 * F1),
        w2=a["L1_ffn_w2"].reshape(E1, 2, P, L).transpose(0, 2, 1, 3), b2=a["L1_ffn_b2"].reshape(1, E1 * L),
        sw1=chunks(a["L1_ffn_shared_w1"], KC), sb1=a["L1_ffn_shared_b1"].reshape(1, L),
        sw2=chunks(a["L1_ffn_shared_w2"], KC), sb2=a["L1_ffn_shared_b2"].reshape(1, L),
    )
    arrays = {k: _np.ascontiguousarray(v) for k, v in arrays.items()}
    nc = _bacc.Bacc("TRN2", target_bir_lowering=False, num_devices=1)
    aps = {k: nc.dram_tensor(k, v.shape, _mybir.dt.from_np(v.dtype), kind="ExternalInput").ap() for k, v in arrays.items()}
    aps["out"] = nc.dram_tensor("out", (NB, S, L), F32, kind="ExternalOutput").ap()
    flamingo_kernel(nc, **aps)
    r = _run(nc, [arrays], core_ids=[0])
    return r.results[0]["out"]
```

```python
import concourse.bass as bass
from concourse import mybir
from concourse.alu_op_type import AluOpType as ALU
from contextlib import ExitStack

F32 = mybir.dt.float32
F16 = mybir.dt.float16
BF16 = mybir.dt.bfloat16
I32 = mybir.dt.int32
U32 = mybir.dt.uint32
U8 = mybir.dt.uint8
ACT = mybir.ActivationFunctionType
AX = mybir.AxisListType

P = 128
NB, S, L = 8, 256, 512
T = NB * S // P
TB = S // P
KC = L // P
EPS = 1e-5

QT = L // P
E0, TOPK, PRIM, F0 = 32, 8, 4, 192
FH = F0 // 2
THRESHOLD = 0.5
ROW = L + E0
G0 = NB * S * TOPK // P + E0
E1, K1, F1 = 8, 2, 256
ROW1 = L + E1
G1 = NB * S * K1 // P + E1
PARTS = ((0, 2), (2, 6), (6, 10), (10, T))
LG_BANKS = ((7, 5), (7, 3))
NONE = 4096


def at(i, per, k):
    return i * per + k


def flamingo_kernel(nc, x, ctx, ctx_t, mask, gains, w_qkv, b_qkv, gate0, sim, w_up, w_down,
                    gate1, w1, b1, w2, b2, sw1, sb1, sw2, sb2, out):
    es = ExitStack()
    with es:
        def sb(name, shape, dt=F32):
            return es.enter_context(nc.sbuf_tensor(name, shape, dt))

        def sem(name):
            return es.enter_context(nc.semaphore(name))

        x_v = x.rearrange("n (j p) l -> p (n j) l", p=P)
        out_v = out.rearrange("n (j p) l -> p (n j) l", p=P)

        def dram(name, shape):
            return nc.dram_tensor(name, shape, F32, kind="Internal").ap()

        rows0_d = dram("rows0_d", [NB * S, ROW])
        rows1_d = dram("rows1_d", [NB * S, ROW1])
        x2_d = dram("x2_d", [NB * S, L])
        rows0_v = rows0_d.rearrange("(t p) l -> p t l", p=P)
        rows1_v = rows1_d.rearrange("(t p) l -> p t l", p=P)
        x2_v = x2_d.rearrange("(t p) l -> p t l", p=P)
        out_rows = out.rearrange("n s l -> (n s) l")

        bank = [es.enter_context(nc.psum_tensor(f"bank{i}", [P, 512], F32)) for i in range(8)]
        X = sb("X", [P, T, L])
        XL = sb("XL", [P, T, L])
        xl_flat = XL[:].rearrange("p t l -> p (t l)")
        big = sb("big", [P, 2 * QT * L])
        ident = sb("ident", [P, P])
        eps_t = sb("eps_t", [P, 1])
        gain_in = sb("gain_in", [P, 4])
        gain = sb("gain", [P, 4])
        stats = sb("stats", [P, T, 6])
        mv = [sb(f"mv{k}", [P, T, 2]) for k in range(4)]
        rstd = [sb(f"rstd{k}", [P, T, 1]) for k in range(4)]
        W = sb("W", [P, 3, TB, S])
        WB = sb("WB", [P, 3, TB])
        vbg = sb("vbg", [P, TB])
        qkv = sb("qkv", [P, 4 * TB * L])
        qT, kT, C = (qkv[:, k * TB * L:(k + 1) * TB * L].rearrange("p (j l) -> p j l", j=TB) for k in (0, 1, 3))
        v = qkv[:, 2 * TB * L:3 * TB * L].rearrange("p (j e) -> p j e", j=QT)
        attn = big[:, 0:QT * L].rearrange("p (j l) -> p j l", j=QT)
        attnT = big[:, QT * L:].rearrange("p (j l) -> p j l", j=QT)
        negmax = sb("negmax", [P, QT])
        sumexp = sb("sumexp", [P, QT])
        rsum = sb("rsum", [P, QT])
        XN = [sb(f"XN{b}", [P, L]) for b in range(2)]
        gate0_sb = sb("gate0_sb", [P, KC, E0])
        gate1_sb = sb("gate1_sb", [P, KC, E1])
        simd = sb("simd", [P, P])
        below = sb("below", [P, P], BF16)
        ones_b = sb("ones_b", [P, P], BF16)
        iota_e = sb("iota_e", [P, E0])
        iota_p = sb("iota_p", [P, P, TOPK], F16)
        iota_g = sb("iota_g", [P, G0 + 2, TOPK], F16)
        ones_e = sb("ones_e", [P, E0])
        token1 = sb("token1", [P, T])
        lg = sb("lg", [P, T, E0])
        e32 = sb("e32", [P, T, E0])
        v8 = sb("v8", [P, T, TOPK])
        i8 = sb("i8", [P, T, TOPK], U32)
        i8f = sb("i8f", [P, T, TOPK])
        e8 = sb("e8", [P, T, TOPK])
        t16 = sb("t16", [P, T])
        fw = sb("fw", [P, T, TOPK])
        act8 = sb("act8", [P, T, TOPK])
        cand = sb("cand", [P, T, 4, PRIM])
        best = sb("best", [P, T, 4])
        sel = sb("sel", [P, T, 4, PRIM])
        left = sb("left", [P, T, 4])
        keep = sb("keep", [P, T, 4])
        moved = sb("moved", [P, T, 4])
        madd4 = sb("madd4", [P, T, 4, PRIM])
        comb = sb("comb", [P, T, E0])
        chosen = sb("chosen", [P, T, E0], BF16)
        cnt_i = sb("cnt_i", [P, E0], I32)
        tiles = sb("tiles", [P, E0])
        tiles_cum = sb("tiles_cum", [P, E0])
        base = sb("base", [P, E0])
        gp = sb("gp", [P, T, E0])
        slot = sb("slot", [P, T, TOPK])
        slot_i = sb("slot_i", [P, T, TOPK], I32)
        part_i = sb("part_i", [P, T, TOPK], I32)
        slot_p = sb("slot_p", [P, T, TOPK], F16)
        slot_g = sb("slot_g", [P, T, TOPK], F16)
        hot_p = [sb(f"hot_p{b}", [P, P, TOPK], F16) for b in range(2)]
        hot_g = [sb(f"hot_g{b}", [P, G0 + 2, TOPK], F16) for b in range(2)]
        cum_col = sb("cum_col", [E0, 1])
        cum_diag = sb("cum_diag", [E0, E0])
        ended = sb("ended", [E0, G0 + 2], BF16)
        lst = sb("lst", [P, G0 + 2])
        lst_i = [sb(f"lst_i{k}", [P, G0 + 2], I32) for k in range(2)]
        lst2 = sb("lst2", [P, G0 + 2])
        zero_g = sb("zero_g", [P, G0 + 2], F16)
        tab = [sb(f"tab{k}", [1, G0 + 2], I32) for k in range(2)]
        done_i = [sb(f"done_i{k}", [1, E0], I32) for k in range(2)]
        pairs_f = sb("pairs_f", [1, 1])
        pairs_i = [sb(f"pairs_i{k}", [1, 1], I32) for k in range(2)]
        XG = [sb(f"XG{b}", [P, ROW]) for b in range(2)]
        gi = [sb(f"gi{b}", [P, 1], I32) for b in range(2)]
        si = [sb(f"si{b}", [P, 1], I32) for b in range(2)]
        XE = sb("XE", [P, KC, P])
        wbuf = sb("wbuf", [P, 2 * KC * 2 * F0 + 2 * 2 * L])
        wup = wbuf[:, 0:2 * KC * 2 * F0].rearrange("p (b c f) -> p b c f", b=2, c=KC)
        wdn = wbuf[:, 2 * KC * 2 * F0:].rearrange("p (b k l) -> p b k l", b=2, k=2)
        sw1_sb = wbuf[:, 0:KC * L].rearrange("p (c f) -> p c f", c=KC)
        sw2_sb = wbuf[:, KC * L:2 * KC * L].rearrange("p (c f) -> p c f", c=KC)
        sb1_c = wbuf[:, 2 * KC * L:2 * KC * L + KC]
        sb2_bc = wbuf[:, 2 * KC * L + L:2 * KC * L + 2 * L]
        b1_bc = wbuf[:, 0:E1 * F1].rearrange("p (e f) -> p e f", e=E1)
        b2_bc = qkv[:].rearrange("p (e f) -> p e f", e=E1)
        XT5 = xl_flat.rearrange("p (c q) -> p c q", c=KC)
        hT4 = [big[:, b * KC * L:(b + 1) * KC * L].rearrange("p (c q) -> p c q", c=KC) for b in range(2)]
        sg = sb("sg", [P, 512])
        hm = sb("hm", [P, 512])
        hT = sb("hT", [P, KC, P])
        Y = [sb(f"Y{b}", [P, L]) for b in range(2)]
        cw = sb("cw", [P, 4])
        cbuf = sb("cbuf", [P, 2 * TB * L + 2 * KC * S])
        C4 = cbuf[:, 0:2 * TB * L].rearrange("p (b j l) -> p b j l", b=2, j=TB)
        CT = cbuf[:, 2 * TB * L:].rearrange("p (b c m) -> p b c m", b=2, c=KC)
        w1_sb = cbuf[:, 0:2 * KC * F1].rearrange("p (b c f) -> p b c f", b=2, c=KC)
        w2_sb = cbuf[:, 2 * KC * F1:].rearrange("p (b k l) -> p b k l", b=2, k=2)
        XN8 = cbuf[:].rearrange("p (t l) -> p t l", l=L)
        XT2 = cbuf[:].rearrange("p (b c q) -> p b c q", b=2, c=KC)
        lgT = [t[0:E0].rearrange("p c q -> p (c q)") for t in (XE, hT)]
        mask_u = sb("mask_u", [P, NB, S], U8)
        mmul = qkv[:, 0:NB * S].rearrange("p (n m) -> p n m", n=NB)
        madd = qkv[:, NB * S:].rearrange("p (n m) -> p n m", n=NB)
        vgain = sb("vgain", [P, NB])
        XT4 = big[:, 0:KC * S].rearrange("p (c s) -> p c s", c=KC)
        sc4, attn4, attnT4 = (big[:, KC * S + k * TB * S:KC * S + (k + 1) * TB * S].rearrange("p (j m) -> p j m", j=TB)
                              for k in range(3))
        negmax4 = sb("negmax4", [P, TB])
        sumexp4 = sb("sumexp4", [P, TB])
        rsum4 = sb("rsum4", [P, TB])

        class Log:
            def __init__(self, eng, name):
                self.eng, self.sem, self.n = eng, sem(name), 0

            def __call__(self, ins):
                ins.then_inc(self.sem, 1)
                self.n += 1

            def wait(self):
                self.eng.wait_ge(self.sem, self.n)

        x_in = [sem(f"x_in{i}") for i in range(len(PARTS))]
        w_in = sem("w_in")
        r_in = sem("r_in")
        ctx_in = sem("ctx_in")
        const_ok = sem("const_ok")
        gain_ok = sem("gain_ok")
        vbg_ok = sem("vbg_ok")
        std_ok = [sem(f"std_ok{k}") for k in range(4)]
        rstd_ok = [sem(f"rstd_ok{k}") for k in range(4)]
        xl_ready = sem("xl_ready")
        vb_added = sem("vb_added")
        qk_mm, v_mm, s_mm, t_mm, a_mm = (sem(f"{k}_mm") for k in "qk v s t a".split())
        act1 = sem("act1")
        max_ready = sem("max_ready")
        rsum_ok = sem("rsum_ok")
        attn_ready = sem("attn_ready")
        dve1 = sem("dve1")
        st_ok = [sem(f"st_ok{k}") for k in range(4)]
        mv_ok = [sem(f"mv_ok{k}") for k in range(4)]
        x_st = sem("x_st")
        xn2, tr2, xt2, lgT_mm, lgT_ok, lg_mm, lg_ok = (sem(k) for k in "xn2 tr2 xt2 lgT_mm lgT_ok lg_mm lg_ok".split())
        row0_st = sem("row0_st")
        exp_in, exp_ok = sem("exp_in"), sem("exp_ok")
        hot_ok, hotT, hotT_ok, simr = sem("hot_ok"), sem("hotT"), sem("hotT_ok"), sem("simr")
        comb_ok = sem("comb_ok")
        comb_st = sem("comb_st")
        chosen_ok, cnt_mm, pos_mm = sem("chosen_ok"), sem("cnt_mm"), sem("pos_mm")
        simr_ok = sem("simr_ok")
        hots_ok = [sem(f"hots_ok{m}") for m in range(2)]
        hots_scaled = [sem(f"hots_scaled{m}") for m in range(2)]
        hots_mm = [sem(f"hots_mm{m}") for m in range(2)]
        ended_ok, tab_mm = sem("ended_ok"), sem("tab_mm")
        tab_ok = [sem(f"tab_ok{m}") for m in range(2)]
        lst_ok = sem("lst_ok")
        gathers_begun, adds_begun, pool_done, all_stored = (
            sem(k) for k in "gathers_begun adds_begun pool_done all_stored".split())
        mask_ok, vgain_ok = sem("mask_ok"), sem("vgain_ok")
        c4_in = [sem(f"c4_in{b}") for b in range(2)]
        ct_in = [sem(f"ct_in{b}") for b in range(2)]
        x3_in = [sem(f"x3_in{q}") for q in range(len(PARTS))]
        (xn4, x4_mm, xt4, s4_mm, sc_ok, max4, exp4, t4_mm, at4, rs4_ok, r4_mm, dve4) = (
            sem(k) for k in "xn4 x4_mm xt4 s4_mm sc_ok max4 exp4 t4_mm at4 rs4_ok r4_mm dve4".split())
        s_in, b_in, xn5, sb2_ok, sb2_added, yb_ok = (sem(k) for k in "s_in b_in xn5 sb2_ok sb2_added yb_ok".split())
        row1_st = [sem(f"row1_st{b}") for b in range(2)]
        out_st = [sem(f"out_st{b}") for b in range(2)]

        def expert_sems(m, names):
            return {n: sem(f"{n}{m}") for n in names.split()}

        sparse = "tr_mm xe_ready up_mm hm_ready ht_mm ht_ready down_mm y_ready gath_a gath_b gi_ok si_ok cw_ok scattered "
        sparse += "up_load_a up_load_b down_load_a down_load_b up_weights down_weights "
        M0 = expert_sems("0", sparse + "act_ready")
        M1 = expert_sems("1", sparse + "pre_ok")
        MS = expert_sems("_shared", "up_mm gelu_ok down_mm scaled y_ready")
        block = es.enter_context(nc.Block())

        hot = big[:].rearrange("p (t k e) -> p t k e", t=T, k=TOPK)
        wide = xl_flat[:, 0:T * TOPK * E0].rearrange("p (t k e) -> p t k e", t=T, k=TOPK)
        wide4 = [W[:, b].rearrange("p d (a k e) -> p (d a) k e", k=PRIM, e=E0) for b in range(2)]
        hotT_sb = [a[:].rearrange("p (t q) -> p t q", t=4) for a in (hm, sg)]
        simr_sb = [a[:].rearrange("p (t j e) -> p t j e", t=4, j=4) for a in (*Y, *XN)]

        def pairs_of(eng, m, gmax):
            return eng.value_load(pairs_i[m][0:1, 0:1], min_val=0, max_val=gmax // 2 - 3) + 3

        @block.sync
        def _(sp):
            def context(n):
                return ctx[bass.ds(n, 1), :, :].rearrange("a (j p) l -> p (a j) l", p=P)

            for q, (lo, hi) in enumerate(PARTS):
                sp.dma_start(X[:, lo:hi, :], x_v[:, lo:hi, :]).then_inc(x_in[q], 16)
                if q == 0:
                    sp.dma_start(gain_in[:], gains.to_broadcast([P, 4])).then_inc(w_in, 16)
                    sp.dma_start(W[:], w_qkv).then_inc(w_in, 16)
                    sp.dma_start(WB[:], b_qkv).then_inc(w_in, 16)
                    sp.dma_start(C, context(0)).then_inc(ctx_in, 16)
            sp.dma_start(gate0_sb[:], gate0).then_inc(r_in, 16)
            sp.dma_start(gate1_sb[:], gate1).then_inc(r_in, 16)
            sp.wait_ge(const_ok, 4)
            for j in range(4):
                sp.dma_start(simd[j * E0:(j + 1) * E0, j * E0:(j + 1) * E0], sim).then_inc(r_in, 16)
            sp.dma_start(mask_u[:], mask.rearrange("(a n) m -> a n m", a=1).to_broadcast([P, NB, S])).then_inc(r_in, 16)
            with sp.Fori(0, NB - 1) as i:
                sp.wait_ge(v_mm, at(i, 2, 2))
                sp.dma_start(C, context(i + 1)).then_inc(ctx_in, 16)
                sp.wait_ge(dve1, at(i, 6, 12))
                sp.dma_start(x2_v[:, bass.ds(i * TB, TB), :], X[:, bass.ds(i * TB, TB), :]).then_inc(x_st, 16)
            sp.wait_ge(dve1, 6 * NB + 6)
            sp.dma_start(x2_v[:, T - TB:T, :], X[:, T - TB:T, :]).then_inc(x_st, 16)
            for q in range(4):
                sp.wait_ge(xn2, 4 * q + 4)
                sp.dma_start(rows0_v[:, 4 * q:4 * q + 4, 0:L], XL[:, 4 * q:4 * q + 4, :]).then_inc(row0_st, 16)
            sp.wait_ge(comb_ok, 1)
            sp.dma_start(rows0_v[:, :, L:ROW], comb[:]).then_inc(comb_st, 16)

            def load_weights(M, m, n_experts, load_up, load_down, loaded=False):
                def arrived(b, count):
                    sp.wait_ge((M["up_load_a"], M["up_load_b"])[b], count)
                    sp.sem_inc(M["up_weights"], 1)
                    sp.wait_ge((M["down_load_a"], M["down_load_b"])[b], count)
                    sp.sem_inc(M["down_weights"], 1)

                if not loaded:
                    for b in range(2):
                        load_up(b, b)
                        load_down(b, b)
                for b in range(2):
                    arrived(b, 16)
                with sp.Fori(0, n_experts // 2 - 1) as i:
                    for b in range(2):
                        done = sp.value_load(done_i[m][0:1, bass.ds(i * 2 + b, 1)], min_val=1, max_val=G0 + 1)
                        sp.wait_ge(M["up_mm"], done)
                        load_up(i * 2 + 2 + b, b)
                        sp.wait_ge(M["down_mm"], done)
                        load_down(i * 2 + 2 + b, b)
                        arrived(b, at(i, 16, 32))

            def load_up0(e, b):
                sp.dma_start(wup[:, b:b + 1, :, :], w_up[bass.ds(e, 1), :, :, :].rearrange("e p c f -> p e c f")).then_inc(
                    (M0["up_load_a"], M0["up_load_b"])[b], 16)

            def load_down0(e, b):
                sp.dma_start(wdn[0:FH, b:b + 1, :, :], w_down[bass.ds(e, 1), :, :, :].rearrange("e p k l -> p e k l")).then_inc(
                    (M0["down_load_a"], M0["down_load_b"])[b], 16)

            sp.wait_ge(tab_ok[0], 1)
            load_weights(M0, 0, E0, load_up0, load_down0)

            def load_ct(n, b):
                sp.dma_start(CT[:, b:b + 1, :, :], ctx_t[bass.ds(n, 1), :, :, :].rearrange("a p c m -> p a c m")).then_inc(ct_in[b], 16)

            def load_c4(n, b):
                sp.dma_start(C4[:, b, :, :], context(n)).then_inc(c4_in[b], 16)

            for b in range(2):
                load_ct(b, b)
                load_c4(b, b)
            pairs0 = pairs_of(sp, 0, G0)
            sp.wait_ge(M0["scattered"], pairs0 * 32)
            for q, (lo, hi) in enumerate(PARTS):
                sp.dma_start(X[:, lo:hi, :], x2_v[:, lo:hi, :]).then_inc(x3_in[q], 16)
            sp.dma_start(sw1_sb, sw1).then_inc(s_in, 16)
            sp.dma_start(sw2_sb, sw2).then_inc(s_in, 16)
            sp.dma_start(sb1_c, sb1).then_inc(s_in, 16)
            sp.dma_start(sb2_bc, sb2.to_broadcast([P, L])).then_inc(s_in, 16)
            with sp.Fori(0, NB // 2 - 1) as i:
                for b in range(2):
                    sp.wait_ge(s4_mm, at(i, 4, 2 * b + 2))
                    load_ct(i * 2 + 2 + b, b)
                    sp.wait_ge(r4_mm, at(i, 4, 2 * b + 2))
                    load_c4(i * 2 + 2 + b, b)
            for q in range(4):
                sp.wait_ge(xn5, 4 * q + 4)
                sp.dma_start(rows1_v[:, 4 * q:4 * q + 4, 0:L], XN8[:, q % 2 * 4:q % 2 * 4 + 4, :]).then_inc(row1_st[q % 2], 16)
            sp.dma_start(b2_bc, b2.to_broadcast([P, E1 * L]).rearrange("p (e f) -> p e f", e=E1)).then_inc(b_in, 16)
            sp.wait_ge(comb_ok, 2)
            sp.dma_start(rows1_v[:, :, L:ROW1], comb[:, :, 0:E1]).then_inc(comb_st, 16)

            def store_out(t):
                sp.wait_ge(MS["y_ready"], t + 1)
                sp.dma_start(out_v[:, t:t + 1, :], Y[t % 2][:].rearrange("p (a l) -> p a l", a=1)).then_inc(out_st[t % 2], 16)

            def load_up1(e, b):
                sp.dma_start(w1_sb[:, b:b + 1, :, :], w1[bass.ds(e, 1), :, :, :].rearrange("e p c f -> p e c f")).then_inc(
                    (M1["up_load_a"], M1["up_load_b"])[b], 16)

            def load_down1(e, b):
                sp.dma_start(w2_sb[:, b:b + 1, :, :], w2[bass.ds(e, 1), :, :, :].rearrange("e p k l -> p e k l")).then_inc(
                    (M1["down_load_a"], M1["down_load_b"])[b], 16)

            for t in range(T // 2):
                store_out(t)
            sp.wait_ge(tab_ok[1], 1)
            for b in range(2):
                load_up1(b, b)
                load_down1(b, b)
            for t in range(T // 2, 3 * T // 4):
                store_out(t)
            sp.wait_ge(MS["up_mm"], KC * T // 4)
            sp.dma_start(b1_bc, b1.to_broadcast([P, E1 * F1]).rearrange("p (e f) -> p e f", e=E1)).then_inc(b_in, 16)
            for t in range(3 * T // 4, T):
                store_out(t)
            load_weights(M1, 1, E1, load_up1, load_down1, loaded=True)
            pairs1 = pairs_of(sp, 1, G1)
            sp.wait_ge(row0_st, 16 * 4)
            for s in row1_st:
                sp.wait_ge(s, 32)
            for s in out_st:
                sp.wait_ge(s, 16 * T // 2)
            sp.wait_ge(M1["scattered"], pairs1 * 32)
            sp.sem_inc(all_stored, 1)
            sp.wait_ge(comb_st, 32)
            sp.wait_ge(x_st, 16 * NB)

        @block.gpsimd
        def _(pool):
            pool.memset(ident[:], 0.0).then_inc(const_ok, 1)
            pool.memset(eps_t[:], EPS).then_inc(const_ok, 1)
            pool.memset(ones_b[:], 1.0).then_inc(const_ok, 1)
            pool.memset(simd[:], 0.0).then_inc(const_ok, 1)
            pool.memset(below[:], 1.0).then_inc(const_ok, 1)
            pool.wait_ge(const_ok, 5)
            pool.affine_select(out=ident[:], in_=ident[:], compare_op=ALU.not_equal, fill=1.0, base=0,
                               pattern=[[-1, P]], channel_multiplier=1).then_inc(const_ok, 1)
            pool.affine_select(out=below[:], in_=below[:], compare_op=ALU.is_gt, fill=0.0, base=0,
                               pattern=[[1, P]], channel_multiplier=-1).then_inc(const_ok, 1)
            pool.wait_ge(vbg_ok, 1)
            with pool.Fori(0, NB) as n:
                for j in range(TB):
                    pool.wait_ge(xl_ready, at(n, TB, j + 1))
                    xt = X[:, bass.ds(n * TB + j, 1), :]
                    pool.tensor_tensor(xt, xt, vbg[:, j:j + 1].unsqueeze(1).to_broadcast([P, 1, L]),
                                       ALU.add).then_inc(vb_added, 1)
            ints = dict(allow_small_or_imprecise_dtypes=True)
            pool.iota(iota_e[:], pattern=[[1, E0]], base=0, channel_multiplier=0, **ints).then_inc(const_ok, 1)
            pool.iota(iota_p[:], pattern=[[1, P], [0, TOPK]], base=0, channel_multiplier=0, **ints).then_inc(const_ok, 1)
            pool.iota(iota_g[:], pattern=[[1, G0 + 2], [0, TOPK]], base=0, channel_multiplier=0, **ints).then_inc(const_ok, 1)
            pool.iota(token1[:], pattern=[[P, T]], base=1, channel_multiplier=1, **ints).then_inc(const_ok, 1)
            pool.memset(ones_e[:], 1.0).then_inc(const_ok, 1)
            pool.memset(zero_g[:], 0.0).then_inc(const_ok, 1)
            pool.memset(XG[0][:], 0.0).then_inc(const_ok, 1)
            pool.memset(XG[1][:], 0.0).then_inc(const_ok, 1)
            pool.wait_ge(r_in, 16 * 7)
            pool.affine_select(out=simd[:], in_=simd[:], compare_op=ALU.not_equal, fill=1.0, base=0,
                               pattern=[[-1, P]], channel_multiplier=1).then_inc(const_ok, 1)
            pool.wait_ge(dve1, 6 * NB + 6)
            pool.tensor_copy(mmul, mask_u[:]).then_inc(mask_ok, 1)
            pool.wait_ge(mask_ok, 1)
            pool.tensor_scalar(madd, mmul, 1e30, -1e30, ALU.mult, ALU.add).then_inc(mask_ok, 1)
            pool.wait_ge(vgain_ok, 1)
            pool.tensor_scalar(mmul, mmul, float(L) ** -0.5, None, ALU.mult).then_inc(mask_ok, 1)

            def experts(M, m, width, rows, dest, gmax, before_adds=None):
                pool.wait_ge(lst_ok, m + 1)
                gath = (M["gath_a"], M["gath_b"])

                def gather(g, b, count):
                    pool.tensor_copy(gi[b][:], lst_i[m][:, bass.ds(g, 1)]).then_inc(M["gi_ok"], 1)
                    pool.wait_ge(M["gi_ok"], count)
                    pool.sem_inc(gathers_begun, 1)
                    pool.indirect_dma_start(out=XG[b][:, 0:width], out_offset=None, in_=rows,
                                            in_offset=bass.IndirectOffsetOnAxis(ap=gi[b][:, 0:1], axis=0),
                                            bounds_check=NB * S - 1, oob_is_err=False).then_inc(gath[b], 16)

                gather(0, 0, 1)
                gather(1, 1, 2)
                if before_adds:
                    before_adds()
                pairs = pairs_of(pool, m, gmax)

                def take(g, b, n):
                    pool.wait_ge(M["tr_mm"], n)
                    pool.wait_ge(M["cw_ok"], n)
                    gather(g + 2, b, n + 2)

                def add(g, b, n, added):
                    if added is not None:
                        pool.wait_ge(M["scattered"], added)
                    pool.tensor_copy(si[b][:], lst_i[m][:, bass.ds(g, 1)]).then_inc(M["si_ok"], 1)
                    pool.wait_ge(M["si_ok"], n)
                    pool.wait_ge(M["y_ready"], n + 2)
                    pool.sem_inc(adds_begun, 1)
                    pool.indirect_dma_start(out=dest, out_offset=bass.IndirectOffsetOnAxis(ap=si[b][:, 0:1], axis=0),
                                            in_=Y[b][:], in_offset=None, bounds_check=NB * S - 1,
                                            oob_is_err=False, compute_op=ALU.add).then_inc(M["scattered"], 16)

                take(0, 0, 1)
                take(1, 1, 2)
                take(2, 0, 3)
                add(0, 0, 1, None)
                take(3, 1, 4)
                add(1, 1, 2, 16)
                with pool.Fori(1, pairs - 1) as i:
                    for b in range(2):
                        take(i * 2 + b + 2, b, at(i, 2, b + 3))
                        add(i * 2 + b, b, at(i, 2, b + 1), at(i, 32, 16 * b))
                add(pairs * 2 - 2, 0, pairs * 2 - 1, pairs * 32 - 32)
                add(pairs * 2 - 1, 1, pairs * 2, pairs * 32 - 16)
                for b in range(2):
                    pool.wait_ge(gath[b], at(pairs, 16, 16))
                pool.sem_inc(pool_done, 1)

            pool.wait_ge(row0_st, 16 * 4)
            pool.wait_ge(comb_st, 16)
            pool.wait_ge(x_st, 16 * NB)
            experts(M0, 0, ROW, rows0_d, x2_d, G0)

            pool.wait_ge(sb2_ok, 1)
            with pool.Fori(0, T) as t:
                pool.wait_ge(xn5, at(t, 1, 1))
                pool.tensor_tensor(X[:, bass.ds(t, 1), :], X[:, bass.ds(t, 1), :],
                                   sb2_bc.rearrange("p (a l) -> p a l", a=1), ALU.add).then_inc(sb2_added, 1)

            def shared_out(t):
                pool.wait_ge(MS["scaled"], t + 1)
                pool.tensor_tensor(Y[t % 2][:], Y[t % 2][:], X[:, t, :], ALU.add).then_inc(MS["y_ready"], 1)

            def last_shared():
                for t in range(3 * T // 4, T):
                    shared_out(t)
                for b in range(2):
                    pool.wait_ge(out_st[b], 16 * T // 2)

            pool.wait_ge(sb2_added, T)
            for t in range(3 * T // 4):
                shared_out(t)
            for s in row1_st:
                pool.wait_ge(s, 32)
            pool.wait_ge(comb_st, 32)
            experts(M1, 1, ROW1, rows1_d, out_rows, G1, last_shared)

        @block.scalar
        def _(act):
            def roots(k, lo, hi, count):
                act.wait_ge(mv_ok[k], count)
                act.activation(rstd[k][:, lo:hi, :], mv[k][:, lo:hi, 1:2], ACT.Sqrt,
                               bias=eps_t[:, 0:1]).then_inc(std_ok[k], 1)

            act.wait_ge(const_ok, 2)
            roots(0, *PARTS[0], PARTS[0][1])
            act.wait_ge(w_in, 48)
            act.activation(gain[:], gain_in[:], ACT.Tanh).then_inc(gain_ok, 1)
            act.wait_ge(gain_ok, 1)
            act.activation(vbg[:], WB[:, 2, :], ACT.Copy, scale=gain[:, 0:1]).then_inc(vbg_ok, 1)

            def project(n):
                for j in range(4):
                    act.wait_ge(qk_mm, at(n, 4, j + 1))
                    dst, b = (qT, 0) if j < 2 else (kT, 1)
                    act.activation(dst[:, j % 2, :], bank[j][:], ACT.Identity,
                                   bias=WB[:, b, j % 2:j % 2 + 1]).then_inc(act1, 1)

            def values(n):
                for j in range(2):
                    act.wait_ge(v_mm, at(n, 2, j + 1))
                    act.activation(v[:, 2 * j:2 * j + 2, :], bank[2 + j][:].rearrange("p (a e) -> p a e", a=2),
                                   ACT.Copy).then_inc(act1, 1)

            def exps(n):
                for j in range(QT):
                    act.wait_ge(max_ready, at(n, QT, j + 1))
                    act.activation(attn[:, j, :], bank[4 + j][:], ACT.Exp, bias=negmax[:, j:j + 1],
                                   accum_out=sumexp[:, j:j + 1]).then_inc(act1, 1)

            project(0)
            roots(0, PARTS[0][1], T, T)
            values(0)
            exps(0)
            with act.Fori(0, NB - 1) as i:
                project(i + 1)
                values(i + 1)
                exps(i + 1)

            roots(1, 0, T - TB, T - TB)
            roots(1, T - TB, T, T)

            def evac_logits(m, E, q_dst, after=None):
                def tile(t):
                    q, j = t // 4, t % 4
                    act.wait_ge(tr2, m * T + t + 1)
                    act.activation(q_dst(q)[:, :, j * P:(j + 1) * P], bank[t % 2][:].rearrange("p (c q) -> p c q", c=KC),
                                   ACT.Copy).then_inc(xt2, 1)

                def four_logits(q):
                    act.wait_ge(lgT_mm, m * 4 + q + 1)
                    act.activation(lgT[q % 2][0:E, :], bank[6][0:E, :], ACT.Copy).then_inc(lgT_ok, 1)

                for q in range(4):
                    if m == 0 and q > 1:
                        second_choices(q - 2)
                    for t in range(4 * q, 4 * q + 4):
                        tile(t)
                    if after:
                        four_logits(q)
                        after(q)
                    elif q:
                        four_logits(q - 1)
                    if m == 0 and q > 1:
                        similarities(q - 2)
                if not after:
                    four_logits(3)

            def second_choices(q):
                act.wait_ge(hotT, q + 1)
                act.activation(hotT_sb[q % 2], bank[2][:].rearrange("p (t q) -> p t q", t=4), ACT.Copy).then_inc(hotT_ok, 1)

            def similarities(q):
                act.wait_ge(simr, q + 1)
                act.activation(simr_sb[q], bank[3][:].rearrange("p (t j e) -> p t j e", t=4, j=4),
                               ACT.Copy).then_inc(simr_ok, 1)

            evac_logits(0, E0, lambda q: XT2[:, q % 2])
            second_choices(2)
            similarities(2)
            act.wait_ge(exp_in, 2)
            act.activation(e32[:], e32[:], ACT.Exp).then_inc(exp_ok, 1)
            act.activation(e8[:], e8[:], ACT.Exp).then_inc(exp_ok, 1)
            second_choices(3)
            similarities(3)

            with act.Fori(0, T // 2) as i:
                for b in range(2):
                    act.wait_ge(hots_ok[0], at(i, 4, 2 * b + 1))
                    act.activation(hot_p[b][:], hot_p[b][:], ACT.Copy,
                                   scale=token1[:, bass.ds(i * 2 + b, 1)]).then_inc(hots_scaled[0], 1)

            def take_rows(M, n):
                act.wait_ge(M["tr_mm"], n)
                act.activation(XE[:], bank[0][:].rearrange("p (c q) -> p c q", c=KC), ACT.Copy).then_inc(M["xe_ready"], 1)

            def silu(g1):
                act.wait_ge(M0["up_mm"], g1 + 1)
                act.activation(sg[:, 0:F0], bank[1][:, 0:F0], ACT.Silu).then_inc(M0["act_ready"], 1)

            act.wait_ge(tab_ok[0], 1)
            pairs0 = pairs_of(act, 0, G0)
            take_rows(M0, 1)
            silu(1)
            take_rows(M0, 2)
            with act.Fori(0, pairs0 - 1) as i:
                for b in range(2):
                    silu(at(i, 2, 2 + b))
                    take_rows(M0, at(i, 2, 3 + b))
            silu(at(pairs0, 2, 0))

            roots(2, *PARTS[0], PARTS[0][1])

            def evac4(n):
                for j in range(TB):
                    act.wait_ge(x4_mm, at(n, 2, j + 1))
                    act.activation(XT4[:, :, j * P:(j + 1) * P], bank[j][:].rearrange("p (c q) -> p c q", c=KC),
                                   ACT.Copy).then_inc(xt4, 1)

            def evac_attn4(n):
                act.wait_ge(t4_mm, at(n, 1, 1))
                act.activation(attnT4, bank[2][:].rearrange("p (m s) -> p m s", m=2), ACT.Copy).then_inc(at4, 1)

            def exps4(n):
                for j in range(TB):
                    act.wait_ge(max4, at(n, 2, j + 1))
                    act.activation(attn4[:, j, :], sc4[:, j, :], ACT.Exp, bias=negmax4[:, j:j + 1],
                                   accum_out=sumexp4[:, j:j + 1]).then_inc(exp4, 1)

            evac4(0)
            roots(2, *PARTS[1], PARTS[1][1])
            exps4(0)
            evac4(1)
            evac_attn4(0)
            roots(2, PARTS[1][1], T, T)
            with act.Fori(0, NB - 2) as i:
                evac4(i + 2)
                exps4(i + 1)
                evac_attn4(i + 1)
            exps4(NB - 1)
            evac_attn4(NB - 1)

            roots(3, 0, T - TB, T - TB)
            roots(3, T - TB, T, T)

            def gelu(M, g1, width):
                act.wait_ge(M["pre_ok"], g1)
                act.activation(hm[:, 0:width], sg[:, 0:width], ACT.Gelu).then_inc(M["hm_ready"], 1)

            def hidden(q):
                if q > 1:
                    act.wait_ge(MS["down_mm"], 4 * (q - 1))
                for f in range(KC):
                    act.wait_ge(MS["up_mm"], KC * q + f + 1)
                    act.activation(hT4[q % 2][:, f, :], bank[(2, 5)[f % 2]][:], ACT.Gelu,
                                   bias=sb1_c[:, f:f + 1]).then_inc(MS["gelu_ok"], 1)

            def scaled_out(tiles):
                for t in tiles:
                    act.wait_ge(MS["down_mm"], t + 1)
                    if t > 1:
                        act.wait_ge(out_st[t % 2], 16 * (t // 2))
                    act.activation(Y[t % 2][:], bank[3 + t % 2][:], ACT.Copy, scale=gain[:, 3:4]).then_inc(MS["scaled"], 1)

            evac_logits(1, E1, lambda q: XT5[:, :, 4 * q * P:(4 * q + 4) * P], lambda q: hidden(q) if q < 2 else None)
            act.wait_ge(exp_in, 3)
            act.activation(e8[:, :, 0:1], e8[:, :, 0:1], ACT.Exp).then_inc(exp_ok, 1)
            scaled_out(range(0, 4))
            hidden(2)
            scaled_out(range(4, 8))
            hidden(3)
            scaled_out(range(8, T))

            act.wait_ge(tab_ok[1], 1)
            pairs1 = pairs_of(act, 1, G1)
            take_rows(M1, 1)
            gelu(M1, 1, F1)
            take_rows(M1, 2)
            with act.Fori(0, pairs1 - 1) as i:
                for b in range(2):
                    gelu(M1, at(i, 2, 2 + b), F1)
                    take_rows(M1, at(i, 2, 3 + b))
            gelu(M1, at(pairs1, 2, 0), F1)

        @block.tensor
        def _(pe):
            def project(n, parts=range(4)):
                pe.wait_ge(ctx_in, at(n, 16, 16))
                pe.wait_ge(xl_ready, at(n, 2, 2))
                for j in parts:
                    w, e = j // 2, j % 2
                    for d in range(TB):
                        rhs = XL[:, bass.ds(n * TB + d, 1), :] if w == 0 else C[:, d, :]
                        mm = pe.matmul(bank[j][:], W[:, w, d, e * P:(e + 1) * P], rhs,
                                       start=(d == 0), stop=(d == TB - 1))
                    mm.then_inc(qk_mm, 1)

            def values(n):
                pe.wait_ge(act1, at(n, 10, 4))
                for lt in range(QT):
                    for d in range(TB):
                        mm = pe.matmul(bank[2 + lt // 2][:, (lt % 2) * S:(lt % 2 + 1) * S],
                                       C[:, d, lt * P:(lt + 1) * P], W[:, 2, d, :],
                                       start=(d == 0), stop=(d == TB - 1))
                    if lt % 2:
                        mm.then_inc(v_mm, 1)

            def scores(n, first):
                for j in range(QT):
                    if not first:
                        pe.wait_ge(dve1, at(n - 1, 6, 6 + j + 1))
                    for e in range(TB):
                        mm = pe.matmul(bank[4 + j][:], qT[:, e, j * P:(j + 1) * P], kT[:, e, :],
                                       start=(e == 0), stop=(e == TB - 1))
                    mm.then_inc(s_mm, 1)

            def transposes(n):
                for j in range(QT):
                    pe.wait_ge(attn_ready, at(n, QT, j + 1))
                    for k in range(QT):
                        mm = pe.transpose(bank[4 + j][:, k * P:(k + 1) * P], attn[:, j, k * P:(k + 1) * P],
                                          ident[:])
                    mm.then_inc(t_mm, 1)

            def apply(n):
                pe.wait_ge(dve1, at(n, 6, 6 + 4))
                for d in range(TB):
                    for k in range(QT):
                        mm = pe.matmul(bank[d][:], v[:, k, d * P:(d + 1) * P], attnT[:, k, :],
                                       start=(k == 0), stop=(k == QT - 1))
                    mm.then_inc(a_mm, 1)

            for m in range(2):
                pe.sem_inc(hots_mm[m], 2)
            pe.wait_ge(const_ok, 7)
            pe.wait_ge(w_in, 48)
            project(0)
            values(0)
            scores(0, True)
            with pe.Fori(0, NB - 1) as i:
                pe.wait_ge(dve1, at(i, 6, 6))
                pe.wait_ge(act1, at(i, 10, 6))
                project(i + 1, range(3))
                transposes(i)
                project(i + 1, [3])
                pe.wait_ge(act1, at(i, 10, 10 + 2))
                apply(i)
                values(i + 1)
                scores(i + 1, False)
            transposes(NB - 1)
            pe.wait_ge(dve1, 6 * NB)
            pe.wait_ge(act1, 10 * NB)
            apply(NB - 1)

            def transpose_tile(dst, src, done):
                for c in range(KC):
                    mm = pe.transpose(dst[:, c * P:(c + 1) * P], src[:, c * P:(c + 1) * P], ident[:])
                mm.then_inc(done, 1)

            def tile_logits(m, E, gate, src, src_ok, xt_of, after=None):
                def tr(t):
                    pe.wait_ge(src_ok, t + 1)
                    pe.wait_ge(xt2, m * T + t - 1) if m * T + t > 1 else None
                    for c in range(KC):
                        mm = pe.transpose(bank[t % 2][:, c * P:(c + 1) * P], src(t)[:, c * P:(c + 1) * P], ident[:])
                    mm.then_inc(tr2, 1)

                def logits(q):
                    pe.wait_ge(xt2, m * T + 4 * q + 4)
                    pe.wait_ge(lgT_ok, m * 4 + q) if m * 4 + q else None
                    for c in range(KC):
                        mm = pe.matmul(bank[6][0:E, :], gate[:, c, :], xt_of(q)[:, c, :],
                                       start=(c == 0), stop=(c == KC - 1))
                    mm.then_inc(lgT_mm, 1)

                def back(q):
                    pe.wait_ge(lgT_ok, m * 4 + q + 1)
                    pe.wait_ge(lg_ok, m * 4 + q - 1) if m * 4 + q > 1 else None
                    for j in range(4):
                        mm = pe.transpose(bank[LG_BANKS[m][q % 2]][:, j * E:(j + 1) * E],
                                          lgT[q % 2][0:E, j * P:(j + 1) * P], ident[0:E, 0:E])
                    mm.then_inc(lg_mm, 1)

                for q in range(4):
                    for t in range(4 * q, 4 * q + 4):
                        tr(t)
                    if m == 0 and q > 1:
                        similarities(q - 2)
                    if q:
                        back(q - 1)
                    logits(q)
                    if m == 0 and q:
                        second_choices(q - 1)
                    if after:
                        after(q)
                back(3)

            def second_choices(q):
                pe.wait_ge(hot_ok, q + 1)
                for j in range(4):
                    mm = pe.transpose(bank[2][:, j * P:(j + 1) * P],
                                      hot[:, 4 * q + j, PRIM:TOPK, :].rearrange("p k e -> p (k e)"), ident[:])
                mm.then_inc(hotT, 1)

            def similarities(q):
                pe.wait_ge(hotT_ok, q + 1)
                if q:
                    pe.wait_ge(simr_ok, q)
                for j in range(4):
                    mm = pe.matmul(bank[3][:, j * P:(j + 1) * P], hotT_sb[q % 2][:, j, :], simd[:], start=True, stop=True)
                mm.then_inc(simr, 1)

            pe.wait_ge(r_in, 32)
            pe.wait_ge(const_ok, 16)
            pe.wait_ge(dve1, 6 * NB + 6)
            tile_logits(0, E0, gate0_sb, lambda t: XL[:, t, :], xn2, lambda q: XT2[:, q % 2])
            similarities(2)
            second_choices(3)
            similarities(3)

            def positions(m, E):
                pe.wait_ge(chosen_ok, m + 1)
                ch = chosen[:, :, 0:E]
                for t in range(T):
                    mm = pe.matmul(bank[1][:, 0:E], ones_b[:], ch[:, t, :], start=(t == 0), stop=(t == T - 1))
                mm.then_inc(cnt_mm, 1)
                out_pos = bank[0][:, 0:T * E].rearrange("p (t e) -> p t e", t=T)
                pe.matmul(out_pos, below[:], ch, start=True, stop=False)
                for t in range(T - 1):
                    later = T - 1 - t
                    pe.matmul(out_pos[:, t + 1:T, :], ones_b[:],
                              ch[:, t:t + 1, :].to_broadcast([P, later, E]), start=False, stop=False)
                pe.matmul(out_pos, zero_g[:, 0:P], ch, start=False, stop=True).then_inc(pos_mm, 1)

            def table(m, E, G):
                pe.wait_ge(ended_ok, m + 1)
                pe.matmul(bank[7][0:1, 0:G + 2], ones_b[0:E, 0:1], ended[0:E, 0:G + 2], start=True,
                          stop=True).then_inc(tab_mm, 1)

            def lists(m, K, G):
                dst = bank[2][:, 0:G + 2]
                pe.matmul(dst, iota_p[:, :, 0], zero_g[:, 0:G + 2], start=True, stop=False)
                per = TOPK // K
                with pe.Fori(0, T // per // 2) as i:
                    for b in range(2):
                        pe.wait_ge(hots_ok[m], at(i, 4, 2 * b + 2))
                        pe.wait_ge(hots_scaled[m], at(i, 2 * (per if m else 1), (b + 1) * (per if m else 1)))
                        for k in range(TOPK):
                            mm = pe.matmul(dst, hot_p[b][:, :, k], hot_g[b][:, 0:G + 2, k], start=False, stop=False)
                        mm.then_inc(hots_mm[m], 1)
                pe.matmul(dst, iota_p[:, :, 0], zero_g[:, 0:G + 2], start=False, stop=True).then_inc(hots_mm[m], 1)

            positions(0, E0)
            table(0, E0, G0)
            lists(0, TOPK, G0)

            def down(M, b, n, size, e, wd):
                pe.wait_ge(M["down_weights"], e + 1)
                pe.wait_ge(M["ht_ready"], n)
                pe.wait_ge(M["y_ready"], n)
                for k in range(2):
                    mm = pe.matmul(bank[3 + b][:], hT[0:size, k, :], wd(k), start=(k == 0), stop=(k == 1))
                mm.then_inc(M["down_mm"], 1)

            def hidden_transposes(M, n, size):
                pe.wait_ge(M["hm_ready"], n)
                for k in range(2):
                    mm = pe.transpose(bank[2][0:size, k * P:(k + 1) * P], hm[:, k * size:(k + 1) * size], ident[:])
                mm.then_inc(M["ht_mm"], 1)

            def experts(M, m, wu, wd, width, size, gmax):
                pe.sem_inc(M["up_mm"], 1)
                pe.sem_inc(M["down_mm"], 1)
                pairs = pairs_of(pe, m, gmax)
                gath = (M["gath_a"], M["gath_b"])

                def expert_of(g):
                    return pe.value_load(tab[m][0:1, bass.ds(g, 1)], min_val=0, max_val=31)

                def tr(b, n):
                    pe.wait_ge(gath[b], n)
                    transpose_tile(bank[0], XG[b], M["tr_mm"])

                def place(w, e, k):
                    return w[0:size if w is wd else P, bass.ds((e % 2), 1), k, :]

                def up(g, e):
                    pe.wait_ge(M["up_weights"], e + 1)
                    pe.wait_ge(M["xe_ready"], g + 1)
                    for c in range(KC):
                        mm = pe.matmul(bank[1][:, 0:width], XE[:, c, :], place(wu, e, c), start=(c == 0), stop=(c == KC - 1))
                    mm.then_inc(M["up_mm"], 1)

                tr(0, 16)
                up(0, expert_of(0))
                tr(1, 16)
                e1 = expert_of(1)
                hidden_transposes(M, 1, size)
                up(1, e1)
                with pe.Fori(0, pairs - 1) as i:
                    g = i * 2 + 1
                    e = [expert_of(g + k - 1) for k in range(2)]
                    for b in range(2):
                        tr(b, at(i, 16, 32))
                        down(M, b, g + b, size, e[b], lambda k: place(wd, e[b], k))
                        e.append(expert_of(g + b + 1))
                        hidden_transposes(M, g + b + 1, size)
                        up(g + b + 1, e[b + 2])
                g = pairs * 2 - 1
                e = [expert_of(g + k - 1) for k in range(2)]
                down(M, 0, g, size, e[0], lambda k: place(wd, e[0], k))
                hidden_transposes(M, g + 1, size)
                down(M, 1, g + 1, size, e[1], lambda k: place(wd, e[1], k))
                return pairs

            pe.wait_ge(tab_ok[0], 1)
            pairs = experts(M0, 0, wup, wdn, 2 * F0, FH, G0)

            def tr4(n):
                pe.wait_ge(xn4, at(n, 2, 2))
                for j in range(TB):
                    transpose_tile(bank[j], XN[j], x4_mm)

            def scores4(n, b, cin):
                pe.wait_ge(ct_in[b], cin)
                pe.wait_ge(xt4, at(n, 2, 2))
                for j in range(TB):
                    for c in range(KC):
                        mm = pe.matmul(bank[5 + j][:, 0:S], XT4[:, c, j * P:(j + 1) * P], CT[:, b, c, :],
                                       start=(c == 0), stop=(c == KC - 1))
                    mm.then_inc(s4_mm, 1)

            def attn_transposes4(n):
                pe.wait_ge(exp4, at(n, 2, 2))
                for j in range(TB):
                    for k in range(2):
                        mm = pe.transpose(bank[2][:, k * S + j * P:k * S + (j + 1) * P],
                                          attn4[:, j, k * P:(k + 1) * P], ident[:])
                mm.then_inc(t4_mm, 1)

            def read4(n, b, cin):
                pe.wait_ge(c4_in[b], cin)
                pe.wait_ge(at4, at(n, 1, 1))
                pe.wait_ge(dve4, at(n, 2, 2))
                for j in range(TB):
                    for k in range(2):
                        mm = pe.matmul(bank[3 + j][:], attnT4[:, k, j * P:(j + 1) * P], C4[:, b, k, :],
                                       start=(k == 0), stop=(k == 1))
                    mm.then_inc(r4_mm, 1)

            pe.wait_ge(M0["y_ready"], at(pairs, 2, 2))
            tr4(0)
            scores4(0, 0, 16)
            tr4(1)
            attn_transposes4(0)
            with pe.Fori(0, NB // 2 - 1) as i:
                for b in range(2):
                    scores4(i * 2 + b + 1, 1 - b, at(i, 16, 16 + 16 * b))
                    tr4(i * 2 + b + 2)
                    read4(i * 2 + b, b, at(i, 16, 16))
                    attn_transposes4(i * 2 + b + 1)
            scores4(NB - 1, 1, 8 * NB)
            read4(NB - 2, 0, 8 * NB)
            attn_transposes4(NB - 1)
            read4(NB - 1, 1, 8 * NB)

            pe.wait_ge(dve4, 2 * NB + 2)
            def shared_up(q):
                for f in range(KC):
                    if q or f > 1:
                        pe.wait_ge(MS["gelu_ok"], KC * q + f - 1)
                    for c in range(KC):
                        mm = pe.matmul(bank[(2, 5)[f % 2]][:], sw1_sb[:, c, f * P:(f + 1) * P],
                                       XT5[:, c, 4 * q * P:(4 * q + 4) * P], start=(c == 0), stop=(c == KC - 1))
                    mm.then_inc(MS["up_mm"], 1)

            def shared_down(q):
                pe.wait_ge(MS["gelu_ok"], KC * (q + 1))
                for t in range(4 * q, 4 * q + 4):
                    if t > 1:
                        pe.wait_ge(MS["scaled"], t - 1)
                    for f in range(KC):
                        mm = pe.matmul(bank[3 + t % 2][:], hT4[q % 2][:, f, t % 4 * P:(t % 4 + 1) * P], sw2_sb[:, f, :],
                                       start=(f == 0), stop=(f == KC - 1))
                    mm.then_inc(MS["down_mm"], 1)

            pe.wait_ge(s_in, 64)
            tile_logits(1, E1, gate1_sb, lambda t: XN8[:, t % 8, :], xn5, lambda q: XT5[:, :, 4 * q * P:(4 * q + 4) * P],
                        lambda q: shared_up(q) if q < 2 else None)
            pe.wait_ge(lg_ok, 8)
            shared_down(0)
            positions(1, E1)
            shared_up(2)
            table(1, E1, G1)
            shared_down(1)
            shared_up(3)
            pe.wait_ge(MS["gelu_ok"], T)
            lists(1, K1, G1)
            shared_down(2)
            shared_down(3)
            pe.wait_ge(tab_ok[1], 1)
            pe.wait_ge(MS["scaled"], T)
            experts(M1, 1, w1_sb, w2_sb, F1, P, G1)

        @block.vector
        def _(dve):
            dve.sem_inc(dve1, 6)
            dve.sem_inc(dve4, 2)
            for M in (M0, M1):
                dve.sem_inc(M["y_ready"], 2)

            def tile_stats(k, t):
                dve.bn_stats(stats[:, bass.ds(t, 1), :], X[:, bass.ds(t, 1), :]).then_inc(st_ok[k], 1)

            def moments(k, lo, hi):
                dve.wait_ge(st_ok[k], hi)
                for t in range(lo, hi):
                    dve.bn_aggr(mv[k][:, t, :], stats[:, t, :]).then_inc(mv_ok[k], 1)

            def inverse(k, lo, hi, n):
                dve.wait_ge(std_ok[k], n)
                dve.reciprocal(rstd[k][:, lo:hi, :], rstd[k][:, lo:hi, :]).then_inc(rstd_ok[k], 1)
                dve.wait_ge(rstd_ok[k], n)

            def norm(k, dst, t, done):
                dve.tensor_scalar(dst, X[:, bass.ds(t, 1), :], mv[k][:, bass.ds(t, 1), 0:1], rstd[k][:, bass.ds(t, 1), 0:1],
                                  ALU.subtract, ALU.mult).then_inc(done, 1)

            for n, parts in ((1, range(1)), (2, range(1, len(PARTS)))):
                lo, hi = PARTS[parts[0]][0], PARTS[parts[-1]][1]
                for q in parts:
                    dve.wait_ge(x_in[q], 16)
                    for t in range(*PARTS[q]):
                        tile_stats(0, t)
                moments(0, lo, hi)
                inverse(0, lo, hi, n)
                dve.wait_ge(mv_ok[0], hi)
                for t in range(lo, hi):
                    norm(0, XL[:, t:t + 1, :], t, xl_ready)

            def softmax(n):
                def scale(j):
                    dve.wait_ge(act1, at(n, 10, 7 + j))
                    dve.reciprocal(rsum[:, j:j + 1], sumexp[:, j:j + 1]).then_inc(rsum_ok, 1)
                    dve.wait_ge(rsum_ok, at(n, QT, j + 1))
                    dve.tensor_scalar(attn[:, j, :], attn[:, j, :], rsum[:, j:j + 1], None,
                                      ALU.mult).then_inc(attn_ready, 1)

                for j in range(QT):
                    dve.wait_ge(s_mm, at(n, QT, j + 1))
                    dve.tensor_reduce(negmax[:, j:j + 1], bank[4 + j][:], AX.X, ALU.max,
                                      negate=True).then_inc(max_ready, 1)
                    if j:
                        scale(j - 1)
                scale(QT - 1)

            def attn_out(n):
                for j in range(QT):
                    dve.wait_ge(t_mm, at(n, QT, j + 1))
                    dve.tensor_copy(attnT[:, :, j * P:(j + 1) * P],
                                    bank[4 + j][:].rearrange("p (k q) -> p k q", k=QT)).then_inc(dve1, 1)

            def outputs(n):
                for d in range(TB):
                    dve.wait_ge(a_mm, at(n, 2, d + 1))
                    dve.wait_ge(vb_added, at(n, 2, d + 1))
                    xt = X[:, bass.ds(n * TB + d, 1), :]
                    dve.scalar_tensor_tensor(out=xt, in0=bank[d][:].rearrange("p (a l) -> p a l", a=1),
                                             scalar=gain[:, 0:1], in1=xt, op0=ALU.mult, op1=ALU.add).then_inc(dve1, 1)

            def row_stats(k, n, d, own, count):
                dve.wait_ge(own, count)
                tile_stats(k, n * TB + d)

            softmax(0)
            with dve.Fori(0, NB - 1) as i:
                attn_out(i)
                outputs(i)
                softmax(i + 1)
                for d in range(TB):
                    row_stats(1, i, d, dve1, at(i, 6, 6 + 5 + d))
            attn_out(NB - 1)

            moments(1, 0, T - TB)
            inverse(1, 0, T - TB, 1)
            dve.wait_ge(mv_ok[1], T - TB)
            for t in range(T // 2):
                norm(1, XL[:, t:t + 1, :], t, xn2)
            outputs(NB - 1)
            for d in range(TB):
                row_stats(1, NB - 1, d, dve1, at(NB - 1, 6, 6 + 5 + d))
            moments(1, T - TB, T)
            inverse(1, T - TB, T, 2)
            dve.wait_ge(mv_ok[1], T)
            for t in range(T // 2, T):
                norm(1, XL[:, t:t + 1, :], t, xn2)

            R = Log(dve, "routing_steps")

            def run(ins):
                R(ins)
                R.wait()

            dve.wait_ge(mask_ok, 2)
            dve.tensor_reduce(vgain[:], mmul, AX.X, ALU.max).then_inc(vgain_ok, 1)
            dve.wait_ge(vgain_ok, 1)
            dve.tensor_scalar(vgain[:], vgain[:], gain[:, 1:2], None, ALU.mult).then_inc(vgain_ok, 1)

            def last(ap, n):
                return ap.unsqueeze(len(ap.shape)).to_broadcast(list(ap.shape) + [n])

            def third(ap, n):
                s = list(ap.shape)
                return ap.unsqueeze(2).to_broadcast([s[0], s[1], n, s[2]])

            def best_experts(m, E, K, hots, last_quarter):
                for q in range(4):
                    ts = slice(4 * q, 4 * q + 4)
                    dve.wait_ge(lg_mm, m * 4 + q + 1)
                    dve.tensor_copy(lg[:, ts, 0:E],
                                    bank[LG_BANKS[m][q % 2]][:, 0:4 * E].rearrange("p (t e) -> p t e", t=4)).then_inc(lg_ok, 1)
                    dve.wait_ge(lg_ok, m * 4 + q + 1)
                    for t in range(4 * q, 4 * q + 4):
                        R(dve.max(v8[:, t, :], lg[:, t, 0:E]))
                    R.wait()
                    for t in range(4 * q, 4 * q + 4):
                        R(dve.max_index(i8[:, t, :], v8[:, t, :], lg[:, t, 0:E]))
                    if q == 3:
                        last_quarter()
                    R.wait()
                    run(dve.tensor_copy(i8f[:, ts, :], i8[:, ts, :]))
                    dve.tensor_tensor(hots[:, ts, :, :],
                                      iota_e[:, 0:E].unsqueeze(1).unsqueeze(1).to_broadcast([P, 4, K, E]),
                                      last(i8f[:, ts, 0:K], E), ALU.is_equal).then_inc(hot_ok, 1)
                    if m == 0 and q:
                        similarities(q - 1)
                dve.wait_ge(hot_ok, m * 4 + 4)

            def similarities(q):
                ts = slice(4 * q, 4 * q + 4)
                dve.wait_ge(hot_ok, q + 1)
                dve.wait_ge(simr_ok, q + 1)
                for j in range(4):
                    run(dve.tensor_tensor(wide4[j % 2], third(simr_sb[q][:, :, j, :], PRIM), hot[:, ts, 0:PRIM, :], ALU.mult))
                    R(dve.tensor_reduce(cand[:, ts, j, :], wide4[j % 2], AX.X, ALU.add))

            def differences0():
                top = v8[:, :, 0:1]
                dve.tensor_tensor(e32[:], lg[:], top.to_broadcast([P, T, E0]), ALU.subtract).then_inc(exp_in, 1)
                dve.tensor_tensor(e8[:], v8[:], top.to_broadcast([P, T, TOPK]), ALU.subtract).then_inc(exp_in, 1)

            dve.wait_ge(const_ok, 15)
            best_experts(0, E0, TOPK, hot, differences0)
            dve.wait_ge(exp_ok, 2)
            run(dve.tensor_reduce(t16[:], e32[:], AX.X, ALU.add))
            run(dve.reciprocal(t16[:], t16[:]))
            run(dve.tensor_tensor(e8[:], e8[:], last(t16[:], TOPK), ALU.mult))
            run(dve.tensor_reduce(t16[:], e8[:], AX.X, ALU.add))
            run(dve.tensor_scalar(t16[:], t16[:], 1e-12, None, ALU.max))
            run(dve.reciprocal(t16[:], t16[:]))
            run(dve.tensor_tensor(fw[:], e8[:], last(t16[:], TOPK), ALU.mult))
            run(dve.tensor_scalar(fw[:], fw[:], gain[:, 2:3], None, ALU.mult))
            similarities(3)
            R.wait()
            dve.wait_ge(row0_st, 16 * 4)
            run(dve.tensor_reduce(best[:], cand[:], AX.X, ALU.max))
            run(dve.tensor_tensor(sel[:], cand[:], last(best[:], PRIM), ALU.is_equal))
            run(dve.tensor_scalar(left[:], sel[:, :, :, 0], -1.0, 1.0, ALU.mult, ALU.add))
            for i in range(1, PRIM):
                run(dve.tensor_tensor(sel[:, :, :, i], sel[:, :, :, i], left[:], ALU.mult))
                if i < PRIM - 1:
                    run(dve.tensor_tensor(left[:], left[:], sel[:, :, :, i], ALU.subtract))
            run(dve.tensor_scalar(keep[:], best[:], THRESHOLD, None, ALU.is_lt))
            run(dve.tensor_tensor(keep[:], fw[:, :, PRIM:TOPK], keep[:], ALU.mult))
            run(dve.tensor_tensor(moved[:], fw[:, :, PRIM:TOPK], keep[:], ALU.subtract))
            run(dve.tensor_copy(fw[:, :, PRIM:TOPK], keep[:]))
            run(dve.tensor_tensor(madd4[:], sel[:], last(moved[:], PRIM), ALU.mult))
            run(dve.tensor_reduce(left[:], madd4[:].rearrange("p t j i -> p t i j"), AX.X, ALU.add))
            run(dve.tensor_tensor(fw[:, :, 0:PRIM], fw[:, :, 0:PRIM], left[:], ALU.add))

            def dispatch(m, E, K, G, hots, room):
                f = fw[:, :, 0:K]
                run(dve.tensor_tensor(room, hots, last(f, E), ALU.mult))
                dve.tensor_reduce(comb[:, :, 0:E], room.rearrange("p t k e -> p t e k"), AX.X,
                                  ALU.add).then_inc(comb_ok, 1)
                dve.wait_ge(comb_ok, m + 1)
                dve.tensor_scalar(chosen[:, :, 0:E], comb[:, :, 0:E], 0.0, None, ALU.not_equal).then_inc(chosen_ok, 1)
                run(dve.tensor_scalar(act8[:, :, 0:K], f, 0.0, None, ALU.not_equal))
                dve.wait_ge(cnt_mm, m + 1)
                ci, tl, cum, bs = cnt_i[:, 0:E], tiles[:, 0:E], tiles_cum[:, 0:E], base[:, 0:E]
                run(dve.tensor_scalar(ci, bank[1][:, 0:E], float(P - 1), None, ALU.add))
                run(dve.tensor_scalar(ci, ci, 7, None, ALU.arith_shift_right))
                run(dve.tensor_copy(tl, ci))
                run(dve.tensor_tensor_scan(cum, ones_e[:, 0:E], tl, 0.0, ALU.mult, ALU.add))
                run(dve.tensor_tensor(cum_diag[0:E, 0:E], cum[0:E, :], ident[0:E, 0:E], ALU.mult))
                run(dve.tensor_reduce(cum_col[0:E, :], cum_diag[0:E, 0:E], AX.X, ALU.add))
                dve.tensor_scalar(ended[0:E, 0:G + 2], iota_g[0:E, 0:G + 2, 0], cum_col[0:E, 0:1], None,
                                  ALU.is_ge).then_inc(ended_ok, 1)
                run(dve.tensor_scalar(done_i[m][:, 0:E], cum[0:1, :], 1.0, None, ALU.add))
                run(dve.tensor_scalar(pairs_i[m][:], cum[0:1, E - 1:E], 1.0, None, ALU.add))
                run(dve.tensor_scalar(pairs_i[m][:], pairs_i[m][:], 1, None, ALU.arith_shift_right))
                run(dve.tensor_copy(pairs_f[:], pairs_i[m][:]))
                run(dve.tensor_scalar(pairs_i[m][:], pairs_f[:], -3.0, 0.0, ALU.add, ALU.max))
                run(dve.tensor_tensor(bs, cum, tl, ALU.subtract))
                run(dve.tensor_scalar(bs, bs, float(P), None, ALU.mult))
                g = gp[:, :, 0:E]
                dve.wait_ge(pos_mm, m + 1)
                run(dve.tensor_tensor(g, bank[0][:, 0:T * E].rearrange("p (t e) -> p t e", t=T),
                                      bs.unsqueeze(1).to_broadcast([P, T, E]), ALU.add))
                run(dve.tensor_tensor(room, hots, third(g, K), ALU.mult))
                dve.wait_ge(tab_mm, m + 1)
                dve.tensor_scalar(tab[m][:, 0:G + 2], bank[7][0:1, 0:G + 2], float(E - 1), None,
                                  ALU.min).then_inc(tab_ok[m], 1)
                s, a = slot[:, :, 0:K], act8[:, :, 0:K]
                run(dve.tensor_reduce(s, room, AX.X, ALU.add))
                run(dve.tensor_scalar(s, s, 1.0, None, ALU.add))
                run(dve.tensor_tensor(s, s, a, ALU.mult))
                run(dve.tensor_scalar(slot_i[:, :, 0:K], s, -1.0, None, ALU.add))
                run(dve.tensor_scalar(part_i[:, :, 0:K], slot_i[:, :, 0:K], P - 1, None, ALU.bitwise_and))
                run(dve.tensor_scalar(slot_i[:, :, 0:K], slot_i[:, :, 0:K], 7, None, ALU.arith_shift_right))
                per = TOPK // K
                packed_p, packed_g = (a[:].rearrange("p t k -> p (t k)")[:, 0:T * K].rearrange("p (q j) -> p q j", j=TOPK)
                                      for a in (slot_p, slot_g))
                for packed, ints in ((packed_p, part_i), (packed_g, slot_i)):
                    run(dve.tensor_copy(packed.rearrange("p q (t k) -> p q t k", k=K),
                                        ints[:, :, 0:K].rearrange("p (q t) k -> p q t k", t=per)))
                with dve.Fori(0, T // per // 2) as i:
                    for b in range(2):
                        dve.wait_ge(hots_mm[m], at(i, 2, b + 1))
                        for dst, numbers, slots, n in ((hot_p[b], iota_p, packed_p, P), (hot_g[b], iota_g, packed_g, G + 2)):
                            dve.tensor_tensor(dst[:, 0:n, :], numbers[:, 0:n, :],
                                              slots[:, bass.ds(i * 2 + b, 1), :].to_broadcast([P, n, TOPK]),
                                              ALU.is_equal).then_inc(hots_ok[m], 1)
                        if m == 1:
                            dve.wait_ge(hots_ok[m], at(i, 4, 2 * b + 1))
                            for j in range(per):
                                places = hot_p[b][:, :, j * K:(j + 1) * K]
                                dve.tensor_scalar(places, places, token1[:, bass.ds((i * 2 + b) * per + j, 1)], None,
                                                  ALU.mult).then_inc(hots_scaled[m], 1)
                dve.wait_ge(hots_mm[m], T // per + 3)
                run(dve.tensor_copy(lst[:, 0:G + 2], bank[2][:, 0:G + 2]))
                run(dve.tensor_scalar(lst2[:, 0:G + 2], lst[:, 0:G + 2], 0.0, float(NONE), ALU.is_equal, ALU.mult))
                dve.scalar_tensor_tensor(out=lst_i[m][:, 0:G + 2], in0=lst[:, 0:G + 2], scalar=-1.0, in1=lst2[:, 0:G + 2],
                                         op0=ALU.add, op1=ALU.add).then_inc(lst_ok, 1)

            dispatch(0, E0, TOPK, G0, hot, wide)

            def hidden_out(M, n, chunks, size):
                dve.wait_ge(M["ht_mm"], n)
                dve.tensor_copy(hT[0:size, 0:chunks, :],
                                bank[2][0:size, 0:chunks * P].rearrange("p (k q) -> p k q", k=chunks)).then_inc(M["ht_ready"], 1)

            def experts(M, m, gmax, size, middle, weighted, n_e, needs_expert):
                pairs = pairs_of(dve, m, gmax)
                gath = (M["gath_a"], M["gath_b"])

                def expert_of(g):
                    return dve.value_load(tab[m][0:1, bass.ds(g, 1)], min_val=0, max_val=n_e - 1)

                def y(g, b, e, early):
                    dve.wait_ge(M["down_mm"], g + 2)
                    dve.wait_ge(M["cw_ok"], g + 1)
                    if not early:
                        dve.wait_ge(M["scattered"], g * 16 - 16)
                    weighted(g, b, e)

                def weights(g, b, e, gcount):
                    dve.wait_ge(gath[b], gcount)
                    dve.tensor_copy(cw[:, bass.ds(g % 4, 1)], XG[b][:, bass.ds(e + L, 1)]).then_inc(M["cw_ok"], 1)

                def tile(g, b, e, ahead, early=False, first=False):
                    middle(g, e[1])
                    if ahead is not None:
                        e.append(expert_of(g + 1))
                        weights(g + 1, 1 - b, e[2], ahead)
                    hidden_out(M, g + 1, 2, size)
                    if not first:
                        y(g - 1, 1 - b, expert_of(g - 1) if needs_expert and e[0] is None else e[0], early)
                    return e[1:]

                e = [None, expert_of(0)]
                weights(0, 0, e[1], 16)
                e = tile(0, 0, e, 16, True, True)
                e = tile(1, 1, e, 32, True)
                tile(2, 0, e, 32, True)
                with dve.Fori(1, pairs - 1) as i:
                    e = [None, expert_of(i * 2 + 1) if needs_expert else None]
                    e = tile(i * 2 + 1, 1, e, at(i, 16, 32))
                    tile(i * 2 + 2, 0, e, at(i, 16, 32))
                g = pairs * 2 - 1
                e = [None, expert_of(g)]
                tile(g, 1, e, None)
                y(g, 1, e[1], False)

            def middle0(g, e):
                dve.wait_ge(M0["act_ready"], g + 1)
                dve.tensor_tensor(hm[:, 0:F0], bank[1][:, F0:2 * F0], sg[:, 0:F0], ALU.mult).then_inc(M0["hm_ready"], 1)

            def weighted0(g, b, ed):
                dve.tensor_scalar(Y[b][:], bank[3 + b][:], cw[:, bass.ds(g % 4, 1)], None, ALU.mult).then_inc(M0["y_ready"], 1)

            dve.wait_ge(lst_ok, 1)
            experts(M0, 0, G0, FH, middle0, weighted0, E0, False)

            def stats3(parts):
                for q in parts:
                    dve.wait_ge(x3_in[q], 16)
                    for t in range(*PARTS[q]):
                        tile_stats(2, t)
                moments(2, PARTS[parts[0]][0], PARTS[q][1])

            stats3([0])
            inverse(2, *PARTS[0], 1)
            dve.wait_ge(mv_ok[2], PARTS[0][1])
            dve.wait_ge(vgain_ok, 2)
            dve.wait_ge(mask_ok, 3)

            def norm4(n):
                for j in range(TB):
                    norm(2, XN[j][:].rearrange("p (a l) -> p a l", a=1), n * TB + j, xn4)

            def softmax4(n):
                for j in range(TB):
                    dve.wait_ge(s4_mm, at(n, 2, j + 1))
                    dve.tensor_tensor(sc4[:, j:j + 1, :], bank[5 + j][:, 0:S].rearrange("p (a m) -> p a m", a=1),
                                      mmul[:, bass.ds(n, 1), :], ALU.mult).then_inc(sc_ok, 1)
                    dve.wait_ge(sc_ok, at(n, 4, 2 * j + 1))
                    dve.tensor_tensor(sc4[:, j:j + 1, :], sc4[:, j:j + 1, :], madd[:, bass.ds(n, 1), :],
                                      ALU.add).then_inc(sc_ok, 1)
                    dve.wait_ge(sc_ok, at(n, 4, 2 * j + 2))
                    dve.tensor_reduce(negmax4[:, j:j + 1], sc4[:, j, :], AX.X, ALU.max, negate=True).then_inc(max4, 1)

            def inverse_sums4(n):
                dve.wait_ge(exp4, at(n, 2, 2))
                dve.reciprocal(rsum4[:], sumexp4[:]).then_inc(rs4_ok, 1)
                dve.wait_ge(rs4_ok, at(n, 2, 1))
                dve.tensor_scalar(rsum4[:], rsum4[:], vgain[:, bass.ds(n, 1)], None, ALU.mult).then_inc(rs4_ok, 1)

            def read_out4(n):
                dve.wait_ge(rs4_ok, at(n, 2, 2))
                for j in range(TB):
                    dve.wait_ge(r4_mm, at(n, 2, j + 1))
                    xt = X[:, bass.ds(n * TB + j, 1), :]
                    dve.scalar_tensor_tensor(out=xt, in0=bank[3 + j][:].rearrange("p (a l) -> p a l", a=1),
                                             scalar=rsum4[:, j:j + 1], in1=xt, op0=ALU.mult, op1=ALU.add).then_inc(dve4, 1)

            def stats4(n):
                for j in range(TB):
                    row_stats(3, n, j, dve4, at(n, 2, 2 + j + 1))

            norm4(0)
            stats3([1])
            softmax4(0)
            inverse(2, *PARTS[1], 2)
            dve.wait_ge(mv_ok[2], PARTS[1][1])
            dve.wait_ge(x4_mm, 2)
            norm4(1)
            stats3([2, 3])
            inverse(2, PARTS[1][1], T, 3)
            dve.wait_ge(mv_ok[2], T)
            with dve.Fori(0, NB - 2) as i:
                inverse_sums4(i)
                dve.wait_ge(x4_mm, at(i, 2, 4))
                norm4(i + 2)
                softmax4(i + 1)
                read_out4(i)
                stats4(i)
            inverse_sums4(NB - 2)
            softmax4(NB - 1)
            read_out4(NB - 2)
            stats4(NB - 2)
            inverse_sums4(NB - 1)
            moments(3, 0, T - TB)
            inverse(3, 0, T - TB, 1)
            dve.wait_ge(mv_ok[3], T - TB)
            read_out4(NB - 1)

            dve.wait_ge(x4_mm, 2 * NB)
            for t in range(T):
                if t == 2:
                    stats4(NB - 1)
                    moments(3, T - TB, T)
                    inverse(3, T - TB, T, 2)
                    dve.wait_ge(mv_ok[3], T)
                if t > 7:
                    dve.wait_ge(tr2, T + t - 7)
                    dve.wait_ge(row1_st[t // 4 % 2], 16)
                norm(3, XN8[:, t % 8:t % 8 + 1, :], t, xn5)
                if t == 7:
                    dve.wait_ge(s_in, 64)
                    dve.tensor_scalar(sb2_bc, sb2_bc, gain[:, 3:4], None, ALU.mult).then_inc(sb2_ok, 1)

            def differences1():
                dve.tensor_tensor(e8[:, :, 0:1], v8[:, :, 1:2], v8[:, :, 0:1], ALU.subtract).then_inc(exp_in, 1)

            n = T * K1 * E1
            hot1, room1 = (XG[b][:, 0:n].rearrange("p (t k e) -> p t k e", t=T, k=K1) for b in range(2))
            best_experts(1, E1, K1, hot1, differences1)
            dve.wait_ge(exp_ok, 3)
            run(dve.tensor_scalar(fw[:, :, 0:1], e8[:, :, 0:1], 1.0, None, ALU.add))
            run(dve.reciprocal(fw[:, :, 0:1], fw[:, :, 0:1]))
            run(dve.tensor_tensor(fw[:, :, 1:2], fw[:, :, 0:1], e8[:, :, 0:1], ALU.mult))
            run(dve.tensor_scalar(fw[:, :, 0:2], fw[:, :, 0:2], gain[:, 3:4], None, ALU.mult))
            dispatch(1, E1, K1, G1, hot1, room1)

            def middle1(g, e):
                dve.wait_ge(M1["up_mm"], g + 2)
                dve.tensor_tensor(sg[:, 0:F1].rearrange("p (a f) -> p a f", a=1),
                                  bank[1][:, 0:F1].rearrange("p (a f) -> p a f", a=1),
                                  b1_bc[:, bass.ds(e, 1), :], ALU.add).then_inc(M1["pre_ok"], 1)

            def weighted1(g, b, ed):
                a1 = "p (a l) -> p a l"
                dve.tensor_tensor(Y[b][:].rearrange(a1, a=1), bank[3 + b][:].rearrange(a1, a=1),
                                  b2_bc[:, bass.ds(ed, 1), :], ALU.add).then_inc(yb_ok, 1)
                dve.wait_ge(yb_ok, g + 1)
                dve.tensor_scalar(Y[b][:], Y[b][:], cw[:, bass.ds(g % 4, 1)], None, ALU.mult).then_inc(M1["y_ready"], 1)

            dve.wait_ge(b_in, 32)
            dve.wait_ge(lst_ok, 2)
            for b in range(2):
                dve.wait_ge(out_st[b], 16 * T // 2)
            experts(M1, 1, G1, P, middle1, weighted1, E1, True)


def kernel(**inputs):
    import numpy as _np
    import concourse.bacc as _bacc
    from concourse import mybir as _mybir
    from concourse.bass_utils import run_bass_kernel_spmd as _run

    def chunks(a, n):
        return a.reshape(n, a.shape[0] // n, a.shape[1]).transpose(1, 0, 2)

    a = {k: _np.asarray(v) for k, v in inputs.items()}
    arrays = dict(
        x=a["x"], ctx=a["ctx_2048"],
        ctx_t=a["ctx_2048"].transpose(0, 2, 1).reshape(NB, KC, P, S).transpose(0, 2, 1, 3),
        mask=a["mask_BxS2_bk0"],
        gains=_np.concatenate([a["g_xattn"], a["g_ffn"]]).reshape(1, 4),
        w_qkv=_np.stack([chunks(a["L0_xattn_" + k + "W"].T, TB) for k in "QKV"], axis=1),
        b_qkv=_np.stack([a["L0_xattn_" + k + "b"].reshape(TB, P).T for k in "QKV"], axis=1),
        gate0=chunks(a["L0_ffn_gate_weight"].T, KC), sim=a["L0_ffn_similarity"],
        w_up=a["L0_ffn_gate_up_proj"].transpose(0, 2, 1).reshape(E0, KC, P, 2 * F0).transpose(0, 2, 1, 3),
        w_down=a["L0_ffn_down_proj"].transpose(0, 2, 1).reshape(E0, 2, FH, L).transpose(0, 2, 1, 3),
        gate1=chunks(a["L1_ffn_gate_w"], KC),
        w1=a["L1_ffn_w1"].reshape(E1, KC, P, F1).transpose(0, 2, 1, 3), b1=a["L1_ffn_b1"].reshape(1, E1 * F1),
        w2=a["L1_ffn_w2"].reshape(E1, 2, P, L).transpose(0, 2, 1, 3), b2=a["L1_ffn_b2"].reshape(1, E1 * L),
        sw1=chunks(a["L1_ffn_shared_w1"], KC), sb1=a["L1_ffn_shared_b1"].reshape(KC, P).T,
        sw2=chunks(a["L1_ffn_shared_w2"], KC), sb2=a["L1_ffn_shared_b2"].reshape(1, L),
    )
    arrays = {k: _np.ascontiguousarray(v) for k, v in arrays.items()}
    nc = _bacc.Bacc("TRN2", target_bir_lowering=False, num_devices=1)
    aps = {k: nc.dram_tensor(k, v.shape, _mybir.dt.from_np(v.dtype), kind="ExternalInput").ap() for k, v in arrays.items()}
    aps["out"] = nc.dram_tensor("out", (NB, S, L), F32, kind="ExternalOutput").ap()
    flamingo_kernel(nc, **aps)
    r = _run(nc, [arrays], core_ids=[0])
    return r.results[0]["out"]
```

```python
import concourse.bass as bass
from concourse import mybir
from concourse.alu_op_type import AluOpType as ALU
from contextlib import ExitStack

F32 = mybir.dt.float32
F16 = mybir.dt.float16
BF16 = mybir.dt.bfloat16
I32 = mybir.dt.int32
U32 = mybir.dt.uint32
U8 = mybir.dt.uint8
ACT = mybir.ActivationFunctionType
AX = mybir.AxisListType

P = 128
NB, S, L = 8, 256, 512
T = NB * S // P
TB = S // P
KC = L // P
EPS = 1e-5

QT = L // P
E0, TOPK, PRIM, F0 = 32, 8, 4, 192
FH = F0 // 2
THRESHOLD = 0.5
ROW = L + E0
G0 = NB * S * TOPK // P + E0
E1, K1, F1 = 8, 2, 256
ROW1 = L + E1
G1 = NB * S * K1 // P + E1
PARTS = ((0, 2), (2, 6), (6, 10), (10, T))
LG_BANKS = ((7, 5), (7, 3))
LIST_BANKS = (2, 6)
NONE = 4096


def at(i, per, k):
    return i * per + k


def flamingo_kernel(nc, x, ctx, ctx_t, mask, gains, w_qkv, b_qkv, gate0, sim, w_up, w_down,
                    gate1, w1, b1, w2, b2, sw1, sb1, sw2, sb2, out):
    es = ExitStack()
    with es:
        def sb(name, shape, dt=F32):
            return es.enter_context(nc.sbuf_tensor(name, shape, dt))

        def sem(name):
            return es.enter_context(nc.semaphore(name))

        x_v = x.rearrange("n (j p) l -> p (n j) l", p=P)
        out_v = out.rearrange("n (j p) l -> p (n j) l", p=P)

        def dram(name, shape):
            return nc.dram_tensor(name, shape, F32, kind="Internal").ap()

        rows0_d = dram("rows0_d", [NB * S, ROW])
        rows1_d = dram("rows1_d", [NB * S, ROW1])
        x2_d = dram("x2_d", [NB * S, L])
        rows0_v = rows0_d.rearrange("(t p) l -> p t l", p=P)
        rows1_v = rows1_d.rearrange("(t p) l -> p t l", p=P)
        x2_v = x2_d.rearrange("(t p) l -> p t l", p=P)
        out_rows = out.rearrange("n s l -> (n s) l")

        bank = [es.enter_context(nc.psum_tensor(f"bank{i}", [P, 512], F32)) for i in range(8)]
        X = sb("X", [P, T, L])
        XL = sb("XL", [P, T, L])
        xl_flat = XL[:].rearrange("p t l -> p (t l)")
        big = sb("big", [P, 2 * QT * L])
        ident = sb("ident", [P, P])
        eps_t = sb("eps_t", [P, 1])
        gain_in = sb("gain_in", [P, 4])
        gain = sb("gain", [P, 4])
        stats = sb("stats", [P, T, 6])
        mv = [sb(f"mv{k}", [P, T, 2]) for k in range(4)]
        rstd = [sb(f"rstd{k}", [P, T, 1]) for k in range(4)]
        W = sb("W", [P, 3, TB, S])
        WB = sb("WB", [P, 3, TB])
        vbg = sb("vbg", [P, TB])
        qkv = sb("qkv", [P, 4 * TB * L])
        qT, kT, C = (qkv[:, k * TB * L:(k + 1) * TB * L].rearrange("p (j l) -> p j l", j=TB) for k in (0, 1, 3))
        v = qkv[:, 2 * TB * L:3 * TB * L].rearrange("p (j e) -> p j e", j=QT)
        attn = big[:, 0:QT * L].rearrange("p (j l) -> p j l", j=QT)
        attnT = big[:, QT * L:].rearrange("p (j l) -> p j l", j=QT)
        negmax = sb("negmax", [P, QT])
        sumexp = sb("sumexp", [P, QT])
        rsum = sb("rsum", [P, QT])
        XN = [sb(f"XN{b}", [P, L]) for b in range(2)]
        gate0_sb = sb("gate0_sb", [P, KC, E0])
        gate1_sb = sb("gate1_sb", [P, KC, E1])
        simd = sb("simd", [P, P])
        below = sb("below", [P, P], BF16)
        ones_b = sb("ones_b", [P, P], BF16)
        iota_e = sb("iota_e", [P, E0])
        iota_p = sb("iota_p", [P, P, TOPK], F16)
        iota_g = sb("iota_g", [P, G0 + 2, TOPK], F16)
        ones_e = sb("ones_e", [P, E0])
        token1 = sb("token1", [P, T])
        lg = sb("lg", [P, T, E0])
        e32 = sb("e32", [P, T, E0])
        v8 = sb("v8", [P, T, TOPK])
        i8 = sb("i8", [P, T, TOPK], U32)
        i8f = sb("i8f", [P, T, TOPK])
        e8 = sb("e8", [P, T, TOPK])
        t16 = sb("t16", [P, T])
        fw = sb("fw", [P, T, TOPK])
        act8 = sb("act8", [P, T, TOPK])
        cand = sb("cand", [P, T, 4, PRIM])
        best = sb("best", [P, T, 4])
        sel = sb("sel", [P, T, 4, PRIM])
        left = sb("left", [P, T, 4])
        keep = sb("keep", [P, T, 4])
        moved = sb("moved", [P, T, 4])
        madd4 = sb("madd4", [P, T, 4, PRIM])
        comb = sb("comb", [P, T, E0])
        chosen = sb("chosen", [P, T, E0], BF16)
        cnt_i = sb("cnt_i", [P, E0], I32)
        tiles = sb("tiles", [P, E0])
        tiles_cum = sb("tiles_cum", [P, E0])
        base = sb("base", [P, E0])
        gp = sb("gp", [P, T, E0])
        slot = sb("slot", [P, T, TOPK])
        slot_i = sb("slot_i", [P, T, TOPK], I32)
        part_i = sb("part_i", [P, T, TOPK], I32)
        slot_p = sb("slot_p", [P, T, TOPK], F16)
        slot_g = sb("slot_g", [P, T, TOPK], F16)
        hot_p = [sb(f"hot_p{b}", [P, P, TOPK], F16) for b in range(2)]
        hot_g = [sb(f"hot_g{b}", [P, G0 + 2, TOPK], F16) for b in range(2)]
        cum_col = sb("cum_col", [E0, 1])
        cum_diag = sb("cum_diag", [E0, E0])
        ended = sb("ended", [E0, G0 + 2], BF16)
        lst = sb("lst", [P, G0 + 2])
        lst_i = [sb(f"lst_i{k}", [P, G0 + 2], I32) for k in range(2)]
        lst2 = sb("lst2", [P, G0 + 2])
        zero_g = sb("zero_g", [P, G0 + 2], F16)
        tab = [sb(f"tab{k}", [1, G0 + 2], I32) for k in range(2)]
        done_i = [sb(f"done_i{k}", [1, E0], I32) for k in range(2)]
        pairs_f = sb("pairs_f", [1, 1])
        pairs_i = [sb(f"pairs_i{k}", [1, 1], I32) for k in range(2)]
        XG = [sb(f"XG{b}", [P, ROW]) for b in range(2)]
        gi = [sb(f"gi{b}", [P, 1], I32) for b in range(2)]
        si = [sb(f"si{b}", [P, 1], I32) for b in range(2)]
        XE = sb("XE", [P, KC, P])
        wbuf = sb("wbuf", [P, 2 * KC * 2 * F0 + 2 * 2 * L])
        wup = wbuf[:, 0:2 * KC * 2 * F0].rearrange("p (b c f) -> p b c f", b=2, c=KC)
        wdn = wbuf[:, 2 * KC * 2 * F0:].rearrange("p (b k l) -> p b k l", b=2, k=2)
        sw1_sb = wbuf[:, 0:KC * L].rearrange("p (c f) -> p c f", c=KC)
        sw2_sb = wbuf[:, KC * L:2 * KC * L].rearrange("p (c f) -> p c f", c=KC)
        sb1_c = wbuf[:, 2 * KC * L:2 * KC * L + KC]
        sb2_bc = wbuf[:, 2 * KC * L + L:2 * KC * L + 2 * L]
        b1_bc = wbuf[:, 0:E1 * F1].rearrange("p (e f) -> p e f", e=E1)
        b2_bc = qkv[:].rearrange("p (e f) -> p e f", e=E1)
        XT5 = xl_flat.rearrange("p (c q) -> p c q", c=KC)
        hT4 = [big[:, b * KC * L:(b + 1) * KC * L].rearrange("p (c q) -> p c q", c=KC) for b in range(2)]
        sg = sb("sg", [P, 512])
        hm = sb("hm", [P, 512])
        hT = sb("hT", [P, KC, P])
        Y = [sb(f"Y{b}", [P, L]) for b in range(2)]
        cw = sb("cw", [P, 4])
        cbuf = sb("cbuf", [P, 2 * TB * L + 2 * KC * S])
        C4 = cbuf[:, 0:2 * TB * L].rearrange("p (b j l) -> p b j l", b=2, j=TB)
        CT = cbuf[:, 2 * TB * L:].rearrange("p (b c m) -> p b c m", b=2, c=KC)
        w1_sb = cbuf[:, 0:2 * KC * F1].rearrange("p (b c f) -> p b c f", b=2, c=KC)
        w2_sb = cbuf[:, 2 * KC * F1:].rearrange("p (b k l) -> p b k l", b=2, k=2)
        XN8 = cbuf[:].rearrange("p (t l) -> p t l", l=L)
        XT2 = cbuf[:].rearrange("p (b c q) -> p b c q", b=2, c=KC)
        lgT = [t[0:E0].rearrange("p c q -> p (c q)") for t in (XE, hT)]
        mask_u = sb("mask_u", [P, NB, S], U8)
        mmul = qkv[:, 0:NB * S].rearrange("p (n m) -> p n m", n=NB)
        madd = qkv[:, NB * S:].rearrange("p (n m) -> p n m", n=NB)
        vgain = sb("vgain", [P, NB])
        XT4 = big[:, 0:KC * S].rearrange("p (c s) -> p c s", c=KC)
        sc4, attn4, attnT4 = (big[:, KC * S + k * TB * S:KC * S + (k + 1) * TB * S].rearrange("p (j m) -> p j m", j=TB)
                              for k in range(3))
        negmax4 = sb("negmax4", [P, TB])
        sumexp4 = sb("sumexp4", [P, TB])
        rsum4 = sb("rsum4", [P, TB])

        class Log:
            def __init__(self, eng, name):
                self.eng, self.sem, self.n = eng, sem(name), 0

            def __call__(self, ins):
                ins.then_inc(self.sem, 1)
                self.n += 1

            def wait(self):
                self.eng.wait_ge(self.sem, self.n)

        x_in = [sem(f"x_in{i}") for i in range(len(PARTS))]
        w_in = sem("w_in")
        routing_in = sem("routing_in")
        ctx_in = sem("ctx_in")
        const_ok = sem("const_ok")
        gain_ok = sem("gain_ok")
        vbias_ok = sem("vbias_ok")
        std_ok = [sem(f"std_ok{k}") for k in range(4)]
        rstd_ok = [sem(f"rstd_ok{k}") for k in range(4)]
        xl_ready = sem("xl_ready")
        vb_added = sem("vb_added")
        qk_mm, values_mm, scores_mm, attnT_mm, out_mm = (
            sem(k) for k in "qk_mm values_mm scores_mm attnT_mm out_mm".split())
        act_attn1 = sem("act_attn1")
        max_ready = sem("max_ready")
        rsum_ok = sem("rsum_ok")
        attn_ready = sem("attn_ready")
        dve_attn1 = sem("dve_attn1")
        st_ok = [sem(f"st_ok{k}") for k in range(4)]
        mv_ok = [sem(f"mv_ok{k}") for k in range(4)]
        x_stored = sem("x_stored")
        normed1_ok, xnT_mm, xnT_ok, logitsT_mm, logitsT_ok, logits_mm, logits_ok = (sem(k) for k in "normed1_ok xnT_mm xnT_ok logitsT_mm logitsT_ok logits_mm logits_ok".split())
        rows0_stored = sem("rows0_stored")
        exp_in, exp_ok = sem("exp_in"), sem("exp_ok")
        hot_ok, choicesT_mm, choicesT_ok, similar_mm = sem("hot_ok"), sem("choicesT_mm"), sem("choicesT_ok"), sem("similar_mm")
        comb_ok = sem("comb_ok")
        comb_stored = sem("comb_stored")
        chosen_ok, counts_mm, positions_mm = sem("chosen_ok"), sem("counts_mm"), sem("positions_mm")
        similar_ok = sem("similar_ok")
        hots_ok = [sem(f"hots_ok{m}") for m in range(2)]
        hots_scaled = [sem(f"hots_scaled{m}") for m in range(2)]
        hots_mm = [sem(f"hots_mm{m}") for m in range(2)]
        ended_ok, table_mm = sem("ended_ok"), sem("table_mm")
        table_ok = [sem(f"table_ok{m}") for m in range(2)]
        lists_ok = sem("lists_ok")
        gathers_begun, adds_begun, pool_done, all_stored = (
            sem(k) for k in "gathers_begun adds_begun pool_done all_stored".split())
        mask_ok, vgain_ok = sem("mask_ok"), sem("vgain_ok")
        c4_in = [sem(f"c4_in{b}") for b in range(2)]
        ct_in = [sem(f"ct_in{b}") for b in range(2)]
        x3_in = [sem(f"x3_in{q}") for q in range(len(PARTS))]
        (normed2_ok, xnT4_mm, xnT4_ok, scores4_mm, masked4_ok, max4_ok, exp4_ok, attnT4_mm, attnT4_ok, rsum4_ok, readout4_mm, dve4) = (
            sem(k) for k in "normed2_ok xnT4_mm xnT4_ok scores4_mm masked4_ok max4_ok exp4_ok attnT4_mm attnT4_ok rsum4_ok readout4_mm dve4".split())
        shared_in, biases_in, normed3_ok, sb2_ok, sb2_added, yb_ok = (sem(k) for k in "shared_in biases_in normed3_ok sb2_ok sb2_added yb_ok".split())
        rows1_stored = [sem(f"rows1_stored{b}") for b in range(2)]
        out_stored = [sem(f"out_stored{b}") for b in range(2)]

        def expert_sems(m, names):
            return {n: sem(f"{n}{m}") for n in names.split()}

        sparse = "tr_mm xe_ready up_mm hm_ready ht_mm ht_ready down_mm y_ready gath_a gath_b gi_ok si_ok cw_ok scattered "
        sparse += "up_load_a up_load_b down_load_a down_load_b up_weights down_weights "
        M0 = expert_sems("0", sparse + "act_ready")
        M1 = expert_sems("1", sparse + "pre_ok")
        MS = expert_sems("_shared", "up_mm gelu_ok down_mm scaled y_ready")
        block = es.enter_context(nc.Block())

        hot = big[:].rearrange("p (t k e) -> p t k e", t=T, k=TOPK)
        wide = xl_flat[:, 0:T * TOPK * E0].rearrange("p (t k e) -> p t k e", t=T, k=TOPK)
        wide4 = [W[:, b].rearrange("p d (a k e) -> p (d a) k e", k=PRIM, e=E0) for b in range(2)]
        hotT_sb = [a[:].rearrange("p (t q) -> p t q", t=4) for a in (hm, sg)]
        simr_sb = [a[:].rearrange("p (t j e) -> p t j e", t=4, j=4) for a in (*Y, *XN)]

        def pairs_of(eng, m, gmax):
            return eng.value_load(pairs_i[m][0:1, 0:1], min_val=0, max_val=gmax // 2 - 3) + 3

        @block.sync
        def _(sp):
            def context(n):
                return ctx[bass.ds(n, 1), :, :].rearrange("a (j p) l -> p (a j) l", p=P)

            for q, (lo, hi) in enumerate(PARTS):
                sp.dma_start(X[:, lo:hi, :], x_v[:, lo:hi, :]).then_inc(x_in[q], 16)
                if q == 0:
                    sp.dma_start(gain_in[:], gains.to_broadcast([P, 4])).then_inc(w_in, 16)
                    sp.dma_start(W[:], w_qkv).then_inc(w_in, 16)
                    sp.dma_start(WB[:], b_qkv).then_inc(w_in, 16)
                    sp.dma_start(C, context(0)).then_inc(ctx_in, 16)
            sp.dma_start(gate0_sb[:], gate0).then_inc(routing_in, 16)
            sp.dma_start(gate1_sb[:], gate1).then_inc(routing_in, 16)
            sp.wait_ge(const_ok, 4)
            for j in range(4):
                sp.dma_start(simd[j * E0:(j + 1) * E0, j * E0:(j + 1) * E0], sim).then_inc(routing_in, 16)
            sp.dma_start(mask_u[:], mask.rearrange("(a n) m -> a n m", a=1).to_broadcast([P, NB, S])).then_inc(routing_in, 16)
            with sp.Fori(0, NB - 1) as i:
                sp.wait_ge(values_mm, at(i, 2, 2))
                sp.dma_start(C, context(i + 1)).then_inc(ctx_in, 16)
                sp.wait_ge(dve_attn1, at(i, 6, 12))
                sp.dma_start(x2_v[:, bass.ds(i * TB, TB), :], X[:, bass.ds(i * TB, TB), :]).then_inc(x_stored, 16)
            sp.wait_ge(dve_attn1, 6 * NB + 6)
            sp.dma_start(x2_v[:, T - TB:T, :], X[:, T - TB:T, :]).then_inc(x_stored, 16)
            for q in range(4):
                sp.wait_ge(normed1_ok, 4 * q + 4)
                sp.dma_start(rows0_v[:, 4 * q:4 * q + 4, 0:L], XL[:, 4 * q:4 * q + 4, :]).then_inc(rows0_stored, 16)
            sp.wait_ge(comb_ok, 1)
            sp.dma_start(rows0_v[:, :, L:ROW], comb[:]).then_inc(comb_stored, 16)

            def load_weights(M, m, n_experts, load_up, load_down, loaded=False):
                def arrived(b, count):
                    sp.wait_ge((M["up_load_a"], M["up_load_b"])[b], count)
                    sp.sem_inc(M["up_weights"], 1)
                    sp.wait_ge((M["down_load_a"], M["down_load_b"])[b], count)
                    sp.sem_inc(M["down_weights"], 1)

                if not loaded:
                    for b in range(2):
                        load_up(b, b)
                        load_down(b, b)
                for b in range(2):
                    arrived(b, 16)
                with sp.Fori(0, n_experts // 2 - 1) as i:
                    for b in range(2):
                        done = sp.value_load(done_i[m][0:1, bass.ds(i * 2 + b, 1)], min_val=1, max_val=G0 + 1)
                        sp.wait_ge(M["up_mm"], done)
                        load_up(i * 2 + 2 + b, b)
                        sp.wait_ge(M["down_mm"], done)
                        load_down(i * 2 + 2 + b, b)
                        arrived(b, at(i, 16, 32))

            def load_up0(e, b):
                sp.dma_start(wup[:, b:b + 1, :, :], w_up[bass.ds(e, 1), :, :, :].rearrange("e p c f -> p e c f")).then_inc(
                    (M0["up_load_a"], M0["up_load_b"])[b], 16)

            def load_down0(e, b):
                sp.dma_start(wdn[0:FH, b:b + 1, :, :], w_down[bass.ds(e, 1), :, :, :].rearrange("e p k l -> p e k l")).then_inc(
                    (M0["down_load_a"], M0["down_load_b"])[b], 16)

            sp.wait_ge(table_ok[0], 1)
            load_weights(M0, 0, E0, load_up0, load_down0)

            def load_ct(n, b):
                sp.dma_start(CT[:, b:b + 1, :, :], ctx_t[bass.ds(n, 1), :, :, :].rearrange("a p c m -> p a c m")).then_inc(ct_in[b], 16)

            def load_c4(n, b):
                sp.dma_start(C4[:, b, :, :], context(n)).then_inc(c4_in[b], 16)

            for b in range(2):
                load_ct(b, b)
                load_c4(b, b)
            pairs0 = pairs_of(sp, 0, G0)
            sp.wait_ge(M0["scattered"], pairs0 * 32)
            for q, (lo, hi) in enumerate(PARTS):
                sp.dma_start(X[:, lo:hi, :], x2_v[:, lo:hi, :]).then_inc(x3_in[q], 16)
            sp.dma_start(sw1_sb, sw1).then_inc(shared_in, 16)
            sp.dma_start(sw2_sb, sw2).then_inc(shared_in, 16)
            sp.dma_start(sb1_c, sb1).then_inc(shared_in, 16)
            sp.dma_start(sb2_bc, sb2.to_broadcast([P, L])).then_inc(shared_in, 16)
            with sp.Fori(0, NB // 2 - 1) as i:
                for b in range(2):
                    sp.wait_ge(scores4_mm, at(i, 4, 2 * b + 2))
                    load_ct(i * 2 + 2 + b, b)
                    sp.wait_ge(readout4_mm, at(i, 4, 2 * b + 2))
                    load_c4(i * 2 + 2 + b, b)
            for q in range(4):
                sp.wait_ge(normed3_ok, 4 * q + 4)
                sp.dma_start(rows1_v[:, 4 * q:4 * q + 4, 0:L], XN8[:, q % 2 * 4:q % 2 * 4 + 4, :]).then_inc(rows1_stored[q % 2], 16)
            sp.dma_start(b2_bc, b2.to_broadcast([P, E1 * L]).rearrange("p (e f) -> p e f", e=E1)).then_inc(biases_in, 16)
            sp.wait_ge(comb_ok, 2)
            sp.dma_start(rows1_v[:, :, L:ROW1], comb[:, :, 0:E1]).then_inc(comb_stored, 16)

            def store_out(t):
                sp.wait_ge(MS["y_ready"], t + 1)
                sp.dma_start(out_v[:, t:t + 1, :], Y[t % 2][:].rearrange("p (a l) -> p a l", a=1)).then_inc(out_stored[t % 2], 16)

            def load_up1(e, b):
                sp.dma_start(w1_sb[:, b:b + 1, :, :], w1[bass.ds(e, 1), :, :, :].rearrange("e p c f -> p e c f")).then_inc(
                    (M1["up_load_a"], M1["up_load_b"])[b], 16)

            def load_down1(e, b):
                sp.dma_start(w2_sb[:, b:b + 1, :, :], w2[bass.ds(e, 1), :, :, :].rearrange("e p k l -> p e k l")).then_inc(
                    (M1["down_load_a"], M1["down_load_b"])[b], 16)

            for t in range(T // 2):
                store_out(t)
            sp.wait_ge(table_ok[1], 1)
            for b in range(2):
                load_up1(b, b)
                load_down1(b, b)
            for t in range(T // 2, 3 * T // 4):
                store_out(t)
            sp.wait_ge(MS["up_mm"], KC * T // 4)
            sp.dma_start(b1_bc, b1.to_broadcast([P, E1 * F1]).rearrange("p (e f) -> p e f", e=E1)).then_inc(biases_in, 16)
            for t in range(3 * T // 4, T):
                store_out(t)
            load_weights(M1, 1, E1, load_up1, load_down1, loaded=True)
            pairs1 = pairs_of(sp, 1, G1)
            sp.wait_ge(rows0_stored, 16 * 4)
            for s in rows1_stored:
                sp.wait_ge(s, 32)
            for s in out_stored:
                sp.wait_ge(s, 16 * T // 2)
            sp.wait_ge(M1["scattered"], pairs1 * 32)
            sp.sem_inc(all_stored, 1)
            sp.wait_ge(comb_stored, 32)
            sp.wait_ge(x_stored, 16 * NB)

        @block.gpsimd
        def _(pool):
            pool.memset(ident[:], 0.0).then_inc(const_ok, 1)
            pool.memset(eps_t[:], EPS).then_inc(const_ok, 1)
            pool.memset(ones_b[:], 1.0).then_inc(const_ok, 1)
            pool.memset(simd[:], 0.0).then_inc(const_ok, 1)
            pool.memset(below[:], 1.0).then_inc(const_ok, 1)
            pool.wait_ge(const_ok, 5)
            pool.affine_select(out=ident[:], in_=ident[:], compare_op=ALU.not_equal, fill=1.0, base=0,
                               pattern=[[-1, P]], channel_multiplier=1).then_inc(const_ok, 1)
            pool.affine_select(out=below[:], in_=below[:], compare_op=ALU.is_gt, fill=0.0, base=0,
                               pattern=[[1, P]], channel_multiplier=-1).then_inc(const_ok, 1)
            pool.wait_ge(vbias_ok, 1)
            with pool.Fori(0, NB) as n:
                for j in range(TB):
                    pool.wait_ge(xl_ready, at(n, TB, j + 1))
                    xt = X[:, bass.ds(n * TB + j, 1), :]
                    pool.tensor_tensor(xt, xt, vbg[:, j:j + 1].unsqueeze(1).to_broadcast([P, 1, L]),
                                       ALU.add).then_inc(vb_added, 1)
            ints = dict(allow_small_or_imprecise_dtypes=True)
            pool.iota(iota_e[:], pattern=[[1, E0]], base=0, channel_multiplier=0, **ints).then_inc(const_ok, 1)
            pool.iota(iota_p[:], pattern=[[1, P], [0, TOPK]], base=0, channel_multiplier=0, **ints).then_inc(const_ok, 1)
            pool.iota(iota_g[:], pattern=[[1, G0 + 2], [0, TOPK]], base=0, channel_multiplier=0, **ints).then_inc(const_ok, 1)
            pool.iota(token1[:], pattern=[[P, T]], base=1, channel_multiplier=1, **ints).then_inc(const_ok, 1)
            pool.memset(ones_e[:], 1.0).then_inc(const_ok, 1)
            pool.memset(zero_g[:], 0.0).then_inc(const_ok, 1)
            pool.memset(XG[0][:], 0.0).then_inc(const_ok, 1)
            pool.memset(XG[1][:], 0.0).then_inc(const_ok, 1)
            pool.wait_ge(routing_in, 16 * 7)
            pool.affine_select(out=simd[:], in_=simd[:], compare_op=ALU.not_equal, fill=1.0, base=0,
                               pattern=[[-1, P]], channel_multiplier=1).then_inc(const_ok, 1)
            pool.wait_ge(dve_attn1, 6 * NB + 6)
            pool.tensor_copy(mmul, mask_u[:]).then_inc(mask_ok, 1)
            pool.wait_ge(mask_ok, 1)
            pool.tensor_scalar(madd, mmul, 1e30, -1e30, ALU.mult, ALU.add).then_inc(mask_ok, 1)
            pool.wait_ge(vgain_ok, 1)
            pool.tensor_scalar(mmul, mmul, float(L) ** -0.5, None, ALU.mult).then_inc(mask_ok, 1)

            def experts(M, m, width, rows, dest, gmax, before_adds=None):
                pool.wait_ge(lists_ok, m + 1)
                gath = (M["gath_a"], M["gath_b"])

                def gather(g, b, count):
                    pool.tensor_copy(gi[b][:], lst_i[m][:, bass.ds(g, 1)]).then_inc(M["gi_ok"], 1)
                    pool.wait_ge(M["gi_ok"], count)
                    pool.sem_inc(gathers_begun, 1)
                    pool.indirect_dma_start(out=XG[b][:, 0:width], out_offset=None, in_=rows,
                                            in_offset=bass.IndirectOffsetOnAxis(ap=gi[b][:, 0:1], axis=0),
                                            bounds_check=NB * S - 1, oob_is_err=False).then_inc(gath[b], 16)

                gather(0, 0, 1)
                gather(1, 1, 2)
                if before_adds:
                    before_adds()
                pairs = pairs_of(pool, m, gmax)

                def take(g, b, n):
                    pool.wait_ge(M["tr_mm"], n)
                    pool.wait_ge(M["cw_ok"], n)
                    gather(g + 2, b, n + 2)

                def add(g, b, n, added):
                    if added is not None:
                        pool.wait_ge(M["scattered"], added)
                    pool.tensor_copy(si[b][:], lst_i[m][:, bass.ds(g, 1)]).then_inc(M["si_ok"], 1)
                    pool.wait_ge(M["si_ok"], n)
                    pool.wait_ge(M["y_ready"], n + 2)
                    pool.sem_inc(adds_begun, 1)
                    pool.indirect_dma_start(out=dest, out_offset=bass.IndirectOffsetOnAxis(ap=si[b][:, 0:1], axis=0),
                                            in_=Y[b][:], in_offset=None, bounds_check=NB * S - 1,
                                            oob_is_err=False, compute_op=ALU.add).then_inc(M["scattered"], 16)

                take(0, 0, 1)
                take(1, 1, 2)
                take(2, 0, 3)
                add(0, 0, 1, None)
                take(3, 1, 4)
                add(1, 1, 2, 16)
                with pool.Fori(1, pairs - 1) as i:
                    for b in range(2):
                        take(i * 2 + b + 2, b, at(i, 2, b + 3))
                        add(i * 2 + b, b, at(i, 2, b + 1), at(i, 32, 16 * b))
                add(pairs * 2 - 2, 0, pairs * 2 - 1, pairs * 32 - 32)
                add(pairs * 2 - 1, 1, pairs * 2, pairs * 32 - 16)
                for b in range(2):
                    pool.wait_ge(gath[b], at(pairs, 16, 16))
                pool.sem_inc(pool_done, 1)

            pool.wait_ge(rows0_stored, 16 * 4)
            pool.wait_ge(comb_stored, 16)
            pool.wait_ge(x_stored, 16 * NB)
            experts(M0, 0, ROW, rows0_d, x2_d, G0)

            pool.wait_ge(sb2_ok, 1)
            with pool.Fori(0, T) as t:
                pool.wait_ge(normed3_ok, at(t, 1, 1))
                pool.tensor_tensor(X[:, bass.ds(t, 1), :], X[:, bass.ds(t, 1), :],
                                   sb2_bc.rearrange("p (a l) -> p a l", a=1), ALU.add).then_inc(sb2_added, 1)

            def shared_out(t):
                pool.wait_ge(MS["scaled"], t + 1)
                pool.tensor_tensor(Y[t % 2][:], Y[t % 2][:], X[:, t, :], ALU.add).then_inc(MS["y_ready"], 1)

            def last_shared():
                for t in range(3 * T // 4, T):
                    shared_out(t)
                for b in range(2):
                    pool.wait_ge(out_stored[b], 16 * T // 2)

            pool.wait_ge(sb2_added, T)
            for t in range(3 * T // 4):
                shared_out(t)
            for s in rows1_stored:
                pool.wait_ge(s, 32)
            pool.wait_ge(comb_stored, 32)
            experts(M1, 1, ROW1, rows1_d, out_rows, G1, last_shared)

        @block.scalar
        def _(act):
            def roots(k, lo, hi, count):
                act.wait_ge(mv_ok[k], count)
                act.activation(rstd[k][:, lo:hi, :], mv[k][:, lo:hi, 1:2], ACT.Sqrt,
                               bias=eps_t[:, 0:1]).then_inc(std_ok[k], 1)

            act.wait_ge(const_ok, 2)
            roots(0, *PARTS[0], PARTS[0][1])
            act.wait_ge(w_in, 48)
            act.activation(gain[:], gain_in[:], ACT.Tanh).then_inc(gain_ok, 1)
            act.wait_ge(gain_ok, 1)
            act.activation(vbg[:], WB[:, 2, :], ACT.Copy, scale=gain[:, 0:1]).then_inc(vbias_ok, 1)

            def project(n):
                for j in range(4):
                    act.wait_ge(qk_mm, at(n, 4, j + 1))
                    dst, b = (qT, 0) if j < 2 else (kT, 1)
                    act.activation(dst[:, j % 2, :], bank[j][:], ACT.Identity,
                                   bias=WB[:, b, j % 2:j % 2 + 1]).then_inc(act_attn1, 1)

            def values(n):
                for j in range(2):
                    act.wait_ge(values_mm, at(n, 2, j + 1))
                    act.activation(v[:, 2 * j:2 * j + 2, :], bank[2 + j][:].rearrange("p (a e) -> p a e", a=2),
                                   ACT.Copy).then_inc(act_attn1, 1)

            def exps(n):
                for j in range(QT):
                    act.wait_ge(max_ready, at(n, QT, j + 1))
                    act.activation(attn[:, j, :], bank[4 + j][:], ACT.Exp, bias=negmax[:, j:j + 1],
                                   accum_out=sumexp[:, j:j + 1]).then_inc(act_attn1, 1)

            project(0)
            roots(0, PARTS[0][1], T, T)
            values(0)
            exps(0)
            with act.Fori(0, NB - 1) as i:
                project(i + 1)
                values(i + 1)
                exps(i + 1)

            roots(1, 0, T - TB, T - TB)
            roots(1, T - TB, T, T)

            def evac_logits(m, E, q_dst, after=None):
                def tile(t):
                    q, j = t // 4, t % 4
                    act.wait_ge(xnT_mm, m * T + t + 1)
                    act.activation(q_dst(q)[:, :, j * P:(j + 1) * P], bank[t % 2][:].rearrange("p (c q) -> p c q", c=KC),
                                   ACT.Copy).then_inc(xnT_ok, 1)

                def four_logits(q):
                    act.wait_ge(logitsT_mm, m * 4 + q + 1)
                    act.activation(lgT[q % 2][0:E, :], bank[6][0:E, :], ACT.Copy).then_inc(logitsT_ok, 1)

                for q in range(4):
                    if m == 0 and q > 1:
                        second_choices(q - 2)
                    for t in range(4 * q, 4 * q + 4):
                        tile(t)
                    if after:
                        four_logits(q)
                        after(q)
                    elif q:
                        four_logits(q - 1)
                    if m == 0 and q > 1:
                        similarities(q - 2)
                if not after:
                    four_logits(3)

            def second_choices(q):
                act.wait_ge(choicesT_mm, q + 1)
                act.activation(hotT_sb[q % 2], bank[2][:].rearrange("p (t q) -> p t q", t=4), ACT.Copy).then_inc(choicesT_ok, 1)

            def similarities(q):
                act.wait_ge(similar_mm, q + 1)
                act.activation(simr_sb[q], bank[3][:].rearrange("p (t j e) -> p t j e", t=4, j=4),
                               ACT.Copy).then_inc(similar_ok, 1)

            evac_logits(0, E0, lambda q: XT2[:, q % 2])
            second_choices(2)
            similarities(2)
            act.wait_ge(exp_in, 2)
            act.activation(e32[:], e32[:], ACT.Exp).then_inc(exp_ok, 1)
            act.activation(e8[:], e8[:], ACT.Exp).then_inc(exp_ok, 1)
            second_choices(3)
            similarities(3)

            with act.Fori(0, T // 2) as i:
                for b in range(2):
                    act.wait_ge(hots_ok[0], at(i, 4, 2 * b + 1))
                    act.activation(hot_p[b][:], hot_p[b][:], ACT.Copy,
                                   scale=token1[:, bass.ds(i * 2 + b, 1)]).then_inc(hots_scaled[0], 1)

            def take_rows(M, n):
                act.wait_ge(M["tr_mm"], n)
                act.activation(XE[:], bank[0][:].rearrange("p (c q) -> p c q", c=KC), ACT.Copy).then_inc(M["xe_ready"], 1)

            def silu(g1):
                act.wait_ge(M0["up_mm"], g1 + 1)
                act.activation(sg[:, 0:F0], bank[1][:, 0:F0], ACT.Silu).then_inc(M0["act_ready"], 1)

            act.wait_ge(table_ok[0], 1)
            pairs0 = pairs_of(act, 0, G0)
            take_rows(M0, 1)
            silu(1)
            take_rows(M0, 2)
            with act.Fori(0, pairs0 - 1) as i:
                for b in range(2):
                    silu(at(i, 2, 2 + b))
                    take_rows(M0, at(i, 2, 3 + b))
            silu(at(pairs0, 2, 0))

            roots(2, *PARTS[0], PARTS[0][1])

            def evac4(n):
                for j in range(TB):
                    act.wait_ge(xnT4_mm, at(n, 2, j + 1))
                    act.activation(XT4[:, :, j * P:(j + 1) * P], bank[j][:].rearrange("p (c q) -> p c q", c=KC),
                                   ACT.Copy).then_inc(xnT4_ok, 1)

            def evac_attn4(n):
                act.wait_ge(attnT4_mm, at(n, 1, 1))
                act.activation(attnT4, bank[2][:].rearrange("p (m s) -> p m s", m=2), ACT.Copy).then_inc(attnT4_ok, 1)

            def exps4(n):
                for j in range(TB):
                    act.wait_ge(max4_ok, at(n, 2, j + 1))
                    act.activation(attn4[:, j, :], sc4[:, j, :], ACT.Exp, bias=negmax4[:, j:j + 1],
                                   accum_out=sumexp4[:, j:j + 1]).then_inc(exp4_ok, 1)

            evac4(0)
            roots(2, *PARTS[1], PARTS[1][1])
            exps4(0)
            evac4(1)
            evac_attn4(0)
            roots(2, PARTS[1][1], T, T)
            with act.Fori(0, NB - 2) as i:
                evac4(i + 2)
                exps4(i + 1)
                evac_attn4(i + 1)
            exps4(NB - 1)
            evac_attn4(NB - 1)

            roots(3, 0, T - TB, T - TB)
            roots(3, T - TB, T, T)

            def gelu(M, g1, width):
                act.wait_ge(M["pre_ok"], g1)
                act.activation(hm[:, 0:width], sg[:, 0:width], ACT.Gelu).then_inc(M["hm_ready"], 1)

            def hidden(q):
                if q > 1:
                    act.wait_ge(MS["down_mm"], 4 * (q - 1))
                for f in range(KC):
                    act.wait_ge(MS["up_mm"], KC * q + f + 1)
                    act.activation(hT4[q % 2][:, f, :], bank[(2, 5)[f % 2]][:], ACT.Gelu,
                                   bias=sb1_c[:, f:f + 1]).then_inc(MS["gelu_ok"], 1)

            def scaled_out(tiles):
                for t in tiles:
                    act.wait_ge(MS["down_mm"], t + 1)
                    if t > 1:
                        act.wait_ge(out_stored[t % 2], 16 * (t // 2))
                    act.activation(Y[t % 2][:], bank[3 + t % 2][:], ACT.Copy, scale=gain[:, 3:4]).then_inc(MS["scaled"], 1)

            evac_logits(1, E1, lambda q: XT5[:, :, 4 * q * P:(4 * q + 4) * P], lambda q: hidden(q) if q < 2 else None)
            act.wait_ge(exp_in, 3)
            act.activation(e8[:, :, 0:1], e8[:, :, 0:1], ACT.Exp).then_inc(exp_ok, 1)
            scaled_out(range(0, 4))
            hidden(2)
            scaled_out(range(4, 8))
            hidden(3)
            scaled_out(range(8, T))

            act.wait_ge(table_ok[1], 1)
            pairs1 = pairs_of(act, 1, G1)
            take_rows(M1, 1)
            gelu(M1, 1, F1)
            take_rows(M1, 2)
            with act.Fori(0, pairs1 - 1) as i:
                for b in range(2):
                    gelu(M1, at(i, 2, 2 + b), F1)
                    take_rows(M1, at(i, 2, 3 + b))
            gelu(M1, at(pairs1, 2, 0), F1)

        @block.tensor
        def _(pe):
            def project(n, parts=range(4)):
                pe.wait_ge(ctx_in, at(n, 16, 16))
                pe.wait_ge(xl_ready, at(n, 2, 2))
                for j in parts:
                    w, e = j // 2, j % 2
                    for d in range(TB):
                        rhs = XL[:, bass.ds(n * TB + d, 1), :] if w == 0 else C[:, d, :]
                        mm = pe.matmul(bank[j][:], W[:, w, d, e * P:(e + 1) * P], rhs,
                                       start=(d == 0), stop=(d == TB - 1))
                    mm.then_inc(qk_mm, 1)

            def values(n):
                pe.wait_ge(act_attn1, at(n, 10, 4))
                for lt in range(QT):
                    for d in range(TB):
                        mm = pe.matmul(bank[2 + lt // 2][:, (lt % 2) * S:(lt % 2 + 1) * S],
                                       C[:, d, lt * P:(lt + 1) * P], W[:, 2, d, :],
                                       start=(d == 0), stop=(d == TB - 1))
                    if lt % 2:
                        mm.then_inc(values_mm, 1)

            def scores(n, first):
                for j in range(QT):
                    if not first:
                        pe.wait_ge(dve_attn1, at(n - 1, 6, 6 + j + 1))
                    for e in range(TB):
                        mm = pe.matmul(bank[4 + j][:], qT[:, e, j * P:(j + 1) * P], kT[:, e, :],
                                       start=(e == 0), stop=(e == TB - 1))
                    mm.then_inc(scores_mm, 1)

            def transposes(n):
                for j in range(QT):
                    pe.wait_ge(attn_ready, at(n, QT, j + 1))
                    for k in range(QT):
                        mm = pe.transpose(bank[4 + j][:, k * P:(k + 1) * P], attn[:, j, k * P:(k + 1) * P],
                                          ident[:])
                    mm.then_inc(attnT_mm, 1)

            def apply(n):
                pe.wait_ge(dve_attn1, at(n, 6, 6 + 4))
                for d in range(TB):
                    for k in range(QT):
                        mm = pe.matmul(bank[d][:], v[:, k, d * P:(d + 1) * P], attnT[:, k, :],
                                       start=(k == 0), stop=(k == QT - 1))
                    mm.then_inc(out_mm, 1)

            for m in range(2):
                pe.sem_inc(hots_mm[m], 2)
            pe.wait_ge(const_ok, 7)
            pe.wait_ge(w_in, 48)
            project(0)
            values(0)
            scores(0, True)
            with pe.Fori(0, NB - 1) as i:
                pe.wait_ge(dve_attn1, at(i, 6, 6))
                pe.wait_ge(act_attn1, at(i, 10, 6))
                project(i + 1, range(3))
                transposes(i)
                project(i + 1, [3])
                pe.wait_ge(act_attn1, at(i, 10, 10 + 2))
                apply(i)
                values(i + 1)
                scores(i + 1, False)
            transposes(NB - 1)
            pe.wait_ge(dve_attn1, 6 * NB)
            pe.wait_ge(act_attn1, 10 * NB)
            apply(NB - 1)

            def transpose_tile(dst, src, done):
                for c in range(KC):
                    mm = pe.transpose(dst[:, c * P:(c + 1) * P], src[:, c * P:(c + 1) * P], ident[:])
                mm.then_inc(done, 1)

            def tile_logits(m, E, gate, src, src_ok, xt_of, after=None):
                def tr(t):
                    pe.wait_ge(src_ok, t + 1)
                    if m * T + t > 1:
                        pe.wait_ge(xnT_ok, m * T + t - 1)
                    for c in range(KC):
                        mm = pe.transpose(bank[t % 2][:, c * P:(c + 1) * P], src(t)[:, c * P:(c + 1) * P], ident[:])
                    mm.then_inc(xnT_mm, 1)

                def logits(q):
                    pe.wait_ge(xnT_ok, m * T + 4 * q + 4)
                    if m * 4 + q:
                        pe.wait_ge(logitsT_ok, m * 4 + q)
                    for c in range(KC):
                        mm = pe.matmul(bank[6][0:E, :], gate[:, c, :], xt_of(q)[:, c, :],
                                       start=(c == 0), stop=(c == KC - 1))
                    mm.then_inc(logitsT_mm, 1)

                def back(q):
                    pe.wait_ge(logitsT_ok, m * 4 + q + 1)
                    if m * 4 + q > 1:
                        pe.wait_ge(logits_ok, m * 4 + q - 1)
                    for j in range(4):
                        mm = pe.transpose(bank[LG_BANKS[m][q % 2]][:, j * E:(j + 1) * E],
                                          lgT[q % 2][0:E, j * P:(j + 1) * P], ident[0:E, 0:E])
                    mm.then_inc(logits_mm, 1)

                for q in range(4):
                    for t in range(4 * q, 4 * q + 4):
                        tr(t)
                    if m == 0 and q > 1:
                        similarities(q - 2)
                    if q:
                        back(q - 1)
                    logits(q)
                    if m == 0 and q:
                        second_choices(q - 1)
                    if after:
                        after(q)
                back(3)

            def second_choices(q):
                pe.wait_ge(hot_ok, q + 1)
                for j in range(4):
                    mm = pe.transpose(bank[2][:, j * P:(j + 1) * P],
                                      hot[:, 4 * q + j, PRIM:TOPK, :].rearrange("p k e -> p (k e)"), ident[:])
                mm.then_inc(choicesT_mm, 1)

            def similarities(q):
                pe.wait_ge(choicesT_ok, q + 1)
                if q:
                    pe.wait_ge(similar_ok, q)
                for j in range(4):
                    mm = pe.matmul(bank[3][:, j * P:(j + 1) * P], hotT_sb[q % 2][:, j, :], simd[:], start=True, stop=True)
                mm.then_inc(similar_mm, 1)

            pe.wait_ge(routing_in, 32)
            pe.wait_ge(const_ok, 16)
            pe.wait_ge(dve_attn1, 6 * NB + 6)
            tile_logits(0, E0, gate0_sb, lambda t: XL[:, t, :], normed1_ok, lambda q: XT2[:, q % 2])
            similarities(2)
            second_choices(3)
            similarities(3)

            def positions(m, E):
                pe.wait_ge(chosen_ok, m + 1)
                ch = chosen[:, :, 0:E]
                for t in range(T):
                    mm = pe.matmul(bank[1][:, 0:E], ones_b[:], ch[:, t, :], start=(t == 0), stop=(t == T - 1))
                mm.then_inc(counts_mm, 1)
                out_pos = bank[0][:, 0:T * E].rearrange("p (t e) -> p t e", t=T)
                pe.matmul(out_pos, below[:], ch, start=True, stop=False)
                for t in range(T - 1):
                    later = T - 1 - t
                    pe.matmul(out_pos[:, t + 1:T, :], ones_b[:],
                              ch[:, t:t + 1, :].to_broadcast([P, later, E]), start=False, stop=False)
                pe.matmul(out_pos, zero_g[:, 0:P], ch, start=False, stop=True).then_inc(positions_mm, 1)

            def table(m, E, G):
                pe.wait_ge(ended_ok, m + 1)
                pe.matmul(bank[7][0:1, 0:G + 2], ones_b[0:E, 0:1], ended[0:E, 0:G + 2], start=True,
                          stop=True).then_inc(table_mm, 1)

            def lists_edge(m, G, first):
                return pe.matmul(bank[LIST_BANKS[m]][:, 0:G + 2], iota_p[:, :, 0], zero_g[:, 0:G + 2], start=first, stop=not first)

            def lists_pair(m, K, G, i):
                per = TOPK // K if m else 1
                for b in range(2):
                    pe.wait_ge(hots_ok[m], at(i, 4, 2 * b + 2))
                    pe.wait_ge(hots_scaled[m], at(i, 2 * per, (b + 1) * per))
                    for k in range(TOPK):
                        mm = pe.matmul(bank[LIST_BANKS[m]][:, 0:G + 2], hot_p[b][:, :, k], hot_g[b][:, 0:G + 2, k],
                                       start=False, stop=False)
                    mm.then_inc(hots_mm[m], 1)

            positions(0, E0)
            table(0, E0, G0)
            lists_edge(0, G0, True)
            with pe.Fori(0, T // 2) as i:
                lists_pair(0, TOPK, G0, i)
            lists_edge(0, G0, False).then_inc(hots_mm[0], 1)

            def down(M, b, n, size, e, wd):
                pe.wait_ge(M["down_weights"], e + 1)
                pe.wait_ge(M["ht_ready"], n)
                pe.wait_ge(M["y_ready"], n)
                for k in range(2):
                    mm = pe.matmul(bank[3 + b][:], hT[0:size, k, :], wd(k), start=(k == 0), stop=(k == 1))
                mm.then_inc(M["down_mm"], 1)

            def hidden_transposes(M, n, size):
                pe.wait_ge(M["hm_ready"], n)
                for k in range(2):
                    mm = pe.transpose(bank[2][0:size, k * P:(k + 1) * P], hm[:, k * size:(k + 1) * size], ident[:])
                mm.then_inc(M["ht_mm"], 1)

            def experts(M, m, wu, wd, width, size, gmax):
                pe.sem_inc(M["up_mm"], 1)
                pe.sem_inc(M["down_mm"], 1)
                pairs = pairs_of(pe, m, gmax)
                gath = (M["gath_a"], M["gath_b"])

                def expert_of(g):
                    return pe.value_load(tab[m][0:1, bass.ds(g, 1)], min_val=0, max_val=31)

                def tr(b, n):
                    pe.wait_ge(gath[b], n)
                    transpose_tile(bank[0], XG[b], M["tr_mm"])

                def place(w, e, k):
                    return w[0:size if w is wd else P, bass.ds((e % 2), 1), k, :]

                def up(g, e):
                    pe.wait_ge(M["up_weights"], e + 1)
                    pe.wait_ge(M["xe_ready"], g + 1)
                    for c in range(KC):
                        mm = pe.matmul(bank[1][:, 0:width], XE[:, c, :], place(wu, e, c), start=(c == 0), stop=(c == KC - 1))
                    mm.then_inc(M["up_mm"], 1)

                tr(0, 16)
                up(0, expert_of(0))
                tr(1, 16)
                e1 = expert_of(1)
                hidden_transposes(M, 1, size)
                up(1, e1)
                with pe.Fori(0, pairs - 1) as i:
                    g = i * 2 + 1
                    e = {-1: expert_of(g - 1)}
                    for b in range(2):
                        tr(b, at(i, 16, 32))
                        down(M, b, g + b, size, e[b - 1], lambda k: place(wd, e[b - 1], k))
                        e[b + 1] = expert_of(g + b + 1)
                        if b == 0:
                            e[0] = expert_of(g)
                        hidden_transposes(M, g + b + 1, size)
                        up(g + b + 1, e[b + 1])
                g = pairs * 2 - 1
                e = [expert_of(g + k - 1) for k in range(2)]
                down(M, 0, g, size, e[0], lambda k: place(wd, e[0], k))
                hidden_transposes(M, g + 1, size)
                down(M, 1, g + 1, size, e[1], lambda k: place(wd, e[1], k))
                return pairs

            pe.wait_ge(table_ok[0], 1)
            pairs = experts(M0, 0, wup, wdn, 2 * F0, FH, G0)

            def tr4(n):
                pe.wait_ge(normed2_ok, at(n, 2, 2))
                for j in range(TB):
                    transpose_tile(bank[j], XN[j], xnT4_mm)

            def scores4(n, b, cin):
                pe.wait_ge(ct_in[b], cin)
                pe.wait_ge(xnT4_ok, at(n, 2, 2))
                for j in range(TB):
                    for c in range(KC):
                        mm = pe.matmul(bank[5 + j][:, 0:S], XT4[:, c, j * P:(j + 1) * P], CT[:, b, c, :],
                                       start=(c == 0), stop=(c == KC - 1))
                    mm.then_inc(scores4_mm, 1)

            def attn_transposes4(n):
                pe.wait_ge(exp4_ok, at(n, 2, 2))
                for j in range(TB):
                    for k in range(2):
                        mm = pe.transpose(bank[2][:, k * S + j * P:k * S + (j + 1) * P],
                                          attn4[:, j, k * P:(k + 1) * P], ident[:])
                mm.then_inc(attnT4_mm, 1)

            def read4(n, b, cin):
                pe.wait_ge(c4_in[b], cin)
                pe.wait_ge(attnT4_ok, at(n, 1, 1))
                pe.wait_ge(dve4, at(n, 2, 2))
                for j in range(TB):
                    for k in range(2):
                        mm = pe.matmul(bank[3 + j][:], attnT4[:, k, j * P:(j + 1) * P], C4[:, b, k, :],
                                       start=(k == 0), stop=(k == 1))
                    mm.then_inc(readout4_mm, 1)

            pe.wait_ge(M0["y_ready"], at(pairs, 2, 2))
            tr4(0)
            scores4(0, 0, 16)
            tr4(1)
            attn_transposes4(0)
            with pe.Fori(0, NB // 2 - 1) as i:
                for b in range(2):
                    scores4(i * 2 + b + 1, 1 - b, at(i, 16, 16 + 16 * b))
                    tr4(i * 2 + b + 2)
                    read4(i * 2 + b, b, at(i, 16, 16))
                    attn_transposes4(i * 2 + b + 1)
            scores4(NB - 1, 1, 8 * NB)
            read4(NB - 2, 0, 8 * NB)
            attn_transposes4(NB - 1)
            read4(NB - 1, 1, 8 * NB)

            pe.wait_ge(dve4, 2 * NB + 2)
            def shared_up(q):
                for f in range(KC):
                    if q or f > 1:
                        pe.wait_ge(MS["gelu_ok"], KC * q + f - 1)
                    for c in range(KC):
                        mm = pe.matmul(bank[(2, 5)[f % 2]][:], sw1_sb[:, c, f * P:(f + 1) * P],
                                       XT5[:, c, 4 * q * P:(4 * q + 4) * P], start=(c == 0), stop=(c == KC - 1))
                    mm.then_inc(MS["up_mm"], 1)

            def shared_down(q):
                pe.wait_ge(MS["gelu_ok"], KC * (q + 1))
                for t in range(4 * q, 4 * q + 4):
                    if t > 1:
                        pe.wait_ge(MS["scaled"], t - 1)
                    for f in range(KC):
                        mm = pe.matmul(bank[3 + t % 2][:], hT4[q % 2][:, f, t % 4 * P:(t % 4 + 1) * P], sw2_sb[:, f, :],
                                       start=(f == 0), stop=(f == KC - 1))
                    mm.then_inc(MS["down_mm"], 1)

            pe.wait_ge(shared_in, 64)
            tile_logits(1, E1, gate1_sb, lambda t: XN8[:, t % 8, :], normed3_ok, lambda q: XT5[:, :, 4 * q * P:(4 * q + 4) * P],
                        lambda q: shared_up(q) if q < 2 else None)
            pe.wait_ge(logits_ok, 8)
            shared_down(0)
            positions(1, E1)
            shared_up(2)
            table(1, E1, G1)
            shared_down(1)
            lists_edge(1, G1, True)
            lists_pair(1, K1, G1, 0)
            shared_up(3)
            lists_pair(1, K1, G1, 1)
            lists_edge(1, G1, False).then_inc(hots_mm[1], 1)
            shared_down(2)
            shared_down(3)
            pe.wait_ge(table_ok[1], 1)
            pe.wait_ge(MS["scaled"], T)
            experts(M1, 1, w1_sb, w2_sb, F1, P, G1)

        @block.vector
        def _(dve):
            dve.sem_inc(dve_attn1, 6)
            dve.sem_inc(dve4, 2)
            for M in (M0, M1):
                dve.sem_inc(M["y_ready"], 2)

            def tile_stats(k, t):
                dve.bn_stats(stats[:, bass.ds(t, 1), :], X[:, bass.ds(t, 1), :]).then_inc(st_ok[k], 1)

            def moments(k, lo, hi):
                dve.wait_ge(st_ok[k], hi)
                for t in range(lo, hi):
                    dve.bn_aggr(mv[k][:, t, :], stats[:, t, :]).then_inc(mv_ok[k], 1)

            def inverse(k, lo, hi, n):
                dve.wait_ge(std_ok[k], n)
                dve.reciprocal(rstd[k][:, lo:hi, :], rstd[k][:, lo:hi, :]).then_inc(rstd_ok[k], 1)
                dve.wait_ge(rstd_ok[k], n)

            def norm(k, dst, t, done):
                dve.tensor_scalar(dst, X[:, bass.ds(t, 1), :], mv[k][:, bass.ds(t, 1), 0:1], rstd[k][:, bass.ds(t, 1), 0:1],
                                  ALU.subtract, ALU.mult).then_inc(done, 1)

            for n, parts in ((1, range(1)), (2, range(1, len(PARTS)))):
                lo, hi = PARTS[parts[0]][0], PARTS[parts[-1]][1]
                for q in parts:
                    dve.wait_ge(x_in[q], 16)
                    for t in range(*PARTS[q]):
                        tile_stats(0, t)
                moments(0, lo, hi)
                inverse(0, lo, hi, n)
                dve.wait_ge(mv_ok[0], hi)
                for t in range(lo, hi):
                    norm(0, XL[:, t:t + 1, :], t, xl_ready)

            def softmax(n):
                def scale(j):
                    dve.wait_ge(act_attn1, at(n, 10, 7 + j))
                    dve.reciprocal(rsum[:, j:j + 1], sumexp[:, j:j + 1]).then_inc(rsum_ok, 1)
                    dve.wait_ge(rsum_ok, at(n, QT, j + 1))
                    dve.tensor_scalar(attn[:, j, :], attn[:, j, :], rsum[:, j:j + 1], None,
                                      ALU.mult).then_inc(attn_ready, 1)

                for j in range(QT):
                    dve.wait_ge(scores_mm, at(n, QT, j + 1))
                    dve.tensor_reduce(negmax[:, j:j + 1], bank[4 + j][:], AX.X, ALU.max,
                                      negate=True).then_inc(max_ready, 1)
                    if j:
                        scale(j - 1)
                scale(QT - 1)

            def attn_out(n):
                for j in range(QT):
                    dve.wait_ge(attnT_mm, at(n, QT, j + 1))
                    dve.tensor_copy(attnT[:, :, j * P:(j + 1) * P],
                                    bank[4 + j][:].rearrange("p (k q) -> p k q", k=QT)).then_inc(dve_attn1, 1)

            def outputs(n):
                for d in range(TB):
                    dve.wait_ge(out_mm, at(n, 2, d + 1))
                    dve.wait_ge(vb_added, at(n, 2, d + 1))
                    xt = X[:, bass.ds(n * TB + d, 1), :]
                    dve.scalar_tensor_tensor(out=xt, in0=bank[d][:].rearrange("p (a l) -> p a l", a=1),
                                             scalar=gain[:, 0:1], in1=xt, op0=ALU.mult, op1=ALU.add).then_inc(dve_attn1, 1)

            def row_stats(k, n, d, own, count):
                dve.wait_ge(own, count)
                tile_stats(k, n * TB + d)

            softmax(0)
            with dve.Fori(0, NB - 1) as i:
                attn_out(i)
                outputs(i)
                softmax(i + 1)
                for d in range(TB):
                    row_stats(1, i, d, dve_attn1, at(i, 6, 6 + 5 + d))
            attn_out(NB - 1)

            moments(1, 0, T - TB)
            inverse(1, 0, T - TB, 1)
            dve.wait_ge(mv_ok[1], T - TB)
            for t in range(T // 2):
                norm(1, XL[:, t:t + 1, :], t, normed1_ok)
            outputs(NB - 1)
            for d in range(TB):
                row_stats(1, NB - 1, d, dve_attn1, at(NB - 1, 6, 6 + 5 + d))
            moments(1, T - TB, T)
            inverse(1, T - TB, T, 2)
            dve.wait_ge(mv_ok[1], T)
            for t in range(T // 2, T):
                norm(1, XL[:, t:t + 1, :], t, normed1_ok)

            R = Log(dve, "routing_steps")

            def run(ins):
                R(ins)
                R.wait()

            dve.wait_ge(mask_ok, 2)
            dve.tensor_reduce(vgain[:], mmul, AX.X, ALU.max).then_inc(vgain_ok, 1)
            dve.wait_ge(vgain_ok, 1)
            dve.tensor_scalar(vgain[:], vgain[:], gain[:, 1:2], None, ALU.mult).then_inc(vgain_ok, 1)

            def last(ap, n):
                return ap.unsqueeze(len(ap.shape)).to_broadcast(list(ap.shape) + [n])

            def third(ap, n):
                s = list(ap.shape)
                return ap.unsqueeze(2).to_broadcast([s[0], s[1], n, s[2]])

            def best_experts(m, E, K, hots, last_quarter):
                for q in range(4):
                    ts = slice(4 * q, 4 * q + 4)
                    dve.wait_ge(logits_mm, m * 4 + q + 1)
                    dve.tensor_copy(lg[:, ts, 0:E],
                                    bank[LG_BANKS[m][q % 2]][:, 0:4 * E].rearrange("p (t e) -> p t e", t=4)).then_inc(logits_ok, 1)
                    dve.wait_ge(logits_ok, m * 4 + q + 1)
                    for t in range(4 * q, 4 * q + 4):
                        R(dve.max(v8[:, t, :], lg[:, t, 0:E]))
                    R.wait()
                    for t in range(4 * q, 4 * q + 4):
                        R(dve.max_index(i8[:, t, :], v8[:, t, :], lg[:, t, 0:E]))
                    if q == 3:
                        last_quarter()
                    R.wait()
                    run(dve.tensor_copy(i8f[:, ts, :], i8[:, ts, :]))
                    dve.tensor_tensor(hots[:, ts, :, :],
                                      iota_e[:, 0:E].unsqueeze(1).unsqueeze(1).to_broadcast([P, 4, K, E]),
                                      last(i8f[:, ts, 0:K], E), ALU.is_equal).then_inc(hot_ok, 1)
                    if m == 0 and q:
                        similarities(q - 1)
                dve.wait_ge(hot_ok, m * 4 + 4)

            def similarities(q):
                ts = slice(4 * q, 4 * q + 4)
                dve.wait_ge(hot_ok, q + 1)
                dve.wait_ge(similar_ok, q + 1)
                for j in range(4):
                    run(dve.tensor_tensor(wide4[j % 2], third(simr_sb[q][:, :, j, :], PRIM), hot[:, ts, 0:PRIM, :], ALU.mult))
                    R(dve.tensor_reduce(cand[:, ts, j, :], wide4[j % 2], AX.X, ALU.add))

            def differences0():
                top = v8[:, :, 0:1]
                dve.tensor_tensor(e32[:], lg[:], top.to_broadcast([P, T, E0]), ALU.subtract).then_inc(exp_in, 1)
                dve.tensor_tensor(e8[:], v8[:], top.to_broadcast([P, T, TOPK]), ALU.subtract).then_inc(exp_in, 1)

            dve.wait_ge(const_ok, 15)
            best_experts(0, E0, TOPK, hot, differences0)
            dve.wait_ge(exp_ok, 2)
            run(dve.tensor_reduce(t16[:], e32[:], AX.X, ALU.add))
            run(dve.reciprocal(t16[:], t16[:]))
            run(dve.tensor_tensor(e8[:], e8[:], last(t16[:], TOPK), ALU.mult))
            run(dve.tensor_reduce(t16[:], e8[:], AX.X, ALU.add))
            run(dve.tensor_scalar(t16[:], t16[:], 1e-12, None, ALU.max))
            run(dve.reciprocal(t16[:], t16[:]))
            run(dve.tensor_tensor(fw[:], e8[:], last(t16[:], TOPK), ALU.mult))
            run(dve.tensor_scalar(fw[:], fw[:], gain[:, 2:3], None, ALU.mult))
            similarities(3)
            R.wait()
            dve.wait_ge(rows0_stored, 16 * 4)
            run(dve.tensor_reduce(best[:], cand[:], AX.X, ALU.max))
            run(dve.tensor_tensor(sel[:], cand[:], last(best[:], PRIM), ALU.is_equal))
            run(dve.tensor_scalar(left[:], sel[:, :, :, 0], -1.0, 1.0, ALU.mult, ALU.add))
            for i in range(1, PRIM):
                run(dve.tensor_tensor(sel[:, :, :, i], sel[:, :, :, i], left[:], ALU.mult))
                if i < PRIM - 1:
                    run(dve.tensor_tensor(left[:], left[:], sel[:, :, :, i], ALU.subtract))
            run(dve.tensor_scalar(keep[:], best[:], THRESHOLD, None, ALU.is_lt))
            run(dve.tensor_tensor(keep[:], fw[:, :, PRIM:TOPK], keep[:], ALU.mult))
            run(dve.tensor_tensor(moved[:], fw[:, :, PRIM:TOPK], keep[:], ALU.subtract))
            run(dve.tensor_copy(fw[:, :, PRIM:TOPK], keep[:]))
            run(dve.tensor_tensor(madd4[:], sel[:], last(moved[:], PRIM), ALU.mult))
            run(dve.tensor_reduce(left[:], madd4[:].rearrange("p t j i -> p t i j"), AX.X, ALU.add))
            run(dve.tensor_tensor(fw[:, :, 0:PRIM], fw[:, :, 0:PRIM], left[:], ALU.add))

            def dispatch(m, E, K, G, hots, room):
                f = fw[:, :, 0:K]
                run(dve.tensor_tensor(room, hots, last(f, E), ALU.mult))
                dve.tensor_reduce(comb[:, :, 0:E], room.rearrange("p t k e -> p t e k"), AX.X,
                                  ALU.add).then_inc(comb_ok, 1)
                dve.wait_ge(comb_ok, m + 1)
                dve.tensor_scalar(chosen[:, :, 0:E], comb[:, :, 0:E], 0.0, None, ALU.not_equal).then_inc(chosen_ok, 1)
                run(dve.tensor_scalar(act8[:, :, 0:K], f, 0.0, None, ALU.not_equal))
                dve.wait_ge(counts_mm, m + 1)
                ci, tl, cum, bs = cnt_i[:, 0:E], tiles[:, 0:E], tiles_cum[:, 0:E], base[:, 0:E]
                run(dve.tensor_scalar(ci, bank[1][:, 0:E], float(P - 1), None, ALU.add))
                run(dve.tensor_scalar(ci, ci, 7, None, ALU.arith_shift_right))
                run(dve.tensor_copy(tl, ci))
                run(dve.tensor_tensor_scan(cum, ones_e[:, 0:E], tl, 0.0, ALU.mult, ALU.add))
                run(dve.tensor_tensor(cum_diag[0:E, 0:E], cum[0:E, :], ident[0:E, 0:E], ALU.mult))
                run(dve.tensor_reduce(cum_col[0:E, :], cum_diag[0:E, 0:E], AX.X, ALU.add))
                dve.tensor_scalar(ended[0:E, 0:G + 2], iota_g[0:E, 0:G + 2, 0], cum_col[0:E, 0:1], None,
                                  ALU.is_ge).then_inc(ended_ok, 1)
                run(dve.tensor_scalar(done_i[m][:, 0:E], cum[0:1, :], 1.0, None, ALU.add))
                run(dve.tensor_scalar(pairs_i[m][:], cum[0:1, E - 1:E], 1.0, None, ALU.add))
                run(dve.tensor_scalar(pairs_i[m][:], pairs_i[m][:], 1, None, ALU.arith_shift_right))
                run(dve.tensor_copy(pairs_f[:], pairs_i[m][:]))
                run(dve.tensor_scalar(pairs_i[m][:], pairs_f[:], -3.0, 0.0, ALU.add, ALU.max))
                run(dve.tensor_tensor(bs, cum, tl, ALU.subtract))
                run(dve.tensor_scalar(bs, bs, float(P), None, ALU.mult))
                g = gp[:, :, 0:E]
                dve.wait_ge(positions_mm, m + 1)
                run(dve.tensor_tensor(g, bank[0][:, 0:T * E].rearrange("p (t e) -> p t e", t=T),
                                      bs.unsqueeze(1).to_broadcast([P, T, E]), ALU.add))
                run(dve.tensor_tensor(room, hots, third(g, K), ALU.mult))
                dve.wait_ge(table_mm, m + 1)
                dve.tensor_scalar(tab[m][:, 0:G + 2], bank[7][0:1, 0:G + 2], float(E - 1), None,
                                  ALU.min).then_inc(table_ok[m], 1)
                s, a = slot[:, :, 0:K], act8[:, :, 0:K]
                run(dve.tensor_reduce(s, room, AX.X, ALU.add))
                run(dve.tensor_scalar(s, s, 1.0, None, ALU.add))
                run(dve.tensor_tensor(s, s, a, ALU.mult))
                run(dve.tensor_scalar(slot_i[:, :, 0:K], s, -1.0, None, ALU.add))
                run(dve.tensor_scalar(part_i[:, :, 0:K], slot_i[:, :, 0:K], P - 1, None, ALU.bitwise_and))
                run(dve.tensor_scalar(slot_i[:, :, 0:K], slot_i[:, :, 0:K], 7, None, ALU.arith_shift_right))
                per = TOPK // K
                packed_p, packed_g = (a[:].rearrange("p t k -> p (t k)")[:, 0:T * K].rearrange("p (q j) -> p q j", j=TOPK)
                                      for a in (slot_p, slot_g))
                for packed, ints in ((packed_p, part_i), (packed_g, slot_i)):
                    run(dve.tensor_copy(packed.rearrange("p q (t k) -> p q t k", k=K),
                                        ints[:, :, 0:K].rearrange("p (q t) k -> p q t k", t=per)))
                with dve.Fori(0, T // per // 2) as i:
                    for b in range(2):
                        dve.wait_ge(hots_mm[m], at(i, 2, b + 1))
                        for dst, numbers, slots, n in ((hot_p[b], iota_p, packed_p, P), (hot_g[b], iota_g, packed_g, G + 2)):
                            dve.tensor_tensor(dst[:, 0:n, :], numbers[:, 0:n, :],
                                              slots[:, bass.ds(i * 2 + b, 1), :].to_broadcast([P, n, TOPK]),
                                              ALU.is_equal).then_inc(hots_ok[m], 1)
                        if m == 1:
                            dve.wait_ge(hots_ok[m], at(i, 4, 2 * b + 1))
                            for j in range(per):
                                places = hot_p[b][:, :, j * K:(j + 1) * K]
                                dve.tensor_scalar(places, places, token1[:, bass.ds((i * 2 + b) * per + j, 1)], None,
                                                  ALU.mult).then_inc(hots_scaled[m], 1)
                dve.wait_ge(hots_mm[m], T // per + 3)
                run(dve.tensor_copy(lst[:, 0:G + 2], bank[LIST_BANKS[m]][:, 0:G + 2]))
                run(dve.tensor_scalar(lst2[:, 0:G + 2], lst[:, 0:G + 2], 0.0, float(NONE), ALU.is_equal, ALU.mult))
                dve.scalar_tensor_tensor(out=lst_i[m][:, 0:G + 2], in0=lst[:, 0:G + 2], scalar=-1.0, in1=lst2[:, 0:G + 2],
                                         op0=ALU.add, op1=ALU.add).then_inc(lists_ok, 1)

            dispatch(0, E0, TOPK, G0, hot, wide)

            def hidden_out(M, n, size):
                dve.wait_ge(M["ht_mm"], n)
                dve.tensor_copy(hT[0:size, 0:2, :],
                                bank[2][0:size, 0:2 * P].rearrange("p (k q) -> p k q", k=2)).then_inc(M["ht_ready"], 1)

            def experts(M, m, gmax, size, middle, weighted, n_e, needs_expert):
                pairs = pairs_of(dve, m, gmax)
                gath = (M["gath_a"], M["gath_b"])

                def expert_of(g):
                    return dve.value_load(tab[m][0:1, bass.ds(g, 1)], min_val=0, max_val=n_e - 1)

                def y(g, b, e, early):
                    dve.wait_ge(M["down_mm"], g + 2)
                    dve.wait_ge(M["cw_ok"], g + 1)
                    if not early:
                        dve.wait_ge(M["scattered"], g * 16 - 16)
                    weighted(g, b, e)

                def weights(g, b, e, gcount):
                    dve.wait_ge(gath[b], gcount)
                    dve.tensor_copy(cw[:, bass.ds(g % 4, 1)], XG[b][:, bass.ds(e + L, 1)]).then_inc(M["cw_ok"], 1)

                def tile(g, b, e, ahead, early=False, first=False):
                    middle(g, e[1])
                    if ahead is not None:
                        e.append(expert_of(g + 1))
                        weights(g + 1, 1 - b, e[2], ahead)
                    hidden_out(M, g + 1, size)
                    if not first:
                        y(g - 1, 1 - b, expert_of(g - 1) if needs_expert and e[0] is None else e[0], early)
                    return e[1:]

                e = [None, expert_of(0)]
                weights(0, 0, e[1], 16)
                e = tile(0, 0, e, 16, True, True)
                e = tile(1, 1, e, 32, True)
                tile(2, 0, e, 32, True)
                with dve.Fori(1, pairs - 1) as i:
                    e = [None, expert_of(i * 2 + 1) if needs_expert else None]
                    e = tile(i * 2 + 1, 1, e, at(i, 16, 32))
                    tile(i * 2 + 2, 0, e, at(i, 16, 32))
                g = pairs * 2 - 1
                e = [None, expert_of(g)]
                tile(g, 1, e, None)
                y(g, 1, e[1], False)

            def middle0(g, e):
                dve.wait_ge(M0["act_ready"], g + 1)
                dve.tensor_tensor(hm[:, 0:F0], bank[1][:, F0:2 * F0], sg[:, 0:F0], ALU.mult).then_inc(M0["hm_ready"], 1)

            def weighted0(g, b, ed):
                dve.tensor_scalar(Y[b][:], bank[3 + b][:], cw[:, bass.ds(g % 4, 1)], None, ALU.mult).then_inc(M0["y_ready"], 1)

            dve.wait_ge(lists_ok, 1)
            experts(M0, 0, G0, FH, middle0, weighted0, E0, False)

            def stats3(parts):
                for q in parts:
                    dve.wait_ge(x3_in[q], 16)
                    for t in range(*PARTS[q]):
                        tile_stats(2, t)
                moments(2, PARTS[parts[0]][0], PARTS[q][1])

            stats3([0])
            inverse(2, *PARTS[0], 1)
            dve.wait_ge(mv_ok[2], PARTS[0][1])
            dve.wait_ge(vgain_ok, 2)
            dve.wait_ge(mask_ok, 3)

            def norm4(n):
                for j in range(TB):
                    norm(2, XN[j][:].rearrange("p (a l) -> p a l", a=1), n * TB + j, normed2_ok)

            def softmax4(n):
                for j in range(TB):
                    dve.wait_ge(scores4_mm, at(n, 2, j + 1))
                    dve.tensor_tensor(sc4[:, j:j + 1, :], bank[5 + j][:, 0:S].rearrange("p (a m) -> p a m", a=1),
                                      mmul[:, bass.ds(n, 1), :], ALU.mult).then_inc(masked4_ok, 1)
                    dve.wait_ge(masked4_ok, at(n, 4, 2 * j + 1))
                    dve.tensor_tensor(sc4[:, j:j + 1, :], sc4[:, j:j + 1, :], madd[:, bass.ds(n, 1), :],
                                      ALU.add).then_inc(masked4_ok, 1)
                    dve.wait_ge(masked4_ok, at(n, 4, 2 * j + 2))
                    dve.tensor_reduce(negmax4[:, j:j + 1], sc4[:, j, :], AX.X, ALU.max, negate=True).then_inc(max4_ok, 1)

            def inverse_sums4(n):
                dve.wait_ge(exp4_ok, at(n, 2, 2))
                dve.reciprocal(rsum4[:], sumexp4[:]).then_inc(rsum4_ok, 1)
                dve.wait_ge(rsum4_ok, at(n, 2, 1))
                dve.tensor_scalar(rsum4[:], rsum4[:], vgain[:, bass.ds(n, 1)], None, ALU.mult).then_inc(rsum4_ok, 1)

            def read_out4(n):
                dve.wait_ge(rsum4_ok, at(n, 2, 2))
                for j in range(TB):
                    dve.wait_ge(readout4_mm, at(n, 2, j + 1))
                    xt = X[:, bass.ds(n * TB + j, 1), :]
                    dve.scalar_tensor_tensor(out=xt, in0=bank[3 + j][:].rearrange("p (a l) -> p a l", a=1),
                                             scalar=rsum4[:, j:j + 1], in1=xt, op0=ALU.mult, op1=ALU.add).then_inc(dve4, 1)

            def stats4(n):
                for j in range(TB):
                    row_stats(3, n, j, dve4, at(n, 2, 2 + j + 1))

            norm4(0)
            stats3([1])
            softmax4(0)
            inverse(2, *PARTS[1], 2)
            dve.wait_ge(mv_ok[2], PARTS[1][1])
            dve.wait_ge(xnT4_mm, 2)
            norm4(1)
            stats3([2, 3])
            inverse(2, PARTS[1][1], T, 3)
            dve.wait_ge(mv_ok[2], T)
            with dve.Fori(0, NB - 2) as i:
                inverse_sums4(i)
                dve.wait_ge(xnT4_mm, at(i, 2, 4))
                norm4(i + 2)
                softmax4(i + 1)
                read_out4(i)
                stats4(i)
            inverse_sums4(NB - 2)
            softmax4(NB - 1)
            read_out4(NB - 2)
            stats4(NB - 2)
            inverse_sums4(NB - 1)
            moments(3, 0, T - TB)
            inverse(3, 0, T - TB, 1)
            dve.wait_ge(mv_ok[3], T - TB)
            read_out4(NB - 1)

            dve.wait_ge(xnT4_mm, 2 * NB)
            for t in range(T):
                if t == 2:
                    stats4(NB - 1)
                    moments(3, T - TB, T)
                    inverse(3, T - TB, T, 2)
                    dve.wait_ge(mv_ok[3], T)
                if t > 7:
                    dve.wait_ge(xnT_mm, T + t - 7)
                    dve.wait_ge(rows1_stored[t // 4 % 2], 16)
                norm(3, XN8[:, t % 8:t % 8 + 1, :], t, normed3_ok)
                if t == 7:
                    dve.wait_ge(shared_in, 64)
                    dve.tensor_scalar(sb2_bc, sb2_bc, gain[:, 3:4], None, ALU.mult).then_inc(sb2_ok, 1)

            def differences1():
                dve.tensor_tensor(e8[:, :, 0:1], v8[:, :, 1:2], v8[:, :, 0:1], ALU.subtract).then_inc(exp_in, 1)

            n = T * K1 * E1
            hot1, room1 = (XG[b][:, 0:n].rearrange("p (t k e) -> p t k e", t=T, k=K1) for b in range(2))
            best_experts(1, E1, K1, hot1, differences1)
            dve.wait_ge(exp_ok, 3)
            run(dve.tensor_scalar(fw[:, :, 0:1], e8[:, :, 0:1], 1.0, None, ALU.add))
            run(dve.reciprocal(fw[:, :, 0:1], fw[:, :, 0:1]))
            run(dve.tensor_tensor(fw[:, :, 1:2], fw[:, :, 0:1], e8[:, :, 0:1], ALU.mult))
            run(dve.tensor_scalar(fw[:, :, 0:2], fw[:, :, 0:2], gain[:, 3:4], None, ALU.mult))
            dispatch(1, E1, K1, G1, hot1, room1)

            def middle1(g, e):
                dve.wait_ge(M1["up_mm"], g + 2)
                dve.tensor_tensor(sg[:, 0:F1].rearrange("p (a f) -> p a f", a=1),
                                  bank[1][:, 0:F1].rearrange("p (a f) -> p a f", a=1),
                                  b1_bc[:, bass.ds(e, 1), :], ALU.add).then_inc(M1["pre_ok"], 1)

            def weighted1(g, b, ed):
                a1 = "p (a l) -> p a l"
                dve.tensor_tensor(Y[b][:].rearrange(a1, a=1), bank[3 + b][:].rearrange(a1, a=1),
                                  b2_bc[:, bass.ds(ed, 1), :], ALU.add).then_inc(yb_ok, 1)
                dve.wait_ge(yb_ok, g + 1)
                dve.tensor_scalar(Y[b][:], Y[b][:], cw[:, bass.ds(g % 4, 1)], None, ALU.mult).then_inc(M1["y_ready"], 1)

            dve.wait_ge(biases_in, 32)
            dve.wait_ge(lists_ok, 2)
            for b in range(2):
                dve.wait_ge(out_stored[b], 16 * T // 2)
            experts(M1, 1, G1, P, middle1, weighted1, E1, True)


def kernel(**inputs):
    import numpy as _np
    import concourse.bacc as _bacc
    from concourse import mybir as _mybir
    from concourse.bass_utils import run_bass_kernel_spmd as _run

    def chunks(a, n):
        return a.reshape(n, a.shape[0] // n, a.shape[1]).transpose(1, 0, 2)

    a = {k: _np.asarray(v) for k, v in inputs.items()}
    arrays = dict(
        x=a["x"], ctx=a["ctx_2048"],
        ctx_t=a["ctx_2048"].transpose(0, 2, 1).reshape(NB, KC, P, S).transpose(0, 2, 1, 3),
        mask=a["mask_BxS2_bk0"],
        gains=_np.concatenate([a["g_xattn"], a["g_ffn"]]).reshape(1, 4),
        w_qkv=_np.stack([chunks(a["L0_xattn_" + k + "W"].T, TB) for k in "QKV"], axis=1),
        b_qkv=_np.stack([a["L0_xattn_" + k + "b"].reshape(TB, P).T for k in "QKV"], axis=1),
        gate0=chunks(a["L0_ffn_gate_weight"].T, KC), sim=a["L0_ffn_similarity"],
        w_up=a["L0_ffn_gate_up_proj"].transpose(0, 2, 1).reshape(E0, KC, P, 2 * F0).transpose(0, 2, 1, 3),
        w_down=a["L0_ffn_down_proj"].transpose(0, 2, 1).reshape(E0, 2, FH, L).transpose(0, 2, 1, 3),
        gate1=chunks(a["L1_ffn_gate_w"], KC),
        w1=a["L1_ffn_w1"].reshape(E1, KC, P, F1).transpose(0, 2, 1, 3), b1=a["L1_ffn_b1"].reshape(1, E1 * F1),
        w2=a["L1_ffn_w2"].reshape(E1, 2, P, L).transpose(0, 2, 1, 3), b2=a["L1_ffn_b2"].reshape(1, E1 * L),
        sw1=chunks(a["L1_ffn_shared_w1"], KC), sb1=a["L1_ffn_shared_b1"].reshape(KC, P).T,
        sw2=chunks(a["L1_ffn_shared_w2"], KC), sb2=a["L1_ffn_shared_b2"].reshape(1, L),
    )
    arrays = {k: _np.ascontiguousarray(v) for k, v in arrays.items()}
    nc = _bacc.Bacc("TRN2", target_bir_lowering=False, num_devices=1)
    aps = {k: nc.dram_tensor(k, v.shape, _mybir.dt.from_np(v.dtype), kind="ExternalInput").ap() for k, v in arrays.items()}
    aps["out"] = nc.dram_tensor("out", (NB, S, L), F32, kind="ExternalOutput").ap()
    flamingo_kernel(nc, **aps)
    r = _run(nc, [arrays], core_ids=[0])
    return r.results[0]["out"]
```
